# Optimizing a Trainium2 kernel written in Bass

```python
import numpy as np
import jax
import jax.numpy as jnp

def _softmax(x, axis=-1):
    return jax.nn.softmax(x, axis=axis)

def _gelu(x):
    return jax.nn.gelu(x, approximate=True)

def _silu(x):
    return jax.nn.silu(x)

def _sigmoid(x):
    return jax.nn.sigmoid(x)

def _layernorm(x, axis=-1, eps=1e-05):
    m = jnp.mean(x, axis=axis, keepdims=True)
    v = jnp.var(x, axis=axis, keepdims=True)
    return (x - m) / jnp.sqrt(v + eps)

def _scatter_add(tgt, idx, src, axis=0):
    return tgt.at[idx].add(src)

def _segment_sum(src, seg, n):
    return jax.ops.segment_sum(src, seg, n)
kernel_name = 'mk_gnn_preln_d2_gnn_r8_b7bef5'

def setup_inputs(seed: int=0):
    np.random.seed(seed)
    _w = jnp.asarray

    def _rec_inputs():
        import jax
        import jax.numpy as jnp
        _gk = jax.random.key(seed)
        x = -0.0009044 + 1 * jax.random.normal(jax.random.fold_in(_gk, 1), (12500, 32), jnp.float32)
        src = jax.random.randint(jax.random.fold_in(_gk, 2), (200000,), 0, 12500, jnp.int32)
        dst = jax.random.randint(jax.random.fold_in(_gk, 3), (200000,), 0, 12500, jnp.int32)
        _o = jnp.argsort(dst, stable=True)
        src = src[_o]
        dst = dst[_o]
        edge_attr_16 = 0.000196303 + 1.00016 * jax.random.normal(jax.random.fold_in(_gk, 12), (200000, 16), jnp.float32)
        return (x, src, dst, edge_attr_16)
    x, src, dst, edge_attr_16 = _rec_inputs()

    def _L0_gnn_setup():
        import jax, jax.numpy as jnp
        import numpy as np
        N = 6250
        E = 200000
        DN = 32
        DE = 16
        DI = DN + DE
        DH = 2 * DI

        def _linear_params(key, fan_in, fan_out, dtype=jnp.float32):
            k1, k2 = jax.random.split(key)
            bound = 1.0 / np.sqrt(fan_in)
            w = jax.random.uniform(k1, (fan_in, fan_out), dtype, -bound, bound)
            b = jax.random.uniform(k2, (fan_out,), dtype, -bound, bound)
            return (w, b)
        key = jax.random.key(seed)
        ks = jax.random.split(key, 7)
        x = jax.random.normal(ks[0], (N, DN), dtype=jnp.float32)
        edge_index = jax.random.randint(ks[1], (2, E), 0, N, dtype=jnp.int64)
        edge_attr = jax.random.normal(ks[2], (E, DE), dtype=jnp.float32)
        w1a, b1a = _linear_params(ks[3], DI, DH)
        w1b, b1b = _linear_params(ks[4], DH, DH)
        w2a, b2a = _linear_params(ks[5], DN + DH, DI)
        w2b, b2b = _linear_params(ks[6], DI, DN)
        return {'x': x, 'edge_index': edge_index, 'edge_attr': edge_attr, 'w1a': w1a, 'b1a': b1a, 'w1b': w1b, 'b1b': b1b, 'w2a': w2a, 'b2a': b2a, 'w2b': w2b, 'b2b': b2b}
    _L0_gnn_all = _L0_gnn_setup()
    _L0_gnn_in = {k: v for k, v in _L0_gnn_all.items() if k in ('w1a', 'b1a', 'w1b', 'b1b', 'w2a', 'b2a', 'w2b', 'b2b')}
    del _L0_gnn_all

    def _L1_gnn_setup():
        import jax, jax.numpy as jnp
        import numpy as np
        N_NODES = 12500
        N_EDGES = 200000
        D_FEAT = 32
        K = 10
        ALPHA = 0.1
        key = jax.random.key(seed)
        k1, k2, k3 = jax.random.split(key, 3)
        feat = jax.random.normal(k1, (N_NODES, D_FEAT), dtype=jnp.float32)
        src = jax.random.randint(k2, (N_EDGES,), 0, N_NODES, dtype=jnp.int64)
        dst = jax.random.randint(k3, (N_EDGES,), 0, N_NODES, dtype=jnp.int64)
        return {'feat': feat, 'src': src, 'dst': dst}
    _L1_gnn_all = _L1_gnn_setup()
    _L1_gnn_in = {k: v for k, v in _L1_gnn_all.items() if k in ()}
    del _L1_gnn_all
    return {'x': x, 'src': src, 'dst': dst, 'edge_attr_16': edge_attr_16, 'L0_gnn_w1a': _L0_gnn_in['w1a'], 'L0_gnn_b1a': _L0_gnn_in['b1a'], 'L0_gnn_w1b': _L0_gnn_in['w1b'], 'L0_gnn_b1b': _L0_gnn_in['b1b'], 'L0_gnn_w2a': _L0_gnn_in['w2a'], 'L0_gnn_b2a': _L0_gnn_in['b2a'], 'L0_gnn_w2b': _L0_gnn_in['w2b'], 'L0_gnn_b2b': _L0_gnn_in['b2b']}

def reference(x, src, dst, edge_attr_16, L0_gnn_w1a, L0_gnn_b1a, L0_gnn_w1b, L0_gnn_b1b, L0_gnn_w2a, L0_gnn_b2a, L0_gnn_w2b, L0_gnn_b2b):
    import jax
    import jax.numpy as jnp

    def _L0_gnn_ref(x, edge_index, edge_attr, w1a, b1a, w1b, b1b, w2a, b2a, w2b, b2b):
        import jax, jax.numpy as jnp
        import numpy as np
        N = 6250
        E = 200000
        DN = 32
        DE = 16
        DI = DN + DE
        DH = 2 * DI

        def _linear_params(key, fan_in, fan_out, dtype=jnp.float32):
            k1, k2 = jax.random.split(key)
            bound = 1.0 / np.sqrt(fan_in)
            w = jax.random.uniform(k1, (fan_in, fan_out), dtype, -bound, bound)
            b = jax.random.uniform(k2, (fan_out,), dtype, -bound, bound)
            return (w, b)
        row = edge_index[0]
        col = edge_index[1]
        h = jnp.concatenate([x[row], edge_attr], axis=1)
        h = jnp.maximum(h @ w1a + b1a, 0.0)
        h = h @ w1b + b1b
        s = jax.ops.segment_sum(h, col, num_segments=x.shape[0])
        cnt = jax.ops.segment_sum(jnp.ones((col.shape[0],), x.dtype), col, num_segments=x.shape[0])
        agg = s / jnp.maximum(cnt, 1.0)[:, None]
        h2 = jnp.concatenate([x, agg], axis=1)
        h2 = jnp.maximum(h2 @ w2a + b2a, 0.0)
        return h2 @ w2b + b2b

    def _L1_gnn_ref(feat, src, dst):
        import jax, jax.numpy as jnp
        import numpy as np
        N_NODES = 12500
        N_EDGES = 200000
        D_FEAT = 32
        K = 10
        ALPHA = 0.1
        n = feat.shape[0]
        ones = jnp.ones(src.shape[0], dtype=feat.dtype)
        out_deg = jax.ops.segment_sum(ones, src, num_segments=n)
        in_deg = jax.ops.segment_sum(ones, dst, num_segments=n)
        src_norm = jnp.clip(out_deg, 1.0, None) ** (-0.5)
        dst_norm = jnp.clip(in_deg, 1.0, None) ** (-0.5)
        feat0 = feat

        def step(f, _):
            f = f * src_norm[:, None]
            agg = jax.ops.segment_sum(f[src], dst, num_segments=n)
            f = agg * dst_norm[:, None]
            f = (1.0 - ALPHA) * f + ALPHA * feat0
            return (f, None)
        feat, _ = jax.lax.scan(step, feat, None, length=K)
        return feat
    edge_index = jnp.stack([src, dst])
    h = jnp.maximum(_layernorm(x, axis=-1), 0.0)
    x = x + _L0_gnn_ref(h, edge_index, edge_attr_16, L0_gnn_w1a, L0_gnn_b1a, L0_gnn_w1b, L0_gnn_b1b, L0_gnn_w2a, L0_gnn_b2a, L0_gnn_w2b, L0_gnn_b2b)
    h = jnp.maximum(_layernorm(x, axis=-1), 0.0)
    x = x + _L1_gnn_ref(h, src, dst)
    return x

_drawn_inputs = setup_inputs


def setup_inputs(seed=0):
    import zlib

    import numpy as np

    out = dict(_drawn_inputs(seed))
    spreads = {}
    factors = {'edge_attr_16': 8.0,
     'L0_gnn_w1a': 4.525,
     'L0_gnn_b1a': 8.0,
     'L0_gnn_b1b': 3.651,
     'L0_gnn_b2a': 2.701}
    for name, (base, spread) in spreads.items():
        noise = np.random.default_rng([zlib.crc32(name.encode()), seed]).standard_normal(out[name].shape)
        drawn = base * np.exp(spread * noise) if base else spread * noise
        out[name] = jnp.asarray(drawn.astype(out[name].dtype))
    for name, factor in factors.items():
        out[name] = (out[name] * factor).astype(out[name].dtype)
    return out
```

```python
from contextlib import ExitStack

import concourse.bass as bass
from concourse import mybir

FP32 = mybir.dt.float32
BF16 = mybir.dt.bfloat16
FP16 = mybir.dt.float16
FP8 = mybir.dt.float8e3
U8 = mybir.dt.uint8
I32 = mybir.dt.int32
ALU = mybir.AluOpType
ACT = mybir.ActivationFunctionType
AX = mybir.AxisListType

P = 128
N = 12500
E = 200000
DN = 32
DE = 16
DI = DN + DE
DH = 2 * DI
STEPS = 10
ALPHA = 0.1
EPS = 1e-5

J = -(-N // P)
NP = P * J
NL = N - P * (J - 1)
G = 16
T = 1568
EP = P * T
EL = E - (P - 1) * T
PAD_NODE = NP - 1
BITS = 7
ROUND = 12582912.0
ZB = 7
ZJ = J // ZB
ZW = ZJ * DN
SLOTS = 2
WD = 4
WBITS = 2
WINDOWS = NP // WD
WG = P // WD
WC = WD * J
TD = T + SLOTS * G
assert P == 1 << BITS and WD == 1 << WBITS and T == J * G and WC <= 512 and T % G == 0 and NP > N and EP >= E and J % ZB == 0 and ZW <= 512


def per_node(tile, d=DN):
    return tile.rearrange("p (j d) -> p j d", d=d)


def spread_over(column, d=DN):
    return column.unsqueeze(2).broadcast_to([P, J, d])


def row_vector(v):
    return v.rearrange("(a d) -> a d", a=1)


class Dram:

    def __init__(self, nc):
        dram = lambda name, shape, dt=FP32: nc.dram_tensor(name, shape, dt).ap()
        self.table = dram("row_table", (NP, DN))
        self.attrs = dram("attrs_padded", (EP, DE))
        self.keys = dram("edge_keys", (EP, 2))
        self.starts = dram("window_starts", (1, WINDOWS), I32)
        self.running = dram("running_sums", (P, TD, DH))
        self.counts = dram("edge_counts", (J + SLOTS, P, J, P), U8)


class Kept:

    def __init__(self, nc, ctx, dram, tag):
        self.tag, self.dram = tag, dram
        sb = lambda name, shape, dt=FP32: ctx.enter_context(nc.sbuf_tensor(f"{name}_{tag}", shape, dt))
        self.banks = ctx.enter_context(nc.psum_tensor(f"banks_{tag}", [P, 8, 512], FP32))
        self.x = sb("x_nodes", [P, J * DN])
        self.h = sb("h_nodes", [P, J * DN])
        self.f = sb("f_nodes", [P, J * DN])
        self.in_deg = sb("in_deg", [P, J])
        self.in_cap = sb("in_cap", [P, J])
        self.in_inv = sb("in_inv", [P, J])
        self.src_norm = sb("src_norm", [P, J])
        self.dst_norm = sb("dst_norm", [P, J])
        self.iota = sb("iota_row", [P, P])
        self.iota16 = sb("iota_row16", [P, P], BF16)
        self.ident = sb("identity", [P, P])
        self.zeros = sb("zeros", [P, 512])
        self.zeros16 = sb("zeros16", [P, P], BF16)
        self.w1a = sb("w1a_b1a", [P, DH])
        self.w1b = sb("w1b_b1b", [DH + 1, DH])
        self.w2a_h = sb("w2a_h", [DN, DI])
        self.w2a_agg = sb("w2a_agg", [DH, DI])
        self.b2a = sb("b2a_col", [DI, 1])
        self.w2b = sb("w2b_b2b", [P, DN])


class Edges:

    def __init__(self, nc, ctx, tag):
        sb = lambda name, shape, dt=FP32: ctx.enter_context(nc.sbuf_tensor(f"{name}_{tag}", shape, dt))
        self.src = sb("src_ends", [P, T], I32)
        self.dst = sb("dst_ends", [P, T], I32)
        self.src_part = sb("src_part", [P, T])
        self.src_place = sb("src_place", [P, T])
        self.dst_part = sb("dst_part", [P, T])
        self.dst_place = sb("dst_place", [P, T])


def setup(nc, b, edges, ins):
    with ExitStack() as ctx:
        sem = lambda name: ctx.enter_context(nc.semaphore(f"{name}_{b.tag}"))
        sb = lambda name, shape, dt=FP32: ctx.enter_context(nc.sbuf_tensor(f"{name}_{b.tag}", shape, dt))
        filled, loaded, attrs_copied, iotas, ident_made, split = (
            sem("filled"), sem("loaded"), sem("attrs_copied"), sem("iotas"), sem("ident_made"), sem("split"))
        zero_rows = sb("zero_rows", [P, (EP - E) * DE // 64])
        iota_i = sb("iota_int", [P, P], I32)
        low, high = sb("end_low", [P, T], I32), sb("end_high", [P, T], I32)
        block = ctx.enter_context(nc.Block())
        LOADS = 17

        @block.sync
        def _(sp):
            cut = lambda t: t.rearrange("(a r) d -> a (r d)", a=320)
            sp.dma_start(cut(b.dram.attrs[0:E, :]), cut(ins["edge_attr_16"])).then_inc(attrs_copied, 16)
            sp.wait_ge(filled, 8)
            sp.dma_start(b.dram.attrs[E:EP, :].rearrange("(p r) d -> p (r d)", p=64), zero_rows[0:64, :]).then_inc(attrs_copied, 16)
            x = ins["x"]
            sp.dma_start(per_node(b.x[:, :])[:, 0:J - 1, :], x[0:P * (J - 1), :].rearrange("(j p) d -> p j d", p=P)).then_inc(loaded, 16)
            sp.dma_start(b.x[0:NL, (J - 1) * DN:J * DN], x[P * (J - 1):N, :]).then_inc(loaded, 16)
            for tile, ends in ((edges.src, ins["src"]), (edges.dst, ins["dst"])):
                sp.dma_start(tile[0:P - 1, :], ends[0:(P - 1) * T].rearrange("(p t) -> p t", t=T)).then_inc(loaded, 16)
                sp.dma_start(tile[P - 1:P, 0:EL], ends[(P - 1) * T:E].rearrange("(p t) -> p t", p=1)).then_inc(loaded, 16)
            for at in (0, 64):
                sp.dma_start(b.w1a[at:at + DI, :], ins["L0_gnn_w1a"]).then_inc(loaded, 16)
                sp.dma_start(b.w1a[at + DI:at + DI + 1, :], row_vector(ins["L0_gnn_b1a"])).then_inc(loaded, 16)
            sp.dma_start(b.w1b[0:DH, :], ins["L0_gnn_w1b"]).then_inc(loaded, 16)
            sp.dma_start(b.w1b[DH:DH + 1, :], row_vector(ins["L0_gnn_b1b"])).then_inc(loaded, 16)
            sp.dma_start(b.w2a_h[:, :], ins["L0_gnn_w2a"][0:DN, :]).then_inc(loaded, 16)
            sp.dma_start(b.w2a_agg[:, :], ins["L0_gnn_w2a"][DN:DN + DH, :]).then_inc(loaded, 16)
            sp.dma_start(b.b2a[:, :], ins["L0_gnn_b2a"].rearrange("(d a) -> d a", a=1)).then_inc(loaded, 16)
            sp.dma_start(b.w2b[0:DI, :], ins["L0_gnn_w2b"]).then_inc(loaded, 16)
            sp.dma_start(b.w2b[64:65, :], row_vector(ins["L0_gnn_b2b"])).then_inc(loaded, 16)
            sp.wait_ge(loaded, LOADS * 16)
            sp.wait_ge(attrs_copied, 32)

        @block.gpsimd
        def _(pool):
            nc.gpsimd.iota(iota_i[:, :], pattern=[[1, P]], base=0, channel_multiplier=0).then_inc(iotas, 1)
            nc.gpsimd.memset(b.ident[:, :], 0.0).then_inc(ident_made, 1)
            pool.wait_ge(ident_made, 1)
            nc.gpsimd.affine_select(out=b.ident[:, :], in_=b.ident[:, :], compare_op=ALU.not_equal, fill=1.0,
                                    base=0, pattern=[[-1, P]], channel_multiplier=1).then_inc(ident_made, 1)
            pool.wait_ge(ident_made, 2)

        @block.vector
        def _(dve):
            for tile, value in ((zero_rows, 0.0), (b.x, 0.0), (edges.src, PAD_NODE), (edges.dst, PAD_NODE), (b.zeros, 0.0),
                                (b.w2b, 0.0), (b.w1a, 0.0), (b.zeros16, 0.0)):
                nc.vector.memset(tile[:, :], value).then_inc(filled, 1)
            dve.wait_ge(iotas, 1)
            nc.vector.tensor_copy(b.iota[:, :], iota_i[:, :]).then_inc(filled, 1)
            nc.vector.tensor_copy(b.iota16[:, :], iota_i[:, :]).then_inc(filled, 1)
            dve.wait_ge(filled, 10)
            dve.wait_ge(loaded, LOADS * 16)
            n = 0
            for ends, part, place in ((edges.src, edges.src_part, edges.src_place), (edges.dst, edges.dst_part, edges.dst_place)):
                nc.vector.tensor_scalar(low[:, :], ends[:, :], P - 1, None, ALU.bitwise_and).then_inc(split, 1)
                nc.vector.tensor_scalar(high[:, :], ends[:, :], BITS, None, ALU.logical_shift_right).then_inc(split, 1)
                dve.wait_ge(split, n + 2)
                nc.vector.tensor_copy(part[:, :], low[:, :]).then_inc(split, 1)
                nc.vector.tensor_copy(place[:, :], high[:, :]).then_inc(split, 1)
                n += 4
                dve.wait_ge(split, n)
            nc.vector.scalar_tensor_tensor(out=edges.src[:, :], in0=edges.src_part[:, :], scalar=float(J), in1=edges.src_place[:, :],
                                           op0=ALU.mult, op1=ALU.add).then_inc(split, 1)
            dve.wait_ge(split, n + 1)


def inverse_root(nc, dve, root, value, term, done, n):
    nc.vector.reciprocal(root, root).then_inc(done, 1)
    dve.wait_ge(done, n + 1)
    nc.vector.tensor_tensor(term, root, root, ALU.mult).then_inc(done, 1)
    dve.wait_ge(done, n + 2)
    nc.vector.tensor_tensor(term, term, value, ALU.mult).then_inc(done, 1)
    dve.wait_ge(done, n + 3)
    nc.vector.tensor_scalar(term, term, -0.5, 1.5, ALU.mult, ALU.add).then_inc(done, 1)
    dve.wait_ge(done, n + 4)
    nc.vector.tensor_tensor(root, root, term, ALU.mult).then_inc(done, 1)
    dve.wait_ge(done, n + 5)


def layer_norm_relu(nc, b, tag):
    tag = f"{tag}_{b.tag}"
    """b.h = relu(layer norm of b.x), node by node."""
    with ExitStack() as ctx:
        done = ctx.enter_context(nc.semaphore(f"ln_done_{tag}"))
        rooted = ctx.enter_context(nc.semaphore(f"ln_rooted_{tag}"))
        mean = ctx.enter_context(nc.sbuf_tensor(f"ln_mean_{tag}", [P, J], FP32))
        var = ctx.enter_context(nc.sbuf_tensor(f"ln_var_{tag}", [P, J], FP32))
        term = ctx.enter_context(nc.sbuf_tensor(f"ln_newton_{tag}", [P, J], FP32))
        square = ctx.enter_context(nc.sbuf_tensor(f"ln_square_{tag}", [P, J * DN], FP32))
        block = ctx.enter_context(nc.Block())

        @block.vector
        def _(dve):
            h = per_node(b.h[:, :])
            nc.vector.tensor_reduce(mean[:, :], per_node(b.x[:, :]), AX.X, ALU.add).then_inc(done, 1)
            dve.wait_ge(done, 1)
            nc.vector.tensor_scalar(mean[:, :], mean[:, :], 1.0 / DN, None, ALU.mult).then_inc(done, 1)
            dve.wait_ge(done, 2)
            nc.vector.tensor_tensor(h, per_node(b.x[:, :]), spread_over(mean[:, :]), ALU.subtract).then_inc(done, 1)
            dve.wait_ge(done, 3)
            nc.vector.tensor_tensor(square[:, :], b.h[:, :], b.h[:, :], ALU.mult).then_inc(done, 1)
            dve.wait_ge(done, 4)
            nc.vector.tensor_reduce(var[:, :], per_node(square[:, :]), AX.X, ALU.add).then_inc(done, 1)
            dve.wait_ge(done, 5)
            nc.vector.tensor_scalar(var[:, :], var[:, :], 1.0 / DN, EPS, ALU.mult, ALU.add).then_inc(done, 1)
            dve.wait_ge(done, 6)
            dve.wait_ge(rooted, 1)
            inverse_root(nc, dve, mean[:, :], var[:, :], term[:, :], done, 6)
            nc.vector.tensor_tensor(h, h, spread_over(mean[:, :]), ALU.mult).then_inc(done, 1)
            dve.wait_ge(done, 12)
            nc.vector.tensor_scalar(b.h[:, :], b.h[:, :], 0.0, None, ALU.max).then_inc(done, 1)
            dve.wait_ge(done, 13)

        @block.scalar
        def _(act):
            act.wait_ge(done, 6)
            nc.scalar.sqrt(mean[:, :], var[:, :]).then_inc(rooted, 1)


def store_table(nc, b, tile):
    tag = b.tag
    """The gather table's rows are the tile's."""
    with nc.semaphore(f"table_stored_{tag}") as stored, nc.Block() as block:
        @block.sync
        def _(sp):
            sp.dma_start(b.dram.table.rearrange("(p j) d -> p (j d)", j=J), tile[:, :]).then_inc(stored, 16)
            sp.wait_ge(stored, 16)


def degrees(nc, b, edges):
    with ExitStack() as ctx:
        sem = lambda name: ctx.enter_context(nc.semaphore(f"{name}_{b.tag}"))
        sb = lambda name, shape, dt=FP32: ctx.enter_context(nc.sbuf_tensor(f"{name}_{b.tag}", shape, dt))
        hot, used, summed, normed = sem("hot_made"), sem("hot_used"), sem("deg_summed"), sem("deg_normed")
        rooted = sem("deg_rooted")
        term, out_cap = sb("deg_newton", [P, J]), sb("out_cap", [P, J])
        part_hot = sb("part_hot", [P, 2, 2, G // 2, P], BF16)
        place_hot = sb("place_hot", [P, 2, 2, G // 2, J], BF16)
        count = b.banks
        block = ctx.enter_context(nc.Block())
        H = G // 2

        @block.vector
        def _(dve):
            with dve.Fori(0, T // G) as i:
                for s in range(2):
                    dve.wait_ge(used, i * 2 + s + 1)
                    for k, (part, place) in enumerate(((edges.dst_part, edges.dst_place), (edges.src_part, edges.src_place))):
                        for c in range(H):
                            col = bass.ds((i * 2 + s) * H + c, 1)
                            nc.vector.tensor_scalar(part_hot[:, s, k, c, :], b.iota16[:, :], part[:, col], None,
                                                    ALU.is_equal).then_inc(hot, 1)
                            nc.vector.tensor_scalar(place_hot[:, s, k, c, :], b.iota16[:, 0:J], place[:, col], None,
                                                    ALU.is_equal).then_inc(hot, 1)
            dve.wait_ge(summed, 1)
            nc.vector.tensor_copy(b.in_deg[:, :], count[:, 0, 0:J]).then_inc(normed, 1)
            nc.vector.tensor_scalar(b.in_cap[:, :], count[:, 0, 0:J], 1.0, None, ALU.max).then_inc(normed, 1)
            nc.vector.tensor_scalar(out_cap[:, :], count[:, 1, 0:J], 1.0, None, ALU.max).then_inc(normed, 1)
            dve.wait_ge(normed, 3)
            nc.vector.reciprocal(b.in_inv[:, :], b.in_cap[:, :]).then_inc(normed, 1)

            dve.wait_ge(rooted, 2)
            inverse_root(nc, dve, b.src_norm[:, :], out_cap[:, :], term[:, :], normed, 4)
            inverse_root(nc, dve, b.dst_norm[:, :], b.in_cap[:, :], term[:, :], normed, 9)

        @block.scalar
        def _(act):
            act.wait_ge(normed, 3)
            nc.scalar.sqrt(b.src_norm[:, :], out_cap[:, :]).then_inc(rooted, 1)
            nc.scalar.sqrt(b.dst_norm[:, :], b.in_cap[:, :]).then_inc(rooted, 1)

        @block.tensor
        def _(pe):
            zero = lambda k, **flags: nc.tensor.matmul(count[:, k, 0:J], b.zeros16[:, 0:P], b.zeros16[:, 0:J],
                                                       skip_group_check=True, **flags)
            zero(0, start=True, stop=False)
            zero(1, start=True, stop=False).then_inc(used, 2)
            with pe.Fori(0, T // G) as i:
                for s in range(2):
                    pe.wait_ge(hot, (i * 2 + s + 1) * 4 * H)
                    for k in range(2):
                        for c in range(H):
                            last = nc.tensor.matmul(count[:, k, 0:J], part_hot[:, s, k, c, :], place_hot[:, s, k, c, :],
                                                    start=False, stop=False, skip_group_check=True)
                    last.then_inc(used, 1)
            zero(0, start=False, stop=True)
            zero(1, start=False, stop=True).then_inc(summed, 1)


def edge_sums(nc, b, edges, agg_tile, messages, s, tiles, third=None):
    idx, rows, turn, msg, part_hot, spread, w_third = tiles
    sums, work = b.banks, b.banks[:, ZB, :]
    sums_to = per_node(agg_tile[:, :], DH + 1) if messages else per_node(b.f[:, :])
    with nc.Block() as block:
        @block.gpsimd
        def _(pool):
            with pool.Fori(0, T // G) as i:
                pool.wait_ge(s["idx_ready"], i + 1)
                pool.sem_inc(s["taken"], 1)
                for c in range(G):
                    pool.indirect_dma_start(out=rows[:, c, 0:DN], out_offset=None, in_=b.dram.table,
                                            in_offset=bass.IndirectOffsetOnAxis(ap=idx[:, c:c + 1], axis=0)) \
                        .then_inc(s["gathered"], 16)
                pool.wait_ge(s["gathered"], (i + 1) * (G * 16))
                pool.sem_inc(s["rows_ready"], 1)
            pool.inc_swdge_sem([s["gathered"]], [T * 16], mode="sub")

        if messages:
            @block.sync
            def _(sp):
                attrs = b.dram.attrs.rearrange("(p t) d -> p t d", t=T)
                with sp.Fori(0, T // G) as i:
                    sp.wait_ge(s["idx_ready"], i + 1)
                    sp.sem_inc(s["taken"], 1)
                    sp.dma_start(rows[:, :, DN:DI], attrs[:, bass.ds(i * G, G), :]).then_inc(s["attrs"], 16)
                    sp.wait_ge(s["attrs"], (i + 1) * 16)
                    sp.sem_inc(s["attrs_ready"], 1)

            @block.scalar
            def _(act):
                with act.Fori(0, T // G) as i:
                    for c in range(0, G, 2):
                        act.wait_ge(s["turned"], i * (G // 2) + c // 2 + 1)
                        nc.scalar.copy(turn[:, :], work[:, 0:P]).then_inc(s["turn_read"], 1)

        @block.vector
        def _(dve):
            nc.vector.memset(rows[:, :, DN:64], 0.0).then_inc(s["ones"], 1)
            dve.wait_ge(s["ones"], 1)
            nc.vector.memset(rows[:, :, DI:DI + 1], 1.0).then_inc(s["ones"], 1)
            if messages:
                nc.vector.tensor_copy(w_third[:, :], b.w1a[:, bass.ds(third * DN, DN)]).then_inc(s["ones"], 1)
            dve.wait_ge(s["ones"], 3 if messages else 2)
            with dve.Fori(0, T // G) as i:
                nc.vector.tensor_copy(idx[:, :], edges.src[:, bass.ds(i * G, G)]).then_inc(s["idx_ready"], 1)
                dve.wait_ge(s["rows_ready"], i + 1)
                for c in range(G):
                    n, r = i * G + c, c % 2
                    row = rows[:, c, 0:DN]
                    if messages:
                        dve.wait_ge(s["mixed"], n + 1)
                        nc.vector.tensor_scalar(msg[:, r, :], work[:, 256:256 + DN], 0.0, None, ALU.max).then_inc(s["mix_read"], 1)
                        dve.wait_ge(s["mix_read"], n + 2)
                        row = msg[:, r, :]
                    dve.wait_ge(s["used"], n + 1)
                    nc.vector.tensor_scalar(part_hot[:, r, :], b.iota[:, :], edges.dst_part[:, bass.ds(n, 1)], None,
                                            ALU.is_equal).then_inc(s["hot"], 1)
                    nc.vector.scalar_tensor_tensor(
                        out=per_node(spread[:, r, :]), in0=spread_over(b.iota[:, 0:J]), scalar=edges.dst_place[:, bass.ds(n, 1)],
                        in1=row.unsqueeze(1).broadcast_to([P, J, DN]), op0=ALU.is_equal, op1=ALU.mult).then_inc(s["hot"], 1)
                dve.wait_ge(s["hot"], (i + 1) * (2 * G))
            dve.wait_ge(s["summed"], 1)
            for z in range(ZB):
                to = (sums_to[:, z * ZJ:(z + 1) * ZJ, bass.ds(third * DN, DN)] if messages
                      else sums_to[:, z * ZJ:(z + 1) * ZJ, :])
                nc.vector.tensor_copy(to, sums[:, z, 0:ZW].rearrange("p (j d) -> p j d", d=DN)).then_inc(s["copied"], 1)
            dve.wait_ge(s["copied"], ZB)

        @block.tensor
        def _(pe):
            def zero(z, **flags):
                return nc.tensor.matmul(sums[:, z, 0:ZW], b.zeros[:, 0:P], b.zeros[:, 0:ZW], skip_group_check=True, **flags)
            for z in range(ZB):
                last = zero(z, start=True, stop=False)
            last.then_inc(s["used"], 2)
            pe.sem_inc(s["mix_read"], 1)
            with pe.Fori(0, T // G) as i:
                for c in range(G):
                    n, r = i * G + c, c % 2
                    if messages:
                        if c == 0:
                            pe.wait_ge(s["rows_ready"], i + 1)
                            pe.wait_ge(s["attrs_ready"], i + 1)
                        pe.wait_ge(s["mix_read"], n + 1)
                        if c % 2 == 0:
                            nc.tensor.transpose(work[:, 0:P], rows[:, c:c + 2, :].rearrange("p c d -> p (c d)"),
                                                b.ident[:, :]).then_inc(s["turned"], 1)
                            pe.wait_ge(s["turn_read"], i * (G // 2) + c // 2 + 1)
                        at = 64 * (c % 2)
                        nc.tensor.matmul(work[:, 256:256 + DN], turn[at:at + DI + 1, :], w_third[at:at + DI + 1, :],
                                         start=True, stop=True).then_inc(s["mixed"], 1)
                    pe.wait_ge(s["hot"], (n + 1) * 2)
                    for z in range(ZB):
                        last = nc.tensor.matmul(sums[:, z, 0:ZW], part_hot[:, r, :], spread[:, r, z * ZW:(z + 1) * ZW],
                                                start=False, stop=False, skip_group_check=True)
                    last.then_inc(s["used"], 1)
            for z in range(ZB):
                last = zero(z, start=False, stop=True)
            last.then_inc(s["summed"], 1)


def node_mlp(nc, b, agg_tile):
    B = 2
    with ExitStack() as ctx:
        tag = b.tag
        sem = lambda name: ctx.enter_context(nc.semaphore(f"mlp_{name}_{tag}"))
        staged, turned, turn_read, agg_mixed, agg_read, hidden, hidden_read, out_made, out_added, filled = (
            sem("staged"), sem("tiles_turned"), sem("tiles_turn_read"), sem("agg_mixed"), sem("agg_mix_read"),
            sem("hidden_made"), sem("hidden_read"), sem("out_made"), sem("out_added"), sem("mid_filled"))
        agg_in = ctx.enter_context(nc.sbuf_tensor(f"agg_in_{tag}", [P, B, DH + 1], FP32))
        h_in = ctx.enter_context(nc.sbuf_tensor(f"h_in_{tag}", [P, B, DN], FP32))
        agg_t = ctx.enter_context(nc.sbuf_tensor(f"agg_t_{tag}", [DH + 1, B * P], FP32))
        h_t = ctx.enter_context(nc.sbuf_tensor(f"h_t_{tag}", [DN, B * P], FP32))
        mix = ctx.enter_context(nc.sbuf_tensor(f"agg_mix_{tag}", [DH, B * P], FP32))
        mid = ctx.enter_context(nc.sbuf_tensor(f"mid_{tag}", [P, B * P], FP32))
        block = ctx.enter_context(nc.Block())
        ps = b.banks
        agg = per_node(agg_tile[:, :], DH + 1)
        h = per_node(b.h[:, :])

        @block.vector
        def _(dve):
            nc.vector.memset(mid[:, :], 0.0).then_inc(filled, 1)
            dve.wait_ge(filled, 1)
            nc.vector.memset(mid[64:65, :], 1.0).then_inc(filled, 1)
            nc.vector.tensor_copy(agg[:, :, DH:DH + 1], b.in_deg[:, :].unsqueeze(2)).then_inc(filled, 1)
            dve.wait_ge(filled, 3)
            with dve.Fori(0, J // B) as i:
                at = bass.ds(i * B, B)
                nc.vector.tensor_tensor(agg_in[:, :, :], agg[:, at, :],
                                        b.in_inv[:, at].unsqueeze(2).broadcast_to([P, B, DH + 1]), ALU.mult).then_inc(staged, 1)
                nc.vector.tensor_copy(h_in[:, :, :], h[:, at, :]).then_inc(staged, 1)
                dve.wait_ge(turned, i + 1)
                nc.vector.tensor_copy(agg_t[:, :], ps[0:DH + 1, 0, 0:B * P]).then_inc(turn_read, 1)
                nc.vector.tensor_copy(h_t[:, :], ps[0:DN, 4, 0:B * P]).then_inc(turn_read, 1)
                dve.wait_ge(out_made, i + 1)
                x = per_node(b.x[:, :])[:, at, :]
                nc.vector.tensor_tensor(x, x, ps[:, 3, 0:B * DN].rearrange("p (j d) -> p j d", d=DN),
                                        ALU.add).then_inc(out_added, 1)
            dve.wait_ge(out_added, J // B)

        @block.scalar
        def _(act):
            act.wait_ge(filled, 2)
            with act.Fori(0, J // B) as i:
                act.wait_ge(agg_mixed, i + 1)
                nc.scalar.copy(mix[:, :], ps[0:DH, 1, 0:B * P]).then_inc(agg_read, 1)
                act.wait_ge(hidden, i + 1)
                nc.scalar.activation(mid[0:DI, :], ps[0:DI, 2, 0:B * P], ACT.Relu, bias=b.b2a[:, :]).then_inc(hidden_read, 1)

        @block.tensor
        def _(pe):
            with pe.Fori(0, J // B) as i:
                pe.wait_ge(staged, 2 * i + 2)
                for c in range(B):
                    nc.tensor.transpose(ps[0:DH + 1, 0, c * P:(c + 1) * P], agg_in[:, c, :], b.ident[:, :])
                    last = nc.tensor.transpose(ps[0:DN, 4, c * P:(c + 1) * P], h_in[:, c, :], b.ident[:, :])
                last.then_inc(turned, 1)
                pe.wait_ge(turn_read, 2 * i + 2)
                nc.tensor.matmul(ps[0:DH, 1, 0:B * P], b.w1b[:, :], agg_t[:, :], start=True, stop=True).then_inc(agg_mixed, 1)
                pe.wait_ge(agg_read, i + 1)
                nc.tensor.matmul(ps[0:DI, 2, 0:B * P], b.w2a_h[:, :], h_t[:, :], start=True, stop=False)
                nc.tensor.matmul(ps[0:DI, 2, 0:B * P], b.w2a_agg[:, :], mix[:, :], start=False, stop=True).then_inc(hidden, 1)
                pe.wait_ge(hidden_read, i + 1)
                for c in range(B):
                    last = nc.tensor.matmul(ps[:, 3, c * DN:(c + 1) * DN], mid[0:65, c * P:(c + 1) * P], b.w2b[0:65, :],
                                            start=True, stop=True)
                last.then_inc(out_made, 1)
                pe.wait_ge(out_added, i + 1)


GATHER_SEMS = ("idx_ready", "taken", "rows_ready", "attrs", "attrs_ready", "turned", "turn_read", "ones", "mixed", "mix_read", "used", "hot",
               "summed", "copied", "scaled", "stored")


def general_layers(nc, b, edges, agg_tile):
    with ExitStack() as ctx:
        s = {name: ctx.enter_context(nc.semaphore(f"any_{name}")) for name in GATHER_SEMS}
        low, high = s["idx_ready"].num, s["stored"].num
        assert high - low == len(GATHER_SEMS) - 1
        s["gathered"] = ctx.enter_context(nc.semaphore("any_gathered"))
        sb = lambda name, shape, dt=FP32: ctx.enter_context(nc.sbuf_tensor(f"any_{name}", shape, dt))
        tiles = (sb("idx", [P, G], I32), sb("rows", [P, G, 64]), sb("turn", [P, P]), sb("msg", [P, 2, DN]),
                 sb("part_hot", [P, 2, P]), sb("spread", [P, 2, J * DN]), sb("w_third", [P, DN]))
        spread = tiles[5]

        def start_again():
            nc.gpsimd.sem_clear(range(low, high + 1))
            nc.all_engine_barrier()

        layer_norm_relu(nc, b, "in")
        store_table(nc, b, b.h)
        with nc.Fori(0, DH // DN) as third:
            edge_sums(nc, b, edges, agg_tile, True, s, tiles, third)
            start_again()
        node_mlp(nc, b, agg_tile)
        layer_norm_relu(nc, b, "mid")
        with nc.Block() as block:
            @block.vector
            def _(dve):
                nc.vector.tensor_copy(b.f[:, :], b.h[:, :]).then_inc(s["scaled"], 1)
                dve.wait_ge(s["scaled"], 1)
        start_again()
        with nc.Fori(0, STEPS) as step:
            with nc.Block() as block:
                @block.vector
                def _(dve):
                    nc.vector.tensor_tensor(per_node(spread[:, 0, :]), per_node(b.f[:, :]), spread_over(b.src_norm[:, :]),
                                            ALU.mult).then_inc(s["scaled"], 1)

                @block.sync
                def _(sp):
                    sp.wait_ge(s["scaled"], 1)
                    sp.dma_start(b.dram.table.rearrange("(p j) d -> p (j d)", j=J), spread[:, 0, :]).then_inc(s["stored"], 16)
                    sp.wait_ge(s["stored"], 16)
            start_again()
            edge_sums(nc, b, edges, agg_tile, False, s, tiles)
            start_again()
            with nc.Block() as block:
                @block.vector
                def _(dve):
                    combine(nc, dve, b, s["scaled"])
            start_again()


def combine(nc, dve, b, scaled):
    nc.vector.tensor_tensor(per_node(b.f[:, :]), per_node(b.f[:, :]), spread_over(b.dst_norm[:, :]), ALU.mult).then_inc(scaled, 1)
    dve.wait_ge(scaled, 1)
    nc.vector.tensor_scalar(b.f[:, :], b.f[:, :], 1.0 - ALPHA, None, ALU.mult).then_inc(scaled, 1)
    dve.wait_ge(scaled, 2)
    nc.vector.scalar_tensor_tensor(out=b.f[:, :], in0=b.h[:, :], scalar=ALPHA, in1=b.f[:, :], op0=ALU.mult,
                                   op1=ALU.add).then_inc(scaled, 1)
    dve.wait_ge(scaled, 3)


def store_result(nc, b, out):
    with nc.semaphore(f"result_added_{b.tag}") as added, nc.semaphore(f"result_stored_{b.tag}") as stored, nc.Block() as block:
        @block.vector
        def _(dve):
            nc.vector.tensor_tensor(b.f[:, :], b.f[:, :], b.x[:, :], ALU.add).then_inc(added, 1)

        @block.sync
        def _(sp):
            sp.wait_ge(added, 1)
            sp.dma_start(out[0:P * (J - 1), :].rearrange("(j p) d -> p j d", p=P), per_node(b.f[:, :])[:, 0:J - 1, :]).then_inc(stored, 16)
            sp.dma_start(out[P * (J - 1):N, :], b.f[0:NL, (J - 1) * DN:J * DN]).then_inc(stored, 16)
            sp.wait_ge(stored, 32)



def prepare_sorted(nc, b, edges, ins, kept):
    same, cont, last_row, unsorted = kept
    with ExitStack() as ctx:
        sem = lambda name: ctx.enter_context(nc.semaphore(f"{name}_{b.tag}"))
        sb = lambda name, shape, dt=FP32: ctx.enter_context(nc.sbuf_tensor(f"{name}_{b.tag}", shape, dt))
        made, keyed, first_in, summed, counted, moved, starts_out, starts_in, tri = (
            sem("prep_made"), sem("keys_made"), sem("next_first_in"), sem("below_summed"), sem("prep_counted"),
            sem("keys_stored"), sem("starts_stored"), sem("starts_turned"), sem("triangle_made"))
        node = sb("dst_number", [P, T])
        keys = sb("keys", [P, T, 2])
        window = sb("dst_window", [P, T], I32)
        inner = sb("dst_in_window", [P, T], I32)
        window_f, inner_f = sb("dst_window_f", [P, T]), sb("dst_in_window_f", [P, T])
        next_i, next_f = sb("next_first_int", [P, 1], I32), sb("next_first", [P, 1])
        below, ones = sb("triangle", [P, P]), sb("ones", [P, P])
        column, through = sb("column_count", [P, J]), sb("columns_through", [P, J])
        start, last = sb("node_start", [P, J]), sb("node_last", [P, J])
        part, turned_starts = sb("last_part", [P, J]), sb("turned_starts", [J, WG], I32)
        drop = sb("drop_any", [P, T])
        block = ctx.enter_context(nc.Block())

        @block.gpsimd
        def _(pool):
            nc.gpsimd.memset(ones[:, :], 1.0).then_inc(tri, 1)
            nc.gpsimd.memset(below[:, :], 1.0).then_inc(tri, 1)
            pool.wait_ge(tri, 2)
            nc.gpsimd.affine_select(out=below[:, :], in_=below[:, :], compare_op=ALU.is_gt, fill=0.0, base=0,
                                    pattern=[[1, P]], channel_multiplier=-1).then_inc(tri, 1)

        @block.sync
        def _(sp):
            sp.wait_ge(made, 1)
            sp.dma_start(next_i[0:P - 2, :], ins["dst"][T:T * (P - 1)].rearrange("(p t) -> p t", t=T)[:, 0:1],
                         allow_slow_non_contiguous=True).then_inc(first_in, 16)
            sp.dma_start(next_i[P - 2:P - 1, :], ins["dst"][T * (P - 1):T * (P - 1) + 1].rearrange("(p t) -> p t", t=1)) \
                .then_inc(first_in, 16)
            sp.wait_ge(keyed, 2)
            sp.dma_start(b.dram.keys.rearrange("(p t) k -> p (t k)", t=T), keys[:, :, :].rearrange("p t k -> p (t k)")) \
                .then_inc(moved, 16)
            sp.wait_ge(starts_in, 1)
            sp.dma_start(b.dram.starts.rearrange("a (j w) -> (a j) w", w=WG), turned_starts[:, :]).then_inc(starts_out, 16)
            sp.wait_ge(starts_out, 16)
            sp.wait_ge(moved, 16)

        @block.vector
        def _(dve):
            n = [0]

            def step(ins_):
                n[0] += 1
                ins_.then_inc(made, 1)
                dve.wait_ge(made, n[0])

            step(nc.vector.memset(next_i[:, :], NP))
            step(nc.vector.scalar_tensor_tensor(out=node[:, :], in0=edges.dst_place[:, :], scalar=float(P),
                                                in1=edges.dst_part[:, :], op0=ALU.mult, op1=ALU.add))
            step(nc.vector.memset(same[:, :], 0.0))
            step(nc.vector.tensor_tensor(same[:, 1:T], node[:, 1:T], node[:, 0:T - 1], ALU.is_equal))
            dve.wait_ge(first_in, 32)
            step(nc.vector.tensor_copy(next_f[:, :], next_i[:, :]))
            step(nc.vector.tensor_tensor(cont[:, :], next_f[:, :], node[:, T - 1:T], ALU.is_equal))
            step(nc.vector.tensor_tensor(drop[:, 1:T], node[:, 1:T], node[:, 0:T - 1], ALU.is_lt))
            step(nc.vector.tensor_tensor(drop[:, 0:1], next_f[:, :], node[:, T - 1:T], ALU.is_lt))
            step(nc.vector.memset(unsorted[:, :], 0.0))
            step(nc.vector.tensor_reduce(unsorted[:, 0:1], drop[:, :], AX.X, ALU.max))
            step(nc.vector.tensor_scalar(window[:, :], edges.dst[:, :], WBITS, None, ALU.logical_shift_right))
            step(nc.vector.tensor_scalar(inner[:, :], edges.dst[:, :], WD - 1, None, ALU.bitwise_and))
            step(nc.vector.tensor_copy(window_f[:, :], window[:, :]))
            step(nc.vector.tensor_copy(inner_f[:, :], inner[:, :]))
            nc.vector.tensor_copy(keys[:, :, 0:1], edges.src_part[:, :].unsqueeze(2)).then_inc(keyed, 1)
            step(nc.vector.scalar_tensor_tensor(out=inner_f[:, :], in0=edges.src_place[:, :], scalar=float(WD),
                                                in1=inner_f[:, :], op0=ALU.mult, op1=ALU.add))
            step(nc.vector.scalar_tensor_tensor(out=inner_f[:, :], in0=window_f[:, :], scalar=float(WC),
                                                in1=inner_f[:, :], op0=ALU.mult, op1=ALU.add))
            step(nc.vector.tensor_scalar(node[:, :], node[:, :], float(N), float(2 * NP * J), ALU.is_ge, ALU.mult))
            nc.vector.tensor_tensor(keys[:, :, 1:2], inner_f[:, :].unsqueeze(2), node[:, :].unsqueeze(2), ALU.add).then_inc(keyed, 1)
            dve.wait_ge(summed, 1)
            step(nc.vector.tensor_copy(column[:, :], b.banks[:, 1, 0:J]))
            step(nc.vector.tensor_tensor_scan(through[:, :], column[:, :], b.zeros[:, 0:J], 0.0, ALU.add, ALU.add))
            step(nc.vector.tensor_tensor(start[:, :], through[:, :], column[:, :], ALU.subtract))
            step(nc.vector.tensor_tensor(start[:, :], start[:, :], b.banks[:, 0, 0:J], ALU.add))
            nc.vector.tensor_copy(column[:, :], start[:, :]).then_inc(counted, 1)
            step(nc.vector.tensor_tensor(last[:, :], start[:, :], b.in_deg[:, :], ALU.add))
            step(nc.vector.tensor_scalar(last[:, :], last[:, :], -1.0, 0.0, ALU.add, ALU.max))
            step(nc.vector.tensor_scalar(part[:, :], last[:, :], 1.0 / T, 0.5 / T - 0.5, ALU.mult, ALU.add))
            step(nc.vector.tensor_scalar(part[:, :], part[:, :], ROUND, None, ALU.add))
            step(nc.vector.tensor_scalar(part[:, :], part[:, :], ROUND, None, ALU.subtract))
            step(nc.vector.tensor_scalar(part[:, :], part[:, :], float(TD - T), float(TD - T), ALU.mult, ALU.add))
            step(nc.vector.tensor_tensor(last_row[:, :], last[:, :], part[:, :], ALU.add))
            dve.wait_ge(summed, 2)
            step(nc.vector.tensor_copy(turned_starts[:, :].unsqueeze(2),
                                       b.banks[0:J, 2, 0:P].rearrange("j (w d) -> j w d", d=WD)[:, :, 0:1]))
            dve.sem_inc(starts_in, 1)
            dve.wait_ge(keyed, 2)

        @block.tensor
        def _(pe):
            pe.wait_ge(tri, 3)
            nc.tensor.matmul(b.banks[:, 0, 0:J], below[:, :], b.in_deg[:, :], start=True, stop=True)
            nc.tensor.matmul(b.banks[:, 1, 0:J], ones[:, :], b.in_deg[:, :], start=True, stop=True).then_inc(summed, 1)
            pe.wait_ge(counted, 1)
            nc.tensor.transpose(b.banks[0:J, 2, 0:P], start[:, :], b.ident[:, :]).then_inc(summed, 1)


def messages_and_counts(nc, b, edges, same, tail):
    Q = 4
    QC, QW = G // Q, WG // Q
    with ExitStack() as ctx:
        sem = lambda name: ctx.enter_context(nc.semaphore(f"{name}_{b.tag}"))
        sb = lambda name, shape, dt=FP32: ctx.enter_context(nc.sbuf_tensor(f"{name}_{b.tag}", shape, dt))
        gathered = [sem(f"gathered{s}") for s in range(SLOTS)]
        attrs_in = [sem(f"attrs_in{s}") for s in range(SLOTS)]
        keys_in = [sem(f"keys_in{s}") for s in range(SLOTS)]
        sums_out = [sem(f"sums_out{s}") for s in range(SLOTS)]
        counts_out = [sem(f"counts_out{s}") for s in range(SLOTS)]
        indexed, taken, passed, turned, turn_read, mixed, mix_read, summed = (
            sem("indexed"), sem("rows_taken"), sem("passed"), sem("pairs_turned"), sem("pairs_read"), sem("mixed"),
            sem("mix_read"), sem("run_summed"))
        hot, counted, count_read, local_made, filled, starts_in, tailed = (
            sem("window_hot"), sem("window_counted"), sem("counts_read"), sem("keys_local"), sem("loop_filled"),
            sem("starts_loaded"), sem("tail_kept"))
        idx = sb("idx", [P, SLOTS, G], I32)
        rows = sb("rows", [P, SLOTS, G, 64])
        turn = sb("turn", [P, 2, 2 * P])
        sums = sb("run_sums", [P, SLOTS, G, DH])
        starts = sb("starts", [1, WINDOWS], I32)
        keys = sb("window_keys", [P, SLOTS, WG, 2])
        local = sb("local_keys", [P, SLOTS, WG])
        base = sb("window_base", [P, 1])
        iota_i, iota_w = sb("iota_wide_int", [P, WC], I32), sb("iota_wide", [P, WC], FP16)
        part_hot = sb("window_src_hot", [P, 2, QW, P], BF16)
        place_hot = sb("window_place_hot", [P, 2, QW, WC], BF16)
        stage = sb("count_stage", [P, SLOTS, J, P], U8)
        block = ctx.enter_context(nc.Block())
        T_BANK, M_BANK, C_BANK = (0, 1), 2, (4, 6)
        n_loops = J // SLOTS

        @block.gpsimd
        def _(pool):
            nc.gpsimd.iota(iota_i[:, :], pattern=[[1, WC]], base=0, channel_multiplier=0).then_inc(filled, 1)
            with pool.Fori(0, n_loops) as i:
                for s in range(SLOTS):
                    g = i * SLOTS + s
                    pool.wait_ge(turned, (g + 1) * Q)
                    pool.sem_inc(taken, 1)
                    nc.gpsimd.tensor_copy(idx[:, s, :], edges.src[:, bass.ds(g * G, G)]).then_inc(indexed, 1)
                    pool.wait_ge(indexed, g + 1)
                    pool.sem_inc(taken, 1)
                    for c in range(G):
                        pool.indirect_dma_start(out=rows[:, s, c, 0:DN], out_offset=None, in_=b.dram.table,
                                                in_offset=bass.IndirectOffsetOnAxis(ap=idx[:, s, c:c + 1], axis=0)) \
                            .then_inc(gathered[s], 16)

        @block.sync
        def _(sp):
            sp.dma_start(starts[:, :], b.dram.starts).then_inc(starts_in, 16)
            sp.wait_ge(starts_in, 16)
            attrs = b.dram.attrs.rearrange("(p t) d -> p t d", t=T)
            firsts = [sp.alloc_register(f"window_first{w}") for w in range(8)]
            sp.wait_ge(filled, 6)

            def store(s, at):
                sp.dma_start(b.dram.running[:, bass.ds(at * G, G) if not isinstance(at, int) else slice(at * G, (at + 1) * G), :],
                             sums[:, s, :, :]).then_inc(sums_out[s], 16)
                sp.dma_start(b.dram.counts[bass.ds(at, 1)].rearrange("a p j c -> (a p) (j c)"),
                             stage[:, s, :, :].rearrange("p j c -> p (j c)")).then_inc(counts_out[s], 16)

            with sp.Fori(0, n_loops) as i:
                for s in range(SLOTS):
                    g = i * SLOTS + s
                    sp.wait_ge(turned, (g + 1) * Q)
                    sp.sem_inc(passed, 1)
                    sp.dma_start(rows[:, s, :, DN:DI], attrs[:, bass.ds(g * G, G), :]).then_inc(attrs_in[s], 16)
                    sp.wait_ge(summed, g * G + G + 1)
                    sp.sem_inc(passed, 1)
                    sp.wait_ge(count_read, (g + 1) * (WG // 2))
                    sp.sem_inc(passed, 1)
                    store(s, g)
                    sp.wait_ge(hot, (g + 1) * (2 * WG))
                    sp.sem_inc(passed, 1)
                    for w in range(0, WG, 8):
                        for k in range(0, 8, 4):
                            sp.reg_load(firsts[k:k + 4], starts[0:1, bass.ds(g * WG + (w + k), 4)])
                        for k in range(8):
                            first = sp.snap(firsts[k], min_val=0, max_val=E)
                            sp.dma_start(keys[:, s, w + k, :], b.dram.keys[bass.ds(first, P), :]).then_inc(keys_in[s], 16)
            for s in range(SLOTS):
                sp.wait_ge(summed, SLOTS * G + J * G - (SLOTS - 1 - s) * G)
                sp.wait_ge(count_read, (SLOTS + J - (SLOTS - 1 - s)) * (WG // 2))
                store(s, J + s)
            for s in range(SLOTS):
                sp.wait_ge(sums_out[s], (n_loops + 1) * 16)
                sp.wait_ge(counts_out[s], (n_loops + 1) * 16)

        @block.vector
        def _(dve):
            nc.vector.memset(rows[:, :, :, DN:64], 0.0).then_inc(filled, 1)
            nc.vector.memset(sums[:, :, :, :], 0.0).then_inc(filled, 1)
            nc.vector.memset(stage[:, :, :, :], 0).then_inc(filled, 1)
            nc.vector.memset(base[:, :], 0.0).then_inc(filled, 1)
            dve.wait_ge(filled, 5)
            nc.vector.memset(rows[:, :, :, DI:DI + 1], 1.0).then_inc(filled, 1)
            nc.vector.tensor_copy(iota_w[:, :], iota_i[:, :]).then_inc(filled, 1)
            dve.wait_ge(filled, 7)
            dve.sem_inc(hot, SLOTS * 2 * WG)
            dve.sem_inc(summed, SLOTS * G)
            with dve.Fori(0, n_loops) as i:
                for s in range(SLOTS):
                    g = i * SLOTS + s
                    dve.wait_ge(keys_in[s], (i + 1) * (WG * 16))
                    nc.vector.tensor_scalar(local[:, s, :].unsqueeze(2), keys[:, s, :, 1:2], base[:, :], None,
                                            ALU.subtract).then_inc(local_made, 1)
                    dve.wait_ge(local_made, g * 2 + 1)
                    nc.vector.tensor_scalar(base[:, :], base[:, :], float(WG * WC), None, ALU.add).then_inc(local_made, 1)
                    for q in range(Q):
                        dve.wait_ge(counted, g * (WG // 2) + (q + 1) * (QW // 2))
                        for w in range(QW):
                            k = q * QW + w
                            nc.vector.tensor_scalar(part_hot[:, q % 2, w, :], b.iota16[:, :], keys[:, s, k, 0:1], None,
                                                    ALU.is_equal).then_inc(hot, 1)
                            nc.vector.tensor_scalar(place_hot[:, q % 2, w, :], iota_w[:, :], float(k * WC), local[:, s, k:k + 1],
                                                    ALU.add, ALU.is_equal).then_inc(hot, 1)
                        for c in range(q * QC, (q + 1) * QC):
                            if c % QC == 0:
                                dve.wait_ge(mix_read, g * Q + q + 2)
                            before = sums[:, s, c - 1, :] if c else sums[:, 1 - s, G - 1, :]
                            dve.wait_ge(summed, SLOTS * G + g * G + c)
                            nc.vector.scalar_tensor_tensor(out=sums[:, s, c, :], in0=before, scalar=same[:, bass.ds(g * G + c, 1)],
                                                           in1=sums[:, s, c, :], op0=ALU.mult, op1=ALU.add).then_inc(summed, 1)
            dve.wait_ge(summed, SLOTS * G + T)
            nc.vector.tensor_copy(tail[:, :], sums[:, SLOTS - 1, G - 1, :]).then_inc(tailed, 1)
            dve.wait_ge(tailed, 1)

        @block.scalar
        def _(act):
            act.wait_ge(filled, 7)
            act.sem_inc(turn_read, 1)
            act.sem_inc(mix_read, 1)
            act.sem_inc(count_read, SLOTS * (WG // 2))
            with act.Fori(0, n_loops) as i:
                for s in range(SLOTS):
                    g = i * SLOTS + s

                    def read_counts(r):
                        at = C_BANK[r % 2]
                        act.wait_ge(counted, SLOTS * (QW // 2) + g * (WG // 2) + (r + 1))
                        act.sem_inc(passed, 1)
                        to = stage[:, s, :, 2 * r * WD:(2 * r + 2) * WD].bitcast(FP8).rearrange("p j (w d) -> p w j d", d=WD)
                        of = b.banks[:, at:at + 2, 0:WC].rearrange("p w (j d) -> p w j d", d=WD)
                        nc.scalar.activation(to, of, ACT.Copy, scale=0.5, saturate=True).then_inc(count_read, 1)

                    act.wait_ge(counts_out[s], (i + 1) * 16)
                    act.wait_ge(sums_out[s], (i + 1) * 16)
                    act.sem_inc(passed, 1)
                    for q in range(Q):
                        m = q % 2
                        act.wait_ge(turned, SLOTS * Q + g * Q + (q + 1))
                        nc.scalar.copy(turn[:, m, :], b.banks[:, T_BANK[m], 0:2 * P]).then_inc(turn_read, 1)
                        read_counts(q * (QW // 2))
                        read_counts(q * (QW // 2) + 1)
                        act.wait_ge(mixed, 2 * g * Q + 2 * (q + 1))
                        nc.scalar.activation(sums[:, s, q * QC:(q + 1) * QC, :].rearrange("p (k o) d -> p o k d", o=2),
                                             b.banks[:, M_BANK:M_BANK + 2, 0:QC // 2 * DH].rearrange("p o (k d) -> p o k d", d=DH),
                                             ACT.Relu).then_inc(mix_read, 1)
                        read_counts(q * (QW // 2) + 2)
                        read_counts(q * (QW // 2) + 3)

        @block.tensor
        def _(pe):
            pe.sem_inc(turned, SLOTS * Q)
            pe.sem_inc(counted, SLOTS * (QW // 2))
            with pe.Fori(0, n_loops) as i:
                for s in range(SLOTS):
                    g = i * SLOTS + s

                    def count(r):
                        pe.wait_ge(hot, SLOTS * 2 * WG + g * (2 * WG) + 4 * (r + 1))
                        pe.wait_ge(count_read, g * (WG // 2) + (r + WG - 1))
                        for k in range(2):
                            w = (2 * r + k) % QW
                            m = (r // (QW // 2)) % 2
                            last = nc.tensor.matmul(b.banks[:, C_BANK[r % 2] + k, 0:WC], part_hot[:, m, w, :],
                                                    place_hot[:, m, w, :], start=True, stop=True)
                        last.then_inc(counted, 1)

                    pe.wait_ge(gathered[s], (i + 1) * (G * 16))
                    pe.wait_ge(attrs_in[s], (i + 1) * 16)
                    for q in range(Q):
                        m = q % 2
                        for k in range(QC // 2):
                            c = q * QC + 2 * k
                            last = nc.tensor.transpose(b.banks[:, T_BANK[m], k * P:(k + 1) * P],
                                                       rows[:, s, c:c + 2, :].rearrange("p c d -> p (c d)"), b.ident[:, :])
                        last.then_inc(turned, 1)
                        count(q * (QW // 2))
                        count(q * (QW // 2) + 1)
                        pe.wait_ge(turn_read, g * Q + (q + 2))
                        pe.wait_ge(mix_read, g * Q + (q + 1))
                        for k in range(QC):
                            at = 64 * (k % 2)
                            last = nc.tensor.matmul(b.banks[:, M_BANK + k % 2, k // 2 * DH:(k // 2 + 1) * DH],
                                                    turn[at:at + DI + 1, m, (k // 2) * P:(k // 2 + 1) * P],
                                                    b.w1a[at:at + DI + 1, :], start=True, stop=True)
                            if k >= QC - 2:
                                last.then_inc(mixed, 1)
                        count(q * (QW // 2) + 2)
                        count(q * (QW // 2) + 3)


def sums_of_nodes(nc, b, edges, agg_tile, cont, last_row, tail):
    C = 7
    with ExitStack() as ctx:
        sem = lambda name: ctx.enter_context(nc.semaphore(f"{name}_{b.tag}"))
        sb = lambda name, shape, dt=FP32: ctx.enter_context(nc.sbuf_tensor(f"{name}_{b.tag}", shape, dt))
        fetched = [sem(f"fetched{s}") for s in range(SLOTS)]
        pointed, copied, has_made, spread_made, carried, added, passed = (
            sem("pointed"), sem("copied"), sem("has_made"), sem("carry_spread"), sem("carried"), sem("carry_added"),
            sem("fetch_passed"))
        idx, got = sb("last_idx", [P, SLOTS, C], I32), sb("last_rows", [P, SLOTS, C, DH])
        has = sb("has_edges", [P, J])
        end_hot, spread = sb("end_hot", [P, P]), sb("carry_rows", [P, J * DN])
        block = ctx.enter_context(nc.Block())
        agg = per_node(agg_tile[:, :], DH + 1)
        rows_of = b.dram.running.rearrange("p t d -> (p t) d")

        @block.gpsimd
        def _(pool):
            with pool.Fori(0, J // (C * SLOTS)) as i:
                for s in range(SLOTS):
                    g = i * SLOTS + s
                    pool.wait_ge(copied, g + 1)
                    pool.sem_inc(passed, 1)
                    nc.gpsimd.tensor_copy(idx[:, s, :], last_row[:, bass.ds(g * C, C)]).then_inc(pointed, 1)
                    pool.wait_ge(pointed, g + 1)
                    pool.sem_inc(passed, 1)
                    for c in range(C):
                        pool.indirect_dma_start(out=got[:, s, c, :], out_offset=None, in_=rows_of,
                                                in_offset=bass.IndirectOffsetOnAxis(ap=idx[:, s, c:c + 1], axis=0)) \
                            .then_inc(fetched[s], 16)

        @block.vector
        def _(dve):
            dve.sem_inc(copied, SLOTS)
            nc.vector.tensor_scalar(has[:, :], b.in_deg[:, :], 0.0, None, ALU.is_gt).then_inc(has_made, 1)
            nc.vector.tensor_scalar(end_hot[:, :], b.iota[:, :], edges.dst_part[:, T - 1:T], cont[:, :],
                                    ALU.is_equal, ALU.mult).then_inc(has_made, 1)
            dve.wait_ge(has_made, 2)
            with dve.Fori(0, J // (C * SLOTS)) as i:
                for s in range(SLOTS):
                    g = i * SLOTS + s
                    dve.wait_ge(fetched[s], (i + 1) * (C * 16))
                    at = bass.ds(g * C, C)
                    nc.vector.tensor_tensor(agg[:, at, 0:DH], got[:, s, :, :],
                                            has[:, at].unsqueeze(2).broadcast_to([P, C, DH]), ALU.mult).then_inc(copied, 1)
            dve.wait_ge(copied, SLOTS + J // C)
            for third in range(DH // DN):
                if third:
                    dve.wait_ge(carried, third)
                nc.vector.scalar_tensor_tensor(
                    out=per_node(spread[:, :]), in0=spread_over(b.iota[:, 0:J]), scalar=edges.dst_place[:, T - 1:T],
                    in1=tail[:, third * DN:(third + 1) * DN].unsqueeze(1).broadcast_to([P, J, DN]),
                    op0=ALU.is_equal, op1=ALU.mult).then_inc(spread_made, 1)
                dve.wait_ge(carried, third + 1)
                for z in range(ZB):
                    to = agg[:, z * ZJ:(z + 1) * ZJ, third * DN:(third + 1) * DN]
                    nc.vector.tensor_tensor(to, to, b.banks[:, z, 0:ZW].rearrange("p (j d) -> p j d", d=DN),
                                            ALU.add).then_inc(added, 1)
                dve.wait_ge(added, (third + 1) * ZB)

        @block.tensor
        def _(pe):
            for third in range(DH // DN):
                pe.wait_ge(spread_made, third + 1)
                if third:
                    pe.wait_ge(added, third * ZB)
                for z in range(ZB):
                    last = nc.tensor.matmul(b.banks[:, z, 0:ZW], end_hot[:, :], spread[:, z * ZW:(z + 1) * ZW],
                                            start=True, stop=True)
                last.then_inc(carried, 1)


SPLITS = 3
WF = SPLITS * DN + 1
TILES = 4
HEAD = J % TILES
BLOCKS = J // TILES
KC = 14
CHUNKS = J // KC
assert HEAD == 2 and BLOCKS % 2 == 0 and J % KC == 0


def propagate(nc, b, exact):
    with ExitStack() as ctx:
        sem = lambda name: ctx.enter_context(nc.semaphore(f"{name}_{b.tag}"))
        sb = lambda name, shape, dt=FP32: ctx.enter_context(nc.sbuf_tensor(f"{name}_{b.tag}", shape, dt))
        chunk_in = [sem(f"chunk_in{k}") for k in range(CHUNKS)]
        head_in, prepared, started, swept, drained, folded, fresh, passed, chain, stacked = (
            sem("head_in"), sem("prop_prepared"), sem("prop_started"), sem("chunk_used"), sem("block_drained"),
            sem("block_folded"), sem("parts_fresh"), sem("sweep_passed"), sem("fresh_chain"), sem("stack_made"))
        folds_read = sem("folds_read")
        parts = sb("feature_parts", [P, 2, J, WF], BF16)
        head = sb("head_counts", [P, HEAD, J, P], U8)
        ring = sb("count_ring", [P, CHUNKS, TILES, KC, P], U8)
        drain = sb("drained", [WF, 2, TILES * P])
        stack = sb("stacked_identities", [WF, DN + 1])
        gain = sb("target_gain", [P, J])
        expect = sb("expected_in_deg", [P, J])
        scaled, rest = sb("scaled", [P, TILES * DN]), sb("rest", [P, TILES * DN])
        block = ctx.enter_context(nc.Block())
        SWEEP, FOLD = (0, 1), (2, 3)
        steps2 = STEPS // 2
        CHAIN = 3 + 2 * SPLITS

        @block.sync
        def _(sp):
            sp.dma_start(head[:, :, :, :].rearrange("p a j c -> p a (j c)"),
                         b.dram.counts[SLOTS:SLOTS + HEAD].rearrange("a p j c -> p a (j c)")).then_inc(head_in, 16)
            with sp.Fori(0, STEPS) as t:
                with sp.Fori(0, BLOCKS) as m:
                    for k in range(CHUNKS):
                        sp.wait_ge(swept, t * (BLOCKS * CHUNKS) + m * CHUNKS + (k + 1))
                        sp.sem_inc(passed, 1)
                        sp.dma_start(ring[:, k, :, :, :].rearrange("p a j c -> p a (j c)"),
                                     b.dram.counts[bass.ds(m * TILES + (SLOTS + HEAD), TILES), :, k * KC:(k + 1) * KC, :]
                                     .rearrange("a p j c -> p a (j c)")).then_inc(chunk_in[k], 16)
            for k in range(CHUNKS):
                sp.wait_ge(chunk_in[k], STEPS * BLOCKS * 16)

        @block.gpsimd
        def _(pool):
            nc.gpsimd.memset(stack[:, :], 0.0).then_inc(stacked, 1)
            for k in range(SPLITS):
                pool.wait_ge(stacked, k + 1)
                nc.gpsimd.affine_select(out=stack[:, 0:DN], in_=stack[:, 0:DN], compare_op=ALU.not_equal, fill=2.0,
                                        base=-k * DN, pattern=[[-1, DN]], channel_multiplier=1).then_inc(stacked, 1)
            nc.gpsimd.affine_select(out=stack[:, DN:DN + 1], in_=stack[:, DN:DN + 1], compare_op=ALU.not_equal, fill=2.0,
                                    base=-SPLITS * DN, pattern=[[0, 1]], channel_multiplier=1).then_inc(stacked, 1)
            pool.wait_ge(prepared, 1)
            nc.gpsimd.affine_select(out=expect[:, J - 1:J], in_=expect[:, J - 1:J], compare_op=ALU.is_ge, fill=0.0,
                                    base=NL - 1, pattern=[[0, 1]], channel_multiplier=-1).then_inc(stacked, 1)

        @block.scalar
        def _(act):
            def drain_block(n, parity, cols):
                nc.scalar.copy(drain[:, parity, 0:cols], b.banks[0:WF, SWEEP[parity], 0:cols]).then_inc(drained, 1)

            act.sem_inc(drained, 1)
            act.wait_ge(started, 1)
            drain_block(0, 0, HEAD * P)
            with act.Fori(0, STEPS) as t:
                with act.Fori(0, BLOCKS // 2) as mm:
                    for odd in (1, 0):
                        act.wait_ge(swept, (t * BLOCKS + mm * 2) * CHUNKS + (3 - odd) * CHUNKS)
                        act.wait_ge(folded, t * (BLOCKS + 1) + mm * 2 + (2 - odd))
                        drain_block(None, odd, TILES * P)
                act.wait_ge(started, t + 2)
                act.wait_ge(folded, (t + 1) * (BLOCKS + 1) + 1)
                drain_block(None, 0, HEAD * P)

        @block.vector
        def _(dve):
            nc.vector.tensor_copy(expect[:, :], b.in_deg[:, :]).then_inc(prepared, 1)
            nc.vector.memset(drain[:, :, :], 0.0).then_inc(prepared, 1)
            nc.vector.memset(parts[:, :, :, SPLITS * DN:WF], 1.0).then_inc(prepared, 1)
            nc.vector.tensor_scalar(gain[:, :], b.dst_norm[:, :], 1.0 - ALPHA, None, ALU.mult).then_inc(prepared, 1)
            nc.vector.tensor_tensor(per_node(b.f[:, :]), per_node(b.h[:, :]), spread_over(b.src_norm[:, :]), ALU.mult).then_inc(prepared, 1)
            for k in range(SPLITS):
                dve.wait_ge(prepared, 5 + 2 * k)
                part = parts[:, 0, :, k * DN:(k + 1) * DN]
                nc.vector.tensor_copy(part, per_node(b.f[:, :])).then_inc(prepared, 1)
                if k < SPLITS - 1:
                    dve.wait_ge(prepared, 6 + 2 * k)
                    nc.vector.tensor_tensor(per_node(b.f[:, :]), per_node(b.f[:, :]), part, ALU.subtract).then_inc(prepared, 1)
            dve.wait_ge(stacked, SPLITS + 3)
            dve.sem_inc(folds_read, 1)

            def new_features(n, side, parity, at, tiles):
                dve.wait_ge(folded, n + 2)
                got = per_node(b.banks[:, FOLD[parity], 0:tiles * (DN + 1)], DN + 1)
                where = at if isinstance(at, slice) else bass.ds(at, tiles)
                t1, t2 = per_node(scaled[:, 0:tiles * DN]), per_node(rest[:, 0:tiles * DN])
                f, h = per_node(b.f[:, :])[:, where, :], per_node(b.h[:, :])[:, where, :]
                spread = lambda column: column[:, where].unsqueeze(2).broadcast_to([P, tiles, DN])
                steps = [0]

                def step(ins_):
                    steps[0] += 1
                    ins_.then_inc(chain, 1)
                    dve.wait_ge(chain, n * CHAIN + steps[0])

                step(nc.vector.tensor_tensor(exact[:, where].unsqueeze(2), got[:, :, DN:DN + 1], expect[:, where].unsqueeze(2),
                                             ALU.is_equal))
                step(nc.vector.tensor_tensor(t1, got[:, :, 0:DN], spread(gain), ALU.mult))
                dve.sem_inc(folds_read, 1)
                step(nc.vector.scalar_tensor_tensor(out=f, in0=h, scalar=ALPHA, in1=t1, op0=ALU.mult, op1=ALU.add))
                step(nc.vector.tensor_tensor(t1, f, spread(b.src_norm), ALU.mult))
                for k in range(SPLITS):
                    part = parts[:, 1 - side, where, k * DN:(k + 1) * DN]
                    of, left = (t1, t2) if k % 2 == 0 else (t2, t1)
                    step(nc.vector.tensor_copy(part, of))
                    if k < SPLITS - 1:
                        step(nc.vector.tensor_tensor(left, of, part, ALU.subtract))
                assert steps[0] == CHAIN
                dve.sem_inc(fresh, 1)

            with dve.Fori(0, steps2) as tt:
                for side in range(2):
                    n = (tt * 2 + side) * (BLOCKS + 1)
                    new_features(n, side, 0, slice(0, HEAD), HEAD)
                    with dve.Fori(0, BLOCKS // 2) as mm:
                        for odd in (1, 0):
                            new_features(n + (mm * 2 + (2 - odd)), side, odd, mm * (2 * TILES) + (HEAD + (1 - odd) * TILES), TILES)

        @block.tensor
        def _(pe):
            def sweep_tile(bank, cols, side, j, matrix):
                return nc.tensor.matmul(b.banks[0:WF, bank, 0:cols], parts[:, side, j, :], matrix.bitcast(FP8),
                                        start=(j == 0), stop=(j == J - 1))

            def fold(parity, tiles):
                for a in range(tiles):
                    last = nc.tensor.matmul(b.banks[:, FOLD[parity], a * (DN + 1):(a + 1) * (DN + 1)],
                                            drain[:, parity, a * P:(a + 1) * P], stack[:, :], start=True, stop=True)
                last.then_inc(folded, 1)

            def head_block(side, known, before):
                for j in range(J):
                    if j in before:
                        before[j]()
                    if (j - HEAD) % TILES == 0 or j == 0:
                        known(0 if j == 0 else (j - HEAD) // TILES + 1)
                    last = sweep_tile(SWEEP[0], HEAD * P, side, j, head[:, :, j, :])
                return last

            pe.wait_ge(stacked, SPLITS + 3)
            pe.wait_ge(head_in, 16)
            pe.sem_inc(swept, CHUNKS)
            pe.wait_ge(prepared, 4 + 2 * SPLITS)
            pe.sem_inc(folded, 1)
            head_block(0, lambda n: None, {}).then_inc(started, 1)
            with pe.Fori(0, steps2) as tt:
                for side in range(2):
                    t = tt * 2 + side
                    with pe.Fori(0, BLOCKS // 2) as mm:
                        for odd in (1, 0):
                            u = 1 if odd else 0
                            n = t * (BLOCKS + 1) + mm * 2 + (1 - u)
                            for k in range(CHUNKS):
                                pe.wait_ge(chunk_in[k], (t * BLOCKS + mm * 2 + (1 - u) + 1) * 16)
                                if k == 0:
                                    pe.wait_ge(drained, n + 1)
                                pe.sem_inc(passed, 1)
                                for j in range(k * KC, (k + 1) * KC):
                                    last = sweep_tile(SWEEP[u], TILES * P, side, j, ring[:, k, :, j - k * KC, :])
                                last.then_inc(swept, 1)
                                if k == 0:
                                    pe.wait_ge(drained, n + 2)
                                    pe.wait_ge(folds_read, n + 1)
                                    pe.sem_inc(passed, 1)
                                    fold(1 - u, TILES)
                    last_n = t * (BLOCKS + 1) + BLOCKS

                    def known(n_block, side=side, last_n=last_n):
                        pe.wait_ge(fresh, last_n - BLOCKS + n_block + 1)
                        pe.sem_inc(passed, 1)

                    def last_fold(last_n=last_n):
                        pe.wait_ge(drained, last_n + 2)
                        pe.wait_ge(folds_read, last_n + 1)
                        pe.sem_inc(passed, 1)
                        fold(0, TILES)

                    pe.wait_ge(drained, last_n + 2)
                    pe.sem_inc(passed, 1)
                    head_block(1 - side, known, {KC: last_fold}).then_inc(started, 1)


def needs_general(nc, b, exact, unsorted, flag):
    with nc.semaphore("flag_made") as made, nc.semaphore("flag_turned") as turned, \
            nc.sbuf_tensor("bad_rows", [P, 2], FP32) as bad, nc.Block() as block:
        @block.vector
        def _(dve):
            nc.vector.tensor_reduce(bad[:, 0:1], exact[:, :], AX.X, ALU.min).then_inc(made, 1)
            dve.wait_ge(made, 1)
            nc.vector.tensor_scalar(bad[:, 0:1], bad[:, 0:1], -1.0, 1.0, ALU.mult, ALU.add).then_inc(made, 1)
            dve.wait_ge(made, 2)
            nc.vector.tensor_tensor(bad[:, 0:1], bad[:, 0:1], unsorted[:, :], ALU.max).then_inc(made, 1)
            dve.wait_ge(turned, 1)
            nc.vector.tensor_reduce(bad[0:1, 1:2], b.banks[0:1, 0, 0:P], AX.X, ALU.max).then_inc(made, 1)
            dve.wait_ge(made, 4)
            nc.vector.tensor_copy(flag[:, :], bad[0:1, 1:2]).then_inc(made, 1)
            dve.wait_ge(made, 5)

        @block.tensor
        def _(pe):
            pe.wait_ge(made, 3)
            nc.tensor.matmul(b.banks[0:1, 0, 0:P], bad[:, 0:1], b.ident[:, :], start=True, stop=True).then_inc(turned, 1)


def general_way(nc, ins, out, dram):
    with ExitStack() as ctx:
        b = Kept(nc, ctx, dram, "any")
        edges = Edges(nc, ctx, "any")
        agg_tile = ctx.enter_context(nc.sbuf_tensor("agg_nodes_any", [P, J * (DH + 1)], FP32))
        setup(nc, b, edges, ins)
        degrees(nc, b, edges)
        general_layers(nc, b, edges, agg_tile)
        store_result(nc, b, out)




def fast_way(nc, ins, out, dram, flag):
    with ExitStack() as ctx:
        b = Kept(nc, ctx, dram, "fast")
        exact = ctx.enter_context(nc.sbuf_tensor("counts_exact", [P, J], FP32))
        unsorted = ctx.enter_context(nc.sbuf_tensor("unsorted", [P, 1], FP32))
        with ExitStack() as edge_ctx:
            sb = lambda name, shape: edge_ctx.enter_context(nc.sbuf_tensor(name, shape, FP32))
            edges = Edges(nc, edge_ctx, "fast")
            same, cont, last_row, tail = sb("same_target", [P, T]), sb("run_goes_on", [P, 1]), sb("last_row", [P, J]), sb("last_sums", [P, DH])
            setup(nc, b, edges, ins)
            degrees(nc, b, edges)
            layer_norm_relu(nc, b, "in")
            store_table(nc, b, b.h)
            prepare_sorted(nc, b, edges, ins, (same, cont, last_row, unsorted))
            messages_and_counts(nc, b, edges, same, tail)
            agg_tile = sb("agg_nodes_fast", [P, J * (DH + 1)])
            sums_of_nodes(nc, b, edges, agg_tile, cont, last_row, tail)
            node_mlp(nc, b, agg_tile)
        layer_norm_relu(nc, b, "mid")
        propagate(nc, b, exact)
        needs_general(nc, b, exact, unsorted, flag)
        store_result(nc, b, out)


def program(nc, ins, out):
    dram = Dram(nc)
    with nc.sbuf_tensor("general_flag", [1, 1], I32) as flag:
        fast_way(nc, ins, out, dram, flag)
        bad = nc.values_load(flag[0:1, 0:1], min_val=0, max_val=1)
        with nc.If(bad > 0):
            nc.all_engine_barrier()
            general_way(nc, ins, out, dram)


INPUTS = ["x", "src", "dst", "edge_attr_16", "L0_gnn_w1a", "L0_gnn_b1a", "L0_gnn_w1b", "L0_gnn_b1b",
          "L0_gnn_w2a", "L0_gnn_b2a", "L0_gnn_w2b", "L0_gnn_b2b"]


def kernel(**inputs):
    import numpy as np
    import concourse.bacc as bacc
    from concourse.bass_utils import run_bass_kernel_spmd

    nc = bacc.Bacc("TRN2", target_bir_lowering=False, num_devices=1)
    arrays, ins = {}, {}
    for name in INPUTS:
        a = np.ascontiguousarray(inputs[name])
        arrays[f"in_{name}"] = a
        ins[name] = nc.dram_tensor(f"in_{name}", a.shape, mybir.dt.from_np(a.dtype), kind="ExternalInput").ap()
    out = nc.dram_tensor("out_nodes", (N, DN), FP32, kind="ExternalOutput").ap()
    program(nc, ins, out)
    result = run_bass_kernel_spmd(nc, [arrays], core_ids=[0])
    return result.results[0]["out_nodes"]
```

```python
from contextlib import ExitStack

import concourse.bass as bass
from concourse import mybir

FP32 = mybir.dt.float32
BF16 = mybir.dt.bfloat16
FP16 = mybir.dt.float16
FP8 = mybir.dt.float8e3
U8 = mybir.dt.uint8
I32 = mybir.dt.int32
ALU = mybir.AluOpType
ACT = mybir.ActivationFunctionType
AX = mybir.AxisListType

P = 128
N = 12500
E = 200000
DN = 32
DE = 16
DI = DN + DE
DH = 2 * DI
STEPS = 10
ALPHA = 0.1
EPS = 1e-5

J = -(-N // P)
NP = P * J
NL = N - P * (J - 1)
G = 16
T = 1568
EP = P * T
EL = E - (P - 1) * T
PAD_NODE = NP - 1
BITS = 7
ROUND = 12582912.0
ZB = 7
ZJ = J // ZB
ZW = ZJ * DN
PLACES_HERE = 6
SLOTS = 2
WD = 4
WBITS = 2
WINDOWS = NP // WD
WG = P // WD
WC = WD * J
TD = T + SLOTS * G
assert P == 1 << BITS and WD == 1 << WBITS and T == J * G and WC <= 512 and T % G == 0 and NP > N and EP >= E and J % ZB == 0 and ZW <= 512


def per_node(tile, d=DN):
    return tile.rearrange("p (j d) -> p j d", d=d)


def spread_over(column, d=DN):
    return column.unsqueeze(2).broadcast_to([P, J, d])


def row_vector(v):
    return v.rearrange("(a d) -> a d", a=1)


class Dram:

    def __init__(self, nc):
        dram = lambda name, shape, dt=FP32: nc.dram_tensor(name, shape, dt).ap()
        self.table = dram("row_table", (NP, DN))
        self.attrs = dram("attrs_padded", (EP, DE))
        self.keys = dram("edge_keys", (EP, 2))
        self.running = dram("running_sums", (P, TD, DH))
        self.counts = dram("edge_counts", (J + SLOTS, P, J, P), U8)


class Kept:

    def __init__(self, nc, ctx, dram, tag):
        self.tag, self.dram = tag, dram
        sb = lambda name, shape, dt=FP32: ctx.enter_context(nc.sbuf_tensor(f"{name}_{tag}", shape, dt))
        self.banks = ctx.enter_context(nc.psum_tensor(f"banks_{tag}", [P, 8, 512], FP32))
        self.x = sb("x_nodes", [P, J * DN])
        self.h = sb("h_nodes", [P, J * DN])
        self.f = sb("f_nodes", [P, J * DN])
        self.in_deg = sb("in_deg", [P, J])
        self.in_cap = sb("in_cap", [P, J])
        self.out_cap = sb("out_cap", [P, J])
        self.in_inv = sb("in_inv", [P, J])
        self.src_norm = sb("src_norm", [P, J])
        self.dst_norm = sb("dst_norm", [P, J])
        self.iota = sb("iota_row", [P, P])
        self.iota16 = sb("iota_row16", [P, P], BF16)
        self.ident = sb("identity", [P, P])
        self.zeros = sb("zeros", [P, 512])
        self.zeros16 = sb("zeros16", [P, P], BF16)
        self.w1a = sb("w1a_b1a", [P, DH])
        self.w1b = sb("w1b_b1b", [DH + 1, DH])
        self.w2a_h = sb("w2a_h", [DN, DI])
        self.w2a_agg = sb("w2a_agg", [DH, DI])
        self.b2a = sb("b2a_col", [DI, 1])
        self.w2b = sb("w2b_b2b", [P, DN])


class Edges:

    def __init__(self, nc, ctx, tag):
        sb = lambda name, shape, dt=FP32: ctx.enter_context(nc.sbuf_tensor(f"{name}_{tag}", shape, dt))
        self.src = sb("src_ends", [P, T], I32)
        self.dst = sb("dst_ends", [P, T], I32)
        self.src_part = sb("src_part", [P, T])
        self.src_place = sb("src_place", [P, T])
        self.dst_part = sb("dst_part", [P, T])
        self.dst_place = sb("dst_place", [P, T])


def setup(nc, b, edges, ins):
    with ExitStack() as ctx:
        sem = lambda name: ctx.enter_context(nc.semaphore(f"{name}_{b.tag}"))
        sb = lambda name, shape, dt=FP32: ctx.enter_context(nc.sbuf_tensor(f"{name}_{b.tag}", shape, dt))
        filled, loaded, attrs_copied, iotas, ident_made, split = (
            sem("filled"), sem("loaded"), sem("attrs_copied"), sem("iotas"), sem("ident_made"), sem("split"))
        zero_rows = sb("zero_rows", [P, (EP - E) * DE // 64])
        iota_i = sb("iota_int", [P, P], I32)
        low, high = sb("end_low", [P, T], I32), sb("end_high", [P, T], I32)
        block = ctx.enter_context(nc.Block())
        LOADS = 17

        @block.sync
        def _(sp):
            cut = lambda t: t.rearrange("(a r) d -> a (r d)", a=320)
            sp.dma_start(cut(b.dram.attrs[0:E, :]), cut(ins["edge_attr_16"])).then_inc(attrs_copied, 16)
            sp.wait_ge(filled, 8)
            sp.dma_start(b.dram.attrs[E:EP, :].rearrange("(p r) d -> p (r d)", p=64), zero_rows[0:64, :]).then_inc(attrs_copied, 16)
            x = ins["x"]
            sp.dma_start(per_node(b.x[:, :])[:, 0:J - 1, :], x[0:P * (J - 1), :].rearrange("(j p) d -> p j d", p=P)).then_inc(loaded, 16)
            sp.dma_start(b.x[0:NL, (J - 1) * DN:J * DN], x[P * (J - 1):N, :]).then_inc(loaded, 16)
            for tile, ends in ((edges.src, ins["src"]), (edges.dst, ins["dst"])):
                sp.dma_start(tile[0:P - 1, :], ends[0:(P - 1) * T].rearrange("(p t) -> p t", t=T)).then_inc(loaded, 16)
                sp.dma_start(tile[P - 1:P, 0:EL], ends[(P - 1) * T:E].rearrange("(p t) -> p t", p=1)).then_inc(loaded, 16)
            for at in (0, 64):
                sp.dma_start(b.w1a[at:at + DI, :], ins["L0_gnn_w1a"]).then_inc(loaded, 16)
                sp.dma_start(b.w1a[at + DI:at + DI + 1, :], row_vector(ins["L0_gnn_b1a"])).then_inc(loaded, 16)
            sp.dma_start(b.w1b[0:DH, :], ins["L0_gnn_w1b"]).then_inc(loaded, 16)
            sp.dma_start(b.w1b[DH:DH + 1, :], row_vector(ins["L0_gnn_b1b"])).then_inc(loaded, 16)
            sp.dma_start(b.w2a_h[:, :], ins["L0_gnn_w2a"][0:DN, :]).then_inc(loaded, 16)
            sp.dma_start(b.w2a_agg[:, :], ins["L0_gnn_w2a"][DN:DN + DH, :]).then_inc(loaded, 16)
            sp.dma_start(b.b2a[:, :], ins["L0_gnn_b2a"].rearrange("(d a) -> d a", a=1)).then_inc(loaded, 16)
            sp.dma_start(b.w2b[0:DI, :], ins["L0_gnn_w2b"]).then_inc(loaded, 16)
            sp.dma_start(b.w2b[64:65, :], row_vector(ins["L0_gnn_b2b"])).then_inc(loaded, 16)
            sp.wait_ge(loaded, LOADS * 16)
            sp.wait_ge(attrs_copied, 32)

        @block.gpsimd
        def _(pool):
            nc.gpsimd.iota(iota_i[:, :], pattern=[[1, P]], base=0, channel_multiplier=0).then_inc(iotas, 1)
            nc.gpsimd.memset(b.ident[:, :], 0.0).then_inc(ident_made, 1)
            pool.wait_ge(ident_made, 1)
            nc.gpsimd.affine_select(out=b.ident[:, :], in_=b.ident[:, :], compare_op=ALU.not_equal, fill=1.0,
                                    base=0, pattern=[[-1, P]], channel_multiplier=1).then_inc(ident_made, 1)
            pool.wait_ge(ident_made, 2)

        @block.vector
        def _(dve):
            for tile, value in ((zero_rows, 0.0), (b.x, 0.0), (edges.src, PAD_NODE), (edges.dst, PAD_NODE), (b.zeros, 0.0),
                                (b.w2b, 0.0), (b.w1a, 0.0), (b.zeros16, 0.0)):
                nc.vector.memset(tile[:, :], value).then_inc(filled, 1)
            dve.wait_ge(iotas, 1)
            nc.vector.tensor_copy(b.iota[:, :], iota_i[:, :]).then_inc(filled, 1)
            nc.vector.tensor_copy(b.iota16[:, :], iota_i[:, :]).then_inc(filled, 1)
            dve.wait_ge(filled, 10)
            dve.wait_ge(loaded, LOADS * 16)
            n = 0
            for ends, part, place in ((edges.src, edges.src_part, edges.src_place), (edges.dst, edges.dst_part, edges.dst_place)):
                nc.vector.tensor_scalar(low[:, :], ends[:, :], P - 1, None, ALU.bitwise_and).then_inc(split, 1)
                nc.vector.tensor_scalar(high[:, :], ends[:, :], BITS, None, ALU.logical_shift_right).then_inc(split, 1)
                dve.wait_ge(split, n + 2)
                nc.vector.tensor_copy(part[:, :], low[:, :]).then_inc(split, 1)
                nc.vector.tensor_copy(place[:, :], high[:, :]).then_inc(split, 1)
                n += 4
                dve.wait_ge(split, n)
            nc.vector.scalar_tensor_tensor(out=edges.src[:, :], in0=edges.src_part[:, :], scalar=float(J), in1=edges.src_place[:, :],
                                           op0=ALU.mult, op1=ALU.add).then_inc(split, 1)
            dve.wait_ge(split, n + 1)


def inverse_root(nc, dve, root, value, term, done, n):
    nc.vector.reciprocal(root, root).then_inc(done, 1)
    dve.wait_ge(done, n + 1)
    nc.vector.tensor_tensor(term, root, root, ALU.mult).then_inc(done, 1)
    dve.wait_ge(done, n + 2)
    nc.vector.tensor_tensor(term, term, value, ALU.mult).then_inc(done, 1)
    dve.wait_ge(done, n + 3)
    nc.vector.tensor_scalar(term, term, -0.5, 1.5, ALU.mult, ALU.add).then_inc(done, 1)
    dve.wait_ge(done, n + 4)
    nc.vector.tensor_tensor(root, root, term, ALU.mult).then_inc(done, 1)
    dve.wait_ge(done, n + 5)


def layer_norm_relu(nc, b, tag):
    tag = f"{tag}_{b.tag}"
    """b.h = relu(layer norm of b.x), node by node."""
    with ExitStack() as ctx:
        done = ctx.enter_context(nc.semaphore(f"ln_done_{tag}"))
        rooted = ctx.enter_context(nc.semaphore(f"ln_rooted_{tag}"))
        mean = ctx.enter_context(nc.sbuf_tensor(f"ln_mean_{tag}", [P, J], FP32))
        var = ctx.enter_context(nc.sbuf_tensor(f"ln_var_{tag}", [P, J], FP32))
        term = ctx.enter_context(nc.sbuf_tensor(f"ln_newton_{tag}", [P, J], FP32))
        square = ctx.enter_context(nc.sbuf_tensor(f"ln_square_{tag}", [P, J * DN], FP32))
        block = ctx.enter_context(nc.Block())

        @block.vector
        def _(dve):
            h = per_node(b.h[:, :])
            nc.vector.tensor_reduce(mean[:, :], per_node(b.x[:, :]), AX.X, ALU.add).then_inc(done, 1)
            dve.wait_ge(done, 1)
            nc.vector.tensor_scalar(mean[:, :], mean[:, :], 1.0 / DN, None, ALU.mult).then_inc(done, 1)
            dve.wait_ge(done, 2)
            nc.vector.tensor_tensor(h, per_node(b.x[:, :]), spread_over(mean[:, :]), ALU.subtract).then_inc(done, 1)
            dve.wait_ge(done, 3)
            nc.vector.tensor_tensor(square[:, :], b.h[:, :], b.h[:, :], ALU.mult).then_inc(done, 1)
            dve.wait_ge(done, 4)
            nc.vector.tensor_reduce(var[:, :], per_node(square[:, :]), AX.X, ALU.add).then_inc(done, 1)
            dve.wait_ge(done, 5)
            nc.vector.tensor_scalar(var[:, :], var[:, :], 1.0 / DN, EPS, ALU.mult, ALU.add).then_inc(done, 1)
            dve.wait_ge(done, 6)
            dve.wait_ge(rooted, 1)
            inverse_root(nc, dve, mean[:, :], var[:, :], term[:, :], done, 6)
            nc.vector.tensor_tensor(h, h, spread_over(mean[:, :]), ALU.mult).then_inc(done, 1)
            dve.wait_ge(done, 12)
            nc.vector.tensor_scalar(b.h[:, :], b.h[:, :], 0.0, None, ALU.max).then_inc(done, 1)
            dve.wait_ge(done, 13)

        @block.scalar
        def _(act):
            act.wait_ge(done, 6)
            nc.scalar.sqrt(mean[:, :], var[:, :]).then_inc(rooted, 1)


def store_table(nc, b, tile):
    tag = b.tag
    """The gather table's rows are the tile's."""
    with nc.semaphore(f"table_stored_{tag}") as stored, nc.Block() as block:
        @block.sync
        def _(sp):
            sp.dma_start(b.dram.table.rearrange("(p j) d -> p (j d)", j=J), tile[:, :]).then_inc(stored, 16)
            sp.wait_ge(stored, 16)


def degrees(nc, b, edges, sides):
    with ExitStack() as ctx:
        sem = lambda name: ctx.enter_context(nc.semaphore(f"{name}_{b.tag}"))
        sb = lambda name, shape, dt=FP32: ctx.enter_context(nc.sbuf_tensor(f"{name}_{b.tag}", shape, dt))
        hot, stages, place_made, used, summed, normed, rooted = (sem("hot_made"), sem("places_staged"), sem("place_hot_made"), sem("hot_used"), sem("deg_summed"),
                                                         sem("deg_normed"), sem("deg_rooted"))
        term = sb("deg_newton", [P, J])
        part_hot = sb("part_hot", [P, 2, sides, G // 2, P], BF16)
        place_hot = sb("place_hot", [P, 2, sides, G // 2, J], BF16)
        staged = sb("places_staged", [P, 2, sides, G // 2])
        count = b.banks
        block = ctx.enter_context(nc.Block())
        H = G // 2
        ends = ((edges.dst_part, edges.dst_place), (edges.src_part, edges.src_place))[0:sides]
        norms = ((b.in_cap, b.dst_norm), (b.out_cap, b.src_norm))[0:sides]

        @block.gpsimd
        def _(pool):
            with pool.Fori(0, T // G) as i:
                for s in range(2):
                    pool.wait_ge(used, i * 2 + s + 1)
                    for k, (_, place) in enumerate(ends):
                        nc.gpsimd.tensor_copy(staged[:, s, k, :], place[:, bass.ds((i * 2 + s) * H, H)]).then_inc(stages, 1)
                        pool.wait_ge(stages, (i * 2 + s) * (2 * sides) + (2 * k + 1))
                        pool.sem_inc(stages, 1)
                        for c in range(PLACES_HERE, H):
                            nc.gpsimd.tensor_scalar(place_hot[:, s, k, c, :], b.iota16[:, 0:J], staged[:, s, k, c:c + 1],
                                                    None, ALU.is_equal).then_inc(place_made, 1)

        @block.vector
        def _(dve):
            with dve.Fori(0, T // G) as i:
                for s in range(2):
                    dve.wait_ge(used, i * 2 + s + 1)
                    for k, (part, place) in enumerate(ends):
                        for c in range(H):
                            col = bass.ds((i * 2 + s) * H + c, 1)
                            nc.vector.tensor_scalar(part_hot[:, s, k, c, :], b.iota16[:, :], part[:, col], None,
                                                    ALU.is_equal).then_inc(hot, 1)
                            if c < PLACES_HERE:
                                nc.vector.tensor_scalar(place_hot[:, s, k, c, :], b.iota16[:, 0:J], place[:, col], None,
                                                        ALU.is_equal).then_inc(hot, 1)
            dve.wait_ge(summed, 1)
            nc.vector.tensor_copy(b.in_deg[:, :], count[:, 0, 0:J]).then_inc(normed, 1)
            for k, (cap, _) in enumerate(norms):
                nc.vector.tensor_scalar(cap[:, :], count[:, k, 0:J], 1.0, None, ALU.max).then_inc(normed, 1)
            dve.wait_ge(normed, 1 + sides)
            nc.vector.reciprocal(b.in_inv[:, :], b.in_cap[:, :]).then_inc(normed, 1)
            dve.wait_ge(rooted, sides)
            for k, (cap, norm) in enumerate(norms):
                inverse_root(nc, dve, norm[:, :], cap[:, :], term[:, :], normed, 2 + sides + 5 * k)

        @block.scalar
        def _(act):
            act.wait_ge(normed, 1 + sides)
            for cap, norm in norms:
                nc.scalar.sqrt(norm[:, :], cap[:, :]).then_inc(rooted, 1)

        @block.tensor
        def _(pe):
            zero = lambda k, **flags: nc.tensor.matmul(count[:, k, 0:J], b.zeros16[:, 0:P], b.zeros16[:, 0:J],
                                                       skip_group_check=True, **flags)
            for k in range(sides):
                last = zero(k, start=True, stop=False)
            last.then_inc(used, 2)
            with pe.Fori(0, T // G) as i:
                for s in range(2):
                    pe.wait_ge(hot, (i * 2 + s + 1) * (sides * (H + PLACES_HERE)))
                    pe.wait_ge(place_made, (i * 2 + s + 1) * (sides * (H - PLACES_HERE)))
                    for k in range(sides):
                        for c in range(H):
                            last = nc.tensor.matmul(count[:, k, 0:J], part_hot[:, s, k, c, :], place_hot[:, s, k, c, :],
                                                    start=False, stop=False, skip_group_check=True)
                    last.then_inc(used, 1)
            for k in range(sides):
                last = zero(k, start=False, stop=True)
            last.then_inc(summed, 1)


def edge_sums(nc, b, edges, agg_tile, messages, s, tiles, third=None):
    idx, rows, turn, msg, part_hot, spread, w_third = tiles
    sums, work = b.banks, b.banks[:, ZB, :]
    sums_to = per_node(agg_tile[:, :], DH + 1) if messages else per_node(b.f[:, :])
    with nc.Block() as block:
        @block.gpsimd
        def _(pool):
            with pool.Fori(0, T // G) as i:
                pool.wait_ge(s["idx_ready"], i + 1)
                pool.sem_inc(s["taken"], 1)
                for c in range(G):
                    pool.indirect_dma_start(out=rows[:, c, 0:DN], out_offset=None, in_=b.dram.table,
                                            in_offset=bass.IndirectOffsetOnAxis(ap=idx[:, c:c + 1], axis=0)) \
                        .then_inc(s["gathered"], 16)
                pool.wait_ge(s["gathered"], (i + 1) * (G * 16))
                pool.sem_inc(s["rows_ready"], 1)
            pool.inc_swdge_sem([s["gathered"]], [T * 16], mode="sub")

        if messages:
            @block.sync
            def _(sp):
                attrs = b.dram.attrs.rearrange("(p t) d -> p t d", t=T)
                with sp.Fori(0, T // G) as i:
                    sp.wait_ge(s["idx_ready"], i + 1)
                    sp.sem_inc(s["taken"], 1)
                    sp.dma_start(rows[:, :, DN:DI], attrs[:, bass.ds(i * G, G), :]).then_inc(s["attrs"], 16)
                    sp.wait_ge(s["attrs"], (i + 1) * 16)
                    sp.sem_inc(s["attrs_ready"], 1)

            @block.scalar
            def _(act):
                with act.Fori(0, T // G) as i:
                    for c in range(0, G, 2):
                        act.wait_ge(s["turned"], i * (G // 2) + c // 2 + 1)
                        nc.scalar.copy(turn[:, :], work[:, 0:P]).then_inc(s["turn_read"], 1)

        @block.vector
        def _(dve):
            nc.vector.memset(rows[:, :, DN:64], 0.0).then_inc(s["ones"], 1)
            dve.wait_ge(s["ones"], 1)
            nc.vector.memset(rows[:, :, DI:DI + 1], 1.0).then_inc(s["ones"], 1)
            if messages:
                nc.vector.tensor_copy(w_third[:, :], b.w1a[:, bass.ds(third * DN, DN)]).then_inc(s["ones"], 1)
            dve.wait_ge(s["ones"], 3 if messages else 2)
            with dve.Fori(0, T // G) as i:
                nc.vector.tensor_copy(idx[:, :], edges.src[:, bass.ds(i * G, G)]).then_inc(s["idx_ready"], 1)
                dve.wait_ge(s["rows_ready"], i + 1)
                for c in range(G):
                    n, r = i * G + c, c % 2
                    row = rows[:, c, 0:DN]
                    if messages:
                        dve.wait_ge(s["mixed"], n + 1)
                        nc.vector.tensor_scalar(msg[:, r, :], work[:, 256:256 + DN], 0.0, None, ALU.max).then_inc(s["mix_read"], 1)
                        dve.wait_ge(s["mix_read"], n + 2)
                        row = msg[:, r, :]
                    dve.wait_ge(s["used"], n + 1)
                    nc.vector.tensor_scalar(part_hot[:, r, :], b.iota[:, :], edges.dst_part[:, bass.ds(n, 1)], None,
                                            ALU.is_equal).then_inc(s["hot"], 1)
                    nc.vector.scalar_tensor_tensor(
                        out=per_node(spread[:, r, :]), in0=spread_over(b.iota[:, 0:J]), scalar=edges.dst_place[:, bass.ds(n, 1)],
                        in1=row.unsqueeze(1).broadcast_to([P, J, DN]), op0=ALU.is_equal, op1=ALU.mult).then_inc(s["hot"], 1)
                dve.wait_ge(s["hot"], (i + 1) * (2 * G))
            dve.wait_ge(s["summed"], 1)
            for z in range(ZB):
                to = (sums_to[:, z * ZJ:(z + 1) * ZJ, bass.ds(third * DN, DN)] if messages
                      else sums_to[:, z * ZJ:(z + 1) * ZJ, :])
                nc.vector.tensor_copy(to, sums[:, z, 0:ZW].rearrange("p (j d) -> p j d", d=DN)).then_inc(s["copied"], 1)
            dve.wait_ge(s["copied"], ZB)

        @block.tensor
        def _(pe):
            def zero(z, **flags):
                return nc.tensor.matmul(sums[:, z, 0:ZW], b.zeros[:, 0:P], b.zeros[:, 0:ZW], skip_group_check=True, **flags)
            for z in range(ZB):
                last = zero(z, start=True, stop=False)
            last.then_inc(s["used"], 2)
            pe.sem_inc(s["mix_read"], 1)
            with pe.Fori(0, T // G) as i:
                for c in range(G):
                    n, r = i * G + c, c % 2
                    if messages:
                        if c == 0:
                            pe.wait_ge(s["rows_ready"], i + 1)
                            pe.wait_ge(s["attrs_ready"], i + 1)
                        pe.wait_ge(s["mix_read"], n + 1)
                        if c % 2 == 0:
                            nc.tensor.transpose(work[:, 0:P], rows[:, c:c + 2, :].rearrange("p c d -> p (c d)"),
                                                b.ident[:, :]).then_inc(s["turned"], 1)
                            pe.wait_ge(s["turn_read"], i * (G // 2) + c // 2 + 1)
                        at = 64 * (c % 2)
                        nc.tensor.matmul(work[:, 256:256 + DN], turn[at:at + DI + 1, :], w_third[at:at + DI + 1, :],
                                         start=True, stop=True).then_inc(s["mixed"], 1)
                    pe.wait_ge(s["hot"], (n + 1) * 2)
                    for z in range(ZB):
                        last = nc.tensor.matmul(sums[:, z, 0:ZW], part_hot[:, r, :], spread[:, r, z * ZW:(z + 1) * ZW],
                                                start=False, stop=False, skip_group_check=True)
                    last.then_inc(s["used"], 1)
            for z in range(ZB):
                last = zero(z, start=False, stop=True)
            last.then_inc(s["summed"], 1)


def node_mlp(nc, b, agg_tile):
    B = 2
    with ExitStack() as ctx:
        tag = b.tag
        sem = lambda name: ctx.enter_context(nc.semaphore(f"mlp_{name}_{tag}"))
        staged, turned, turn_read, agg_mixed, agg_read, hidden, hidden_read, out_made, out_added, filled = (
            sem("staged"), sem("tiles_turned"), sem("tiles_turn_read"), sem("agg_mixed"), sem("agg_mix_read"),
            sem("hidden_made"), sem("hidden_read"), sem("out_made"), sem("out_added"), sem("mid_filled"))
        agg_in = ctx.enter_context(nc.sbuf_tensor(f"agg_in_{tag}", [P, B, DH + 1], FP32))
        h_in = ctx.enter_context(nc.sbuf_tensor(f"h_in_{tag}", [P, B, DN], FP32))
        agg_t = ctx.enter_context(nc.sbuf_tensor(f"agg_t_{tag}", [DH + 1, B * P], FP32))
        h_t = ctx.enter_context(nc.sbuf_tensor(f"h_t_{tag}", [DN, B * P], FP32))
        mix = ctx.enter_context(nc.sbuf_tensor(f"agg_mix_{tag}", [DH, B * P], FP32))
        mid = ctx.enter_context(nc.sbuf_tensor(f"mid_{tag}", [P, B * P], FP32))
        block = ctx.enter_context(nc.Block())
        ps = b.banks
        agg = per_node(agg_tile[:, :], DH + 1)
        h = per_node(b.h[:, :])

        @block.vector
        def _(dve):
            nc.vector.memset(mid[:, :], 0.0).then_inc(filled, 1)
            dve.wait_ge(filled, 1)
            nc.vector.memset(mid[64:65, :], 1.0).then_inc(filled, 1)
            nc.vector.tensor_copy(agg[:, :, DH:DH + 1], b.in_deg[:, :].unsqueeze(2)).then_inc(filled, 1)
            dve.wait_ge(filled, 3)
            with dve.Fori(0, J // B) as i:
                at = bass.ds(i * B, B)
                nc.vector.tensor_tensor(agg_in[:, :, :], agg[:, at, :],
                                        b.in_inv[:, at].unsqueeze(2).broadcast_to([P, B, DH + 1]), ALU.mult).then_inc(staged, 1)
                nc.vector.tensor_copy(h_in[:, :, :], h[:, at, :]).then_inc(staged, 1)
                dve.wait_ge(turned, i + 1)
                nc.vector.tensor_copy(agg_t[:, :], ps[0:DH + 1, 0, 0:B * P]).then_inc(turn_read, 1)
                nc.vector.tensor_copy(h_t[:, :], ps[0:DN, 4, 0:B * P]).then_inc(turn_read, 1)
                dve.wait_ge(out_made, i + 1)
                x = per_node(b.x[:, :])[:, at, :]
                nc.vector.tensor_tensor(x, x, ps[:, 3, 0:B * DN].rearrange("p (j d) -> p j d", d=DN),
                                        ALU.add).then_inc(out_added, 1)
            dve.wait_ge(out_added, J // B)

        @block.scalar
        def _(act):
            act.wait_ge(filled, 2)
            with act.Fori(0, J // B) as i:
                act.wait_ge(agg_mixed, i + 1)
                nc.scalar.copy(mix[:, :], ps[0:DH, 1, 0:B * P]).then_inc(agg_read, 1)
                act.wait_ge(hidden, i + 1)
                nc.scalar.activation(mid[0:DI, :], ps[0:DI, 2, 0:B * P], ACT.Relu, bias=b.b2a[:, :]).then_inc(hidden_read, 1)

        @block.tensor
        def _(pe):
            with pe.Fori(0, J // B) as i:
                pe.wait_ge(staged, 2 * i + 2)
                for c in range(B):
                    nc.tensor.transpose(ps[0:DH + 1, 0, c * P:(c + 1) * P], agg_in[:, c, :], b.ident[:, :])
                    last = nc.tensor.transpose(ps[0:DN, 4, c * P:(c + 1) * P], h_in[:, c, :], b.ident[:, :])
                last.then_inc(turned, 1)
                pe.wait_ge(turn_read, 2 * i + 2)
                nc.tensor.matmul(ps[0:DH, 1, 0:B * P], b.w1b[:, :], agg_t[:, :], start=True, stop=True).then_inc(agg_mixed, 1)
                pe.wait_ge(agg_read, i + 1)
                nc.tensor.matmul(ps[0:DI, 2, 0:B * P], b.w2a_h[:, :], h_t[:, :], start=True, stop=False)
                nc.tensor.matmul(ps[0:DI, 2, 0:B * P], b.w2a_agg[:, :], mix[:, :], start=False, stop=True).then_inc(hidden, 1)
                pe.wait_ge(hidden_read, i + 1)
                for c in range(B):
                    last = nc.tensor.matmul(ps[:, 3, c * DN:(c + 1) * DN], mid[0:65, c * P:(c + 1) * P], b.w2b[0:65, :],
                                            start=True, stop=True)
                last.then_inc(out_made, 1)
                pe.wait_ge(out_added, i + 1)


GATHER_SEMS = ("idx_ready", "taken", "rows_ready", "attrs", "attrs_ready", "turned", "turn_read", "ones", "mixed", "mix_read", "used", "hot",
               "summed", "copied", "scaled", "stored")


def general_layers(nc, b, edges, agg_tile):
    with ExitStack() as ctx:
        s = {name: ctx.enter_context(nc.semaphore(f"any_{name}")) for name in GATHER_SEMS}
        low, high = s["idx_ready"].num, s["stored"].num
        assert high - low == len(GATHER_SEMS) - 1
        s["gathered"] = ctx.enter_context(nc.semaphore("any_gathered"))
        sb = lambda name, shape, dt=FP32: ctx.enter_context(nc.sbuf_tensor(f"any_{name}", shape, dt))
        tiles = (sb("idx", [P, G], I32), sb("rows", [P, G, 64]), sb("turn", [P, P]), sb("msg", [P, 2, DN]),
                 sb("part_hot", [P, 2, P]), sb("spread", [P, 2, J * DN]), sb("w_third", [P, DN]))
        spread = tiles[5]

        def start_again():
            nc.gpsimd.sem_clear(range(low, high + 1))
            nc.all_engine_barrier()

        layer_norm_relu(nc, b, "in")
        store_table(nc, b, b.h)
        with nc.Fori(0, DH // DN) as third:
            edge_sums(nc, b, edges, agg_tile, True, s, tiles, third)
            start_again()
        node_mlp(nc, b, agg_tile)
        layer_norm_relu(nc, b, "mid")
        with nc.Block() as block:
            @block.vector
            def _(dve):
                nc.vector.tensor_copy(b.f[:, :], b.h[:, :]).then_inc(s["scaled"], 1)
                dve.wait_ge(s["scaled"], 1)
        start_again()
        with nc.Fori(0, STEPS) as step:
            with nc.Block() as block:
                @block.vector
                def _(dve):
                    nc.vector.tensor_tensor(per_node(spread[:, 0, :]), per_node(b.f[:, :]), spread_over(b.src_norm[:, :]),
                                            ALU.mult).then_inc(s["scaled"], 1)

                @block.sync
                def _(sp):
                    sp.wait_ge(s["scaled"], 1)
                    sp.dma_start(b.dram.table.rearrange("(p j) d -> p (j d)", j=J), spread[:, 0, :]).then_inc(s["stored"], 16)
                    sp.wait_ge(s["stored"], 16)
            start_again()
            edge_sums(nc, b, edges, agg_tile, False, s, tiles)
            start_again()
            with nc.Block() as block:
                @block.vector
                def _(dve):
                    combine(nc, dve, b, s["scaled"])
            start_again()


def combine(nc, dve, b, scaled):
    nc.vector.tensor_tensor(per_node(b.f[:, :]), per_node(b.f[:, :]), spread_over(b.dst_norm[:, :]), ALU.mult).then_inc(scaled, 1)
    dve.wait_ge(scaled, 1)
    nc.vector.tensor_scalar(b.f[:, :], b.f[:, :], 1.0 - ALPHA, None, ALU.mult).then_inc(scaled, 1)
    dve.wait_ge(scaled, 2)
    nc.vector.scalar_tensor_tensor(out=b.f[:, :], in0=b.h[:, :], scalar=ALPHA, in1=b.f[:, :], op0=ALU.mult,
                                   op1=ALU.add).then_inc(scaled, 1)
    dve.wait_ge(scaled, 3)


def store_result(nc, b, out):
    with nc.semaphore(f"result_added_{b.tag}") as added, nc.semaphore(f"result_stored_{b.tag}") as stored, nc.Block() as block:
        @block.vector
        def _(dve):
            nc.vector.tensor_tensor(b.f[:, :], b.f[:, :], b.x[:, :], ALU.add).then_inc(added, 1)

        @block.sync
        def _(sp):
            sp.wait_ge(added, 1)
            sp.dma_start(out[0:P * (J - 1), :].rearrange("(j p) d -> p j d", p=P), per_node(b.f[:, :])[:, 0:J - 1, :]).then_inc(stored, 16)
            sp.dma_start(out[P * (J - 1):N, :], b.f[0:NL, (J - 1) * DN:J * DN]).then_inc(stored, 16)
            sp.wait_ge(stored, 32)



def prepare_sorted(nc, b, edges, ins, kept):
    same, cont, last_row, window_row, unsorted = kept
    with ExitStack() as ctx:
        sem = lambda name: ctx.enter_context(nc.semaphore(f"{name}_{b.tag}"))
        sb = lambda name, shape, dt=FP32: ctx.enter_context(nc.sbuf_tensor(f"{name}_{b.tag}", shape, dt))
        made, keyed, first_in, summed, counted, moved, tri = (
            sem("prep_made"), sem("keys_made"), sem("next_first_in"), sem("below_summed"), sem("prep_counted"),
            sem("keys_stored"), sem("triangle_made"))
        node = sb("dst_number", [P, T])
        keys = sb("keys", [P, T, 2])
        window = sb("dst_window", [P, T], I32)
        inner = sb("dst_in_window", [P, T], I32)
        window_f, inner_f = sb("dst_window_f", [P, T]), sb("dst_in_window_f", [P, T])
        next_i, next_f = sb("next_first_int", [P, 1], I32), sb("next_first", [P, 1])
        below, ones = sb("triangle", [P, P]), sb("ones", [P, P])
        column, through = sb("column_count", [P, J]), sb("columns_through", [P, J])
        start, last = sb("node_start", [P, J]), sb("node_last", [P, J])
        part, first_of = sb("last_part", [P, J]), sb("first_of_window", [P, WG])
        drop = sb("drop_any", [P, T])
        block = ctx.enter_context(nc.Block())

        @block.gpsimd
        def _(pool):
            nc.gpsimd.memset(ones[:, :], 1.0).then_inc(tri, 1)
            nc.gpsimd.memset(below[:, :], 1.0).then_inc(tri, 1)
            pool.wait_ge(tri, 2)
            nc.gpsimd.affine_select(out=below[:, :], in_=below[:, :], compare_op=ALU.is_gt, fill=0.0, base=0,
                                    pattern=[[1, P]], channel_multiplier=-1).then_inc(tri, 1)
            nc.gpsimd.memset(first_of[:, :], 0.0).then_inc(tri, 1)
            nc.gpsimd.memset(window_row[:, :], 0).then_inc(tri, 1)
            pool.wait_ge(tri, 5)
            nc.gpsimd.affine_select(out=first_of[:, :], in_=first_of[:, :], compare_op=ALU.not_equal, fill=2.0, base=0,
                                    pattern=[[-WD, WG]], channel_multiplier=1).then_inc(tri, 1)

        @block.sync
        def _(sp):
            sp.wait_ge(made, 1)
            sp.dma_start(next_i[0:P - 2, :], ins["dst"][T:T * (P - 1)].rearrange("(p t) -> p t", t=T)[:, 0:1],
                         allow_slow_non_contiguous=True).then_inc(first_in, 16)
            sp.dma_start(next_i[P - 2:P - 1, :], ins["dst"][T * (P - 1):T * (P - 1) + 1].rearrange("(p t) -> p t", t=1)) \
                .then_inc(first_in, 16)
            sp.wait_ge(keyed, 2)
            sp.dma_start(b.dram.keys.rearrange("(p t) k -> p (t k)", t=T), keys[:, :, :].rearrange("p t k -> p (t k)")) \
                .then_inc(moved, 16)
            sp.wait_ge(moved, 16)

        @block.vector
        def _(dve):
            n = [0]

            def step(ins_):
                n[0] += 1
                ins_.then_inc(made, 1)
                dve.wait_ge(made, n[0])

            step(nc.vector.memset(next_i[:, :], NP))
            step(nc.vector.scalar_tensor_tensor(out=node[:, :], in0=edges.dst_place[:, :], scalar=float(P),
                                                in1=edges.dst_part[:, :], op0=ALU.mult, op1=ALU.add))
            step(nc.vector.memset(same[:, :], 0.0))
            step(nc.vector.tensor_tensor(same[:, 1:T], node[:, 1:T], node[:, 0:T - 1], ALU.is_equal))
            dve.wait_ge(first_in, 32)
            step(nc.vector.tensor_copy(next_f[:, :], next_i[:, :]))
            step(nc.vector.tensor_tensor(cont[:, :], next_f[:, :], node[:, T - 1:T], ALU.is_equal))
            step(nc.vector.tensor_tensor(drop[:, 1:T], node[:, 1:T], node[:, 0:T - 1], ALU.is_lt))
            step(nc.vector.tensor_tensor(drop[:, 0:1], next_f[:, :], node[:, T - 1:T], ALU.is_lt))
            step(nc.vector.memset(unsorted[:, :], 0.0))
            step(nc.vector.tensor_reduce(unsorted[:, 0:1], drop[:, :], AX.X, ALU.max))
            step(nc.vector.tensor_scalar(window[:, :], edges.dst[:, :], WBITS, None, ALU.logical_shift_right))
            step(nc.vector.tensor_scalar(inner[:, :], edges.dst[:, :], WD - 1, None, ALU.bitwise_and))
            step(nc.vector.tensor_copy(window_f[:, :], window[:, :]))
            step(nc.vector.tensor_copy(inner_f[:, :], inner[:, :]))
            nc.vector.tensor_copy(keys[:, :, 0:1], edges.src_part[:, :].unsqueeze(2)).then_inc(keyed, 1)
            step(nc.vector.scalar_tensor_tensor(out=inner_f[:, :], in0=edges.src_place[:, :], scalar=float(WD),
                                                in1=inner_f[:, :], op0=ALU.mult, op1=ALU.add))
            step(nc.vector.scalar_tensor_tensor(out=inner_f[:, :], in0=window_f[:, :], scalar=float(WC),
                                                in1=inner_f[:, :], op0=ALU.mult, op1=ALU.add))
            step(nc.vector.tensor_scalar(node[:, :], node[:, :], float(N), float(2 * NP * J), ALU.is_ge, ALU.mult))
            nc.vector.tensor_tensor(keys[:, :, 1:2], inner_f[:, :].unsqueeze(2), node[:, :].unsqueeze(2), ALU.add).then_inc(keyed, 1)
            dve.wait_ge(summed, 1)
            step(nc.vector.tensor_copy(column[:, :], b.banks[:, 1, 0:J]))
            step(nc.vector.tensor_tensor_scan(through[:, :], column[:, :], b.zeros[:, 0:J], 0.0, ALU.add, ALU.add))
            step(nc.vector.tensor_tensor(start[:, :], through[:, :], column[:, :], ALU.subtract))
            step(nc.vector.tensor_tensor(start[:, :], start[:, :], b.banks[:, 0, 0:J], ALU.add))
            nc.vector.tensor_copy(column[:, :], start[:, :]).then_inc(counted, 1)
            step(nc.vector.tensor_tensor(last[:, :], start[:, :], b.in_deg[:, :], ALU.add))
            step(nc.vector.tensor_scalar(last[:, :], last[:, :], -1.0, 0.0, ALU.add, ALU.max))
            step(nc.vector.tensor_scalar(part[:, :], last[:, :], 1.0 / T, 0.5 / T - 0.5, ALU.mult, ALU.add))
            step(nc.vector.tensor_scalar(part[:, :], part[:, :], ROUND, None, ALU.add))
            step(nc.vector.tensor_scalar(part[:, :], part[:, :], ROUND, None, ALU.subtract))
            step(nc.vector.tensor_scalar(part[:, :], part[:, :], float(TD - T), float(TD - T), ALU.mult, ALU.add))
            step(nc.vector.tensor_tensor(last_row[:, :], last[:, :], part[:, :], ALU.add))
            dve.wait_ge(summed, 2)
            step(nc.vector.tensor_copy(window_row[:, 0:J], b.banks[0:WG, 2, 0:J]))
            dve.wait_ge(keyed, 2)

        @block.tensor
        def _(pe):
            pe.wait_ge(tri, 6)
            nc.tensor.matmul(b.banks[:, 0, 0:J], below[:, :], b.in_deg[:, :], start=True, stop=True)
            nc.tensor.matmul(b.banks[:, 1, 0:J], ones[:, :], b.in_deg[:, :], start=True, stop=True).then_inc(summed, 1)
            pe.wait_ge(counted, 1)
            nc.tensor.matmul(b.banks[0:WG, 2, 0:J], first_of[:, :], start[:, :], start=True, stop=True).then_inc(summed, 1)


def messages_and_counts(nc, b, edges, same, window_row, tail):
    Q = 4
    QC, QW = G // Q, WG // Q
    with ExitStack() as ctx:
        sem = lambda name: ctx.enter_context(nc.semaphore(f"{name}_{b.tag}"))
        sb = lambda name, shape, dt=FP32: ctx.enter_context(nc.sbuf_tensor(f"{name}_{b.tag}", shape, dt))
        gathered = [sem(f"gathered{s}") for s in range(SLOTS)]
        attrs_in = [sem(f"attrs_in{s}") for s in range(SLOTS)]
        keys_in = [sem(f"keys_in{s}") for s in range(SLOTS)]
        sums_out = [sem(f"sums_out{s}") for s in range(SLOTS)]
        counts_out = [sem(f"counts_out{s}") for s in range(SLOTS)]
        indexed, taken, passed, turned, turn_read, mixed, mix_read, summed = (
            sem("indexed"), sem("rows_taken"), sem("passed"), sem("pairs_turned"), sem("pairs_read"), sem("mixed"),
            sem("mix_read"), sem("run_summed"))
        hot, hot_used, counted, count_read, local_made, filled, keys_pointed, keys_turned, tailed, rooted, all_summed = (
            sem("window_hot"), sem("window_hot_used"), sem("window_counted"), sem("counts_read"), sem("keys_local"), sem("loop_filled"),
            sem("keys_pointed"), sem("keys_turned"), sem("tail_kept"), sem("out_rooted"), sem("all_summed"))
        idx = sb("idx", [P, SLOTS, G], I32)
        rows = sb("rows", [P, SLOTS, G, 64])
        turn = sb("turn", [P, 2, 2 * P])
        sums = sb("run_sums", [P, SLOTS, G, DH])
        key_idx = sb("key_idx", [WG, SLOTS], I32)
        raw_keys = sb("raw_keys", [P, SLOTS, P, 2])
        keys = sb("window_keys", [P, SLOTS, WG])
        local = sb("local_keys", [P, SLOTS, WG])
        term = sb("out_newton", [P, J])
        base = sb("window_base", [P, 1])
        iota_i, iota_w = sb("iota_wide_int", [P, WC], I32), sb("iota_wide", [P, WC], FP16)
        part_hot = sb("window_src_hot", [P, 2, QW, P], BF16)
        place_hot = sb("window_place_hot", [P, 2, QW, WC], BF16)
        stage = sb("count_stage", [P, SLOTS, J, P], U8)
        block = ctx.enter_context(nc.Block())
        T_BANK, S_BANK, M_BANK, C_BANK = 0, 1, 2, (4, 6)
        KEYS_AT = 400
        n_loops = J // SLOTS

        @block.gpsimd
        def _(pool):
            nc.gpsimd.iota(iota_i[:, :], pattern=[[1, WC]], base=0, channel_multiplier=0).then_inc(filled, 1)

            def fetch_keys(s, group):
                nc.gpsimd.tensor_copy(key_idx[:, s:s + 1], window_row[:, group]).then_inc(keys_pointed, 1)
                pool.wait_ge(keys_pointed, group_number + 1)
                pool.sem_inc(taken, 1)
                pool.indirect_dma_start(out=raw_keys[0:WG, s, :, :].rearrange("p e k -> p (e k)"), out_offset=None,
                                        in_=b.dram.keys.rearrange("e (k a) -> (e k) a", a=1),
                                        in_offset=bass.IndirectOffsetOnAxis(ap=key_idx[:, s:s + 1], axis=0)).then_inc(keys_in[s], 16)

            pool.wait_ge(filled, 8)
            group_number = 0
            fetch_keys(0, slice(0, 1))
            with pool.Fori(0, n_loops) as i:
                for s in range(SLOTS):
                    g = i * SLOTS + s
                    pool.wait_ge(turned, (g + 1) * Q)
                    pool.sem_inc(taken, 1)
                    pool.wait_ge(keys_turned, g + 1)
                    pool.sem_inc(taken, 1)
                    group_number = g + 1
                    fetch_keys(1 - s, bass.ds(g + 1, 1))
                    pool.sem_inc(taken, 1)
                    nc.gpsimd.tensor_copy(idx[:, s, :], edges.src[:, bass.ds(g * G, G)]).then_inc(indexed, 1)
                    pool.wait_ge(indexed, g + 1)
                    pool.sem_inc(taken, 1)
                    for c in range(G):
                        pool.indirect_dma_start(out=rows[:, s, c, 0:DN], out_offset=None, in_=b.dram.table,
                                                in_offset=bass.IndirectOffsetOnAxis(ap=idx[:, s, c:c + 1], axis=0)) \
                            .then_inc(gathered[s], 16)

        @block.sync
        def _(sp):
            attrs = b.dram.attrs.rearrange("(p t) d -> p t d", t=T)
            sp.wait_ge(filled, 8)

            def store(s, at):
                sp.dma_start(b.dram.running[:, bass.ds(at * G, G) if not isinstance(at, int) else slice(at * G, (at + 1) * G), :],
                             sums[:, s, :, :]).then_inc(sums_out[s], 16)
                sp.dma_start(b.dram.counts[bass.ds(at, 1)].rearrange("a p j c -> (a p) (j c)"),
                             stage[:, s, :, :].rearrange("p j c -> p (j c)")).then_inc(counts_out[s], 16)

            with sp.Fori(0, n_loops) as i:
                for s in range(SLOTS):
                    g = i * SLOTS + s
                    sp.wait_ge(turned, (g + 1) * Q)
                    sp.sem_inc(passed, 1)
                    sp.dma_start(rows[:, s, :, DN:DI], attrs[:, bass.ds(g * G, G), :]).then_inc(attrs_in[s], 16)
                    sp.wait_ge(summed, g * G + G + 1)
                    sp.sem_inc(passed, 1)
                    sp.wait_ge(count_read, (g + 1) * (WG // 2))
                    sp.sem_inc(passed, 1)
                    store(s, g)
            for s in range(SLOTS):
                sp.wait_ge(summed, SLOTS * G + J * G - (SLOTS - 1 - s) * G)
                sp.wait_ge(count_read, (SLOTS + J - (SLOTS - 1 - s)) * (WG // 2))
                store(s, J + s)
            for s in range(SLOTS):
                sp.wait_ge(sums_out[s], (n_loops + 1) * 16)
                sp.wait_ge(counts_out[s], (n_loops + 1) * 16)

        @block.vector
        def _(dve):
            nc.vector.memset(rows[:, :, :, DN:64], 0.0).then_inc(filled, 1)
            nc.vector.memset(sums[:, :, :, :], 0.0).then_inc(filled, 1)
            nc.vector.memset(stage[:, :, :, :], 0).then_inc(filled, 1)
            nc.vector.memset(base[:, :], 0.0).then_inc(filled, 1)
            nc.vector.memset(raw_keys[:, :, :, :], 0.0).then_inc(filled, 1)
            dve.wait_ge(filled, 6)
            nc.vector.memset(rows[:, :, :, DI:DI + 1], 1.0).then_inc(filled, 1)
            nc.vector.tensor_copy(iota_w[:, :], iota_i[:, :]).then_inc(filled, 1)
            dve.wait_ge(filled, 8)
            dve.sem_inc(hot, SLOTS * 2 * WG)
            dve.sem_inc(summed, SLOTS * G)
            with dve.Fori(0, n_loops) as i:
                for s in range(SLOTS):
                    g = i * SLOTS + s
                    dve.wait_ge(keys_turned, g + 2)
                    nc.vector.tensor_copy(keys[:, s, :], b.banks[:, M_BANK, KEYS_AT:KEYS_AT + WG]).then_inc(local_made, 1)
                    nc.vector.tensor_scalar(local[:, s, :], b.banks[:, M_BANK, KEYS_AT + WG:KEYS_AT + 2 * WG], base[:, :], None,
                                            ALU.subtract).then_inc(local_made, 1)
                    dve.wait_ge(local_made, g * 3 + 2)
                    nc.vector.tensor_scalar(base[:, :], base[:, :], float(WG * WC), None, ALU.add).then_inc(local_made, 1)
                    for q in range(Q):
                        dve.wait_ge(hot_used, g * (WG // 2) + (q + 1) * (QW // 2))
                        for w in range(QW):
                            k = q * QW + w
                            nc.vector.tensor_scalar(part_hot[:, q % 2, w, :], b.iota16[:, :], keys[:, s, k:k + 1], None,
                                                    ALU.is_equal).then_inc(hot, 1)
                            nc.vector.tensor_scalar(place_hot[:, q % 2, w, :], iota_w[:, :], float(k * WC), local[:, s, k:k + 1],
                                                    ALU.add, ALU.is_equal).then_inc(hot, 1)
                            if w < QW - QC:
                                continue
                            c = q * QC + w - (QW - QC)
                            if c % QC == 0:
                                dve.wait_ge(mix_read, g * Q + (q + 2))
                            before = sums[:, s, c - 1, :] if c else sums[:, 1 - s, G - 1, :]
                            dve.wait_ge(summed, g * G + (SLOTS * G + c))
                            nc.vector.scalar_tensor_tensor(out=sums[:, s, c, :], in0=before, scalar=same[:, bass.ds(g * G + c, 1)],
                                                           in1=sums[:, s, c, :], op0=ALU.mult, op1=ALU.add).then_inc(summed, 1)
            dve.wait_ge(summed, SLOTS * G + T)
            nc.vector.tensor_copy(tail[:, :], sums[:, SLOTS - 1, G - 1, :]).then_inc(tailed, 1)
            dve.wait_ge(all_summed, 1)
            nc.vector.tensor_reduce(b.src_norm[:, :], b.banks[:, S_BANK, 0:WC].rearrange("p (j d) -> p j d", d=WD), AX.X,
                                    ALU.add).then_inc(tailed, 1)
            dve.wait_ge(tailed, 2)
            nc.vector.tensor_scalar(b.out_cap[:, :], b.src_norm[:, :], 1.0, None, ALU.max).then_inc(tailed, 1)
            dve.wait_ge(rooted, 1)
            inverse_root(nc, dve, b.src_norm[:, :], b.out_cap[:, :], term[:, :], tailed, 3)

        @block.scalar
        def _(act):
            act.wait_ge(filled, 8)
            act.sem_inc(turn_read, 1)
            act.sem_inc(mix_read, 1)
            act.sem_inc(count_read, SLOTS * (WG // 2))
            with act.Fori(0, n_loops) as i:
                for s in range(SLOTS):
                    g = i * SLOTS + s

                    def read_counts(r):
                        at = C_BANK[r % 2]
                        act.wait_ge(counted, g * (WG // 2) + (r + 1))
                        act.sem_inc(passed, 1)
                        to = stage[:, s, :, 2 * r * WD:(2 * r + 2) * WD].bitcast(FP8).rearrange("p j (w d) -> p w j d", d=WD)
                        of = b.banks[:, at:at + 2, 0:WC].rearrange("p w (j d) -> p w j d", d=WD)
                        nc.scalar.activation(to, of, ACT.Copy, scale=0.5, saturate=True).then_inc(count_read, 1)

                    act.wait_ge(counts_out[s], (i + 1) * 16)
                    act.wait_ge(sums_out[s], (i + 1) * 16)
                    act.sem_inc(passed, 1)

                    def keep_turned(q):
                        act.wait_ge(turned, SLOTS * Q + g * Q + (q + 1))
                        nc.scalar.copy(turn[:, q % 2, :], b.banks[:, T_BANK, 0:2 * P]).then_inc(turn_read, 1)

                    def relu_messages(q):
                        act.wait_ge(mixed, 2 * g * Q + 2 * (q + 1))
                        nc.scalar.activation(sums[:, s, q * QC:(q + 1) * QC, :].rearrange("p (k o) d -> p o k d", o=2),
                                             b.banks[:, M_BANK:M_BANK + 2, 0:QC // 2 * DH].rearrange("p o (k d) -> p o k d", d=DH),
                                             ACT.Relu).then_inc(mix_read, 1)

                    keep_turned(0)
                    relu_messages(0)
                    for r in range(WG // 2):
                        read_counts(r)
                        q, at = divmod(r, QW // 2)
                        if q < Q - 1 and at == 1:
                            keep_turned(q + 1)
                        if q < Q - 1 and at == 2:
                            relu_messages(q + 1)
            act.wait_ge(tailed, 3)
            nc.scalar.sqrt(b.src_norm[:, :], b.out_cap[:, :]).then_inc(rooted, 1)

        @block.tensor
        def _(pe):
            pe.sem_inc(hot_used, SLOTS * (QW // 2))

            def turn_keys(s):
                for k in range(2):
                    last = nc.tensor.matmul(b.banks[:, M_BANK, KEYS_AT + k * WG:KEYS_AT + (k + 1) * WG], raw_keys[:, s, :, k],
                                            b.ident[:, 0:WG], start=True, stop=True, skip_group_check=True)
                last.then_inc(keys_turned, 1)

            nc.tensor.matmul(b.banks[:, S_BANK, 0:P], b.zeros16[:, :], b.zeros16[:, :], start=True, stop=False, skip_group_check=True)
            for at in range(P, WC, P):
                nc.tensor.matmul(b.banks[:, S_BANK, at:min(at + P, WC)], b.zeros16[:, :], b.zeros16[:, 0:min(P, WC - at)],
                                 start=True, stop=False, skip_group_check=True)
            pe.sem_inc(keys_turned, 1)
            pe.wait_ge(keys_in[0], 16)
            turn_keys(0)
            pe.sem_inc(turned, SLOTS * Q)
            with pe.Fori(0, n_loops) as i:
                for s in range(SLOTS):
                    g = i * SLOTS + s

                    def count(r):
                        m = (r // (QW // 2)) % 2
                        pe.wait_ge(hot, SLOTS * 2 * WG + g * (2 * WG) + 4 * (r + 1))
                        pe.wait_ge(count_read, g * (WG // 2) + (r + WG - 1))
                        for k in range(2):
                            w = (2 * r + k) % QW
                            last = nc.tensor.matmul(b.banks[:, C_BANK[r % 2] + k, 0:WC], part_hot[:, m, w, :],
                                                    place_hot[:, m, w, :], start=True, stop=True)
                        last.then_inc(counted, 1)
                        for k in range(2):
                            w = (2 * r + k) % QW
                            last = nc.tensor.matmul(b.banks[:, S_BANK, 0:WC], part_hot[:, m, w, :], place_hot[:, m, w, :],
                                                    start=False, stop=False, skip_group_check=True)
                        last.then_inc(hot_used, 1)

                    pe.wait_ge(gathered[s], (i + 1) * (G * 16))
                    pe.wait_ge(attrs_in[s], (i + 1) * 16)

                    def turn_rows(q):
                        for k in range(QC // 2):
                            c = q * QC + 2 * k
                            last = nc.tensor.transpose(b.banks[:, T_BANK, k * P:(k + 1) * P],
                                                       rows[:, s, c:c + 2, :].rearrange("p c d -> p (c d)"), b.ident[:, :])
                        last.then_inc(turned, 1)

                    def mix(q):
                        pe.wait_ge(turn_read, g * Q + (q + 2))
                        pe.wait_ge(mix_read, g * Q + (q + 1))
                        if q == 0:
                            pe.wait_ge(local_made, g * 3 + 2)
                        if q == Q - 1:
                            pe.wait_ge(keys_in[1 - s], (i + (1 + s)) * 16)
                            turn_keys(1 - s)
                        for k in range(QC):
                            at = 64 * (k % 2)
                            last = nc.tensor.matmul(b.banks[:, M_BANK + k % 2, k // 2 * DH:(k // 2 + 1) * DH],
                                                    turn[at:at + DI + 1, q % 2, (k // 2) * P:(k // 2 + 1) * P],
                                                    b.w1a[at:at + DI + 1, :], start=True, stop=True)
                            if k >= QC - 2:
                                last.then_inc(mixed, 1)

                    turn_rows(0)
                    mix(0)
                    for r in range(WG // 2):
                        count(r)
                        q, at = divmod(r, QW // 2)
                        if q < Q - 1 and at == 1:
                            turn_rows(q + 1)
                        if q < Q - 1 and at == 2:
                            mix(q + 1)
            nc.tensor.matmul(b.banks[:, S_BANK, 0:P], b.zeros16[:, :], b.zeros16[:, :], start=False, stop=True,
                             skip_group_check=True).then_inc(all_summed, 1)


def sums_of_nodes(nc, b, edges, agg_tile, cont, last_row, tail):
    C = 7
    with ExitStack() as ctx:
        sem = lambda name: ctx.enter_context(nc.semaphore(f"{name}_{b.tag}"))
        sb = lambda name, shape, dt=FP32: ctx.enter_context(nc.sbuf_tensor(f"{name}_{b.tag}", shape, dt))
        fetched = [sem(f"fetched{s}") for s in range(SLOTS)]
        pointed, copied, has_made, spread_made, carried, added, passed = (
            sem("pointed"), sem("copied"), sem("has_made"), sem("carry_spread"), sem("carried"), sem("carry_added"),
            sem("fetch_passed"))
        idx, got = sb("last_idx", [P, SLOTS, C], I32), sb("last_rows", [P, SLOTS, C, DH])
        has = sb("has_edges", [P, J])
        end_hot, spread = sb("end_hot", [P, P]), sb("carry_rows", [P, J * DN])
        block = ctx.enter_context(nc.Block())
        agg = per_node(agg_tile[:, :], DH + 1)
        rows_of = b.dram.running.rearrange("p t d -> (p t) d")

        @block.gpsimd
        def _(pool):
            with pool.Fori(0, J // (C * SLOTS)) as i:
                for s in range(SLOTS):
                    g = i * SLOTS + s
                    pool.wait_ge(copied, g + 1)
                    pool.sem_inc(passed, 1)
                    nc.gpsimd.tensor_copy(idx[:, s, :], last_row[:, bass.ds(g * C, C)]).then_inc(pointed, 1)
                    pool.wait_ge(pointed, g + 1)
                    pool.sem_inc(passed, 1)
                    for c in range(C):
                        pool.indirect_dma_start(out=got[:, s, c, :], out_offset=None, in_=rows_of,
                                                in_offset=bass.IndirectOffsetOnAxis(ap=idx[:, s, c:c + 1], axis=0)) \
                            .then_inc(fetched[s], 16)

        @block.vector
        def _(dve):
            dve.sem_inc(copied, SLOTS)
            nc.vector.tensor_scalar(has[:, :], b.in_deg[:, :], 0.0, None, ALU.is_gt).then_inc(has_made, 1)
            nc.vector.tensor_scalar(end_hot[:, :], b.iota[:, :], edges.dst_part[:, T - 1:T], cont[:, :],
                                    ALU.is_equal, ALU.mult).then_inc(has_made, 1)
            dve.wait_ge(has_made, 2)
            with dve.Fori(0, J // (C * SLOTS)) as i:
                for s in range(SLOTS):
                    g = i * SLOTS + s
                    dve.wait_ge(fetched[s], (i + 1) * (C * 16))
                    at = bass.ds(g * C, C)
                    nc.vector.tensor_tensor(agg[:, at, 0:DH], got[:, s, :, :],
                                            has[:, at].unsqueeze(2).broadcast_to([P, C, DH]), ALU.mult).then_inc(copied, 1)
            dve.wait_ge(copied, SLOTS + J // C)
            for third in range(DH // DN):
                if third:
                    dve.wait_ge(carried, third)
                nc.vector.scalar_tensor_tensor(
                    out=per_node(spread[:, :]), in0=spread_over(b.iota[:, 0:J]), scalar=edges.dst_place[:, T - 1:T],
                    in1=tail[:, third * DN:(third + 1) * DN].unsqueeze(1).broadcast_to([P, J, DN]),
                    op0=ALU.is_equal, op1=ALU.mult).then_inc(spread_made, 1)
                dve.wait_ge(carried, third + 1)
                for z in range(ZB):
                    to = agg[:, z * ZJ:(z + 1) * ZJ, third * DN:(third + 1) * DN]
                    nc.vector.tensor_tensor(to, to, b.banks[:, z, 0:ZW].rearrange("p (j d) -> p j d", d=DN),
                                            ALU.add).then_inc(added, 1)
                dve.wait_ge(added, (third + 1) * ZB)

        @block.tensor
        def _(pe):
            for third in range(DH // DN):
                pe.wait_ge(spread_made, third + 1)
                if third:
                    pe.wait_ge(added, third * ZB)
                for z in range(ZB):
                    last = nc.tensor.matmul(b.banks[:, z, 0:ZW], end_hot[:, :], spread[:, z * ZW:(z + 1) * ZW],
                                            start=True, stop=True)
                last.then_inc(carried, 1)


SPLITS = 3
WF = SPLITS * DN + 1
TILES = 4
HEAD = J % TILES
BLOCKS = J // TILES
KC = 14
CHUNKS = J // KC
assert HEAD == 2 and BLOCKS % 2 == 0 and J % KC == 0


def propagate(nc, b, exact):
    with ExitStack() as ctx:
        sem = lambda name: ctx.enter_context(nc.semaphore(f"{name}_{b.tag}"))
        sb = lambda name, shape, dt=FP32: ctx.enter_context(nc.sbuf_tensor(f"{name}_{b.tag}", shape, dt))
        chunk_in = [sem(f"chunk_in{k}") for k in range(CHUNKS)]
        head_in, prepared, started, swept, drained, folded, fresh, passed, chain, stacked = (
            sem("head_in"), sem("prop_prepared"), sem("prop_started"), sem("chunk_used"), sem("block_drained"),
            sem("block_folded"), sem("parts_fresh"), sem("sweep_passed"), sem("fresh_chain"), sem("stack_made"))
        folds_read = sem("folds_read")
        parts = sb("feature_parts", [P, 2, J, WF], BF16)
        head = sb("head_counts", [P, HEAD, J, P], U8)
        ring = sb("count_ring", [P, CHUNKS, TILES, KC, P], U8)
        drain = sb("drained", [WF, 2, TILES * P])
        stack = sb("stacked_identities", [WF, DN + 1])
        gain = sb("target_gain", [P, J])
        expect = sb("expected_in_deg", [P, J])
        scaled, rest = sb("scaled", [P, TILES * DN]), sb("rest", [P, TILES * DN])
        block = ctx.enter_context(nc.Block())
        SWEEP, FOLD = (0, 1), (2, 3)
        steps2 = STEPS // 2
        CHAIN = 3 + 2 * SPLITS

        @block.sync
        def _(sp):
            sp.dma_start(head[:, :, :, :].rearrange("p a j c -> p a (j c)"),
                         b.dram.counts[SLOTS:SLOTS + HEAD].rearrange("a p j c -> p a (j c)")).then_inc(head_in, 16)
            with sp.Fori(0, STEPS) as t:
                with sp.Fori(0, BLOCKS) as m:
                    for k in range(CHUNKS):
                        sp.wait_ge(swept, t * (BLOCKS * CHUNKS) + m * CHUNKS + (k + 1))
                        sp.sem_inc(passed, 1)
                        sp.dma_start(ring[:, k, :, :, :].rearrange("p a j c -> p a (j c)"),
                                     b.dram.counts[bass.ds(m * TILES + (SLOTS + HEAD), TILES), :, k * KC:(k + 1) * KC, :]
                                     .rearrange("a p j c -> p a (j c)")).then_inc(chunk_in[k], 16)
            for k in range(CHUNKS):
                sp.wait_ge(chunk_in[k], STEPS * BLOCKS * 16)

        @block.gpsimd
        def _(pool):
            nc.gpsimd.memset(stack[:, :], 0.0).then_inc(stacked, 1)
            for k in range(SPLITS):
                pool.wait_ge(stacked, k + 1)
                nc.gpsimd.affine_select(out=stack[:, 0:DN], in_=stack[:, 0:DN], compare_op=ALU.not_equal, fill=2.0,
                                        base=-k * DN, pattern=[[-1, DN]], channel_multiplier=1).then_inc(stacked, 1)
            nc.gpsimd.affine_select(out=stack[:, DN:DN + 1], in_=stack[:, DN:DN + 1], compare_op=ALU.not_equal, fill=2.0,
                                    base=-SPLITS * DN, pattern=[[0, 1]], channel_multiplier=1).then_inc(stacked, 1)
            pool.wait_ge(prepared, 1)
            nc.gpsimd.affine_select(out=expect[:, J - 1:J], in_=expect[:, J - 1:J], compare_op=ALU.is_ge, fill=0.0,
                                    base=NL - 1, pattern=[[0, 1]], channel_multiplier=-1).then_inc(stacked, 1)

        @block.scalar
        def _(act):
            def drain_block(n, parity, cols):
                nc.scalar.copy(drain[:, parity, 0:cols], b.banks[0:WF, SWEEP[parity], 0:cols]).then_inc(drained, 1)

            act.sem_inc(drained, 1)
            act.wait_ge(started, 1)
            drain_block(0, 0, HEAD * P)
            with act.Fori(0, STEPS) as t:
                with act.Fori(0, BLOCKS // 2) as mm:
                    for odd in (1, 0):
                        act.wait_ge(swept, (t * BLOCKS + mm * 2) * CHUNKS + (3 - odd) * CHUNKS)
                        act.wait_ge(folded, t * (BLOCKS + 1) + mm * 2 + (2 - odd))
                        drain_block(None, odd, TILES * P)
                act.wait_ge(started, t + 2)
                act.wait_ge(folded, (t + 1) * (BLOCKS + 1) + 1)
                drain_block(None, 0, HEAD * P)

        @block.vector
        def _(dve):
            nc.vector.tensor_copy(expect[:, :], b.in_deg[:, :]).then_inc(prepared, 1)
            nc.vector.memset(drain[:, :, :], 0.0).then_inc(prepared, 1)
            nc.vector.memset(parts[:, :, :, SPLITS * DN:WF], 1.0).then_inc(prepared, 1)
            nc.vector.tensor_scalar(gain[:, :], b.dst_norm[:, :], 1.0 - ALPHA, None, ALU.mult).then_inc(prepared, 1)
            nc.vector.tensor_tensor(per_node(b.f[:, :]), per_node(b.h[:, :]), spread_over(b.src_norm[:, :]), ALU.mult).then_inc(prepared, 1)
            for k in range(SPLITS):
                dve.wait_ge(prepared, 5 + 2 * k)
                part = parts[:, 0, :, k * DN:(k + 1) * DN]
                nc.vector.tensor_copy(part, per_node(b.f[:, :])).then_inc(prepared, 1)
                if k < SPLITS - 1:
                    dve.wait_ge(prepared, 6 + 2 * k)
                    nc.vector.tensor_tensor(per_node(b.f[:, :]), per_node(b.f[:, :]), part, ALU.subtract).then_inc(prepared, 1)
            dve.wait_ge(stacked, SPLITS + 3)
            dve.sem_inc(folds_read, 1)

            def new_features(n, side, parity, at, tiles):
                dve.wait_ge(folded, n + 2)
                got = per_node(b.banks[:, FOLD[parity], 0:tiles * (DN + 1)], DN + 1)
                where = at if isinstance(at, slice) else bass.ds(at, tiles)
                t1, t2 = per_node(scaled[:, 0:tiles * DN]), per_node(rest[:, 0:tiles * DN])
                f, h = per_node(b.f[:, :])[:, where, :], per_node(b.h[:, :])[:, where, :]
                spread = lambda column: column[:, where].unsqueeze(2).broadcast_to([P, tiles, DN])
                steps = [0]

                def step(ins_):
                    steps[0] += 1
                    ins_.then_inc(chain, 1)
                    dve.wait_ge(chain, n * CHAIN + steps[0])

                step(nc.vector.tensor_tensor(exact[:, where].unsqueeze(2), got[:, :, DN:DN + 1], expect[:, where].unsqueeze(2),
                                             ALU.is_equal))
                step(nc.vector.tensor_tensor(t1, got[:, :, 0:DN], spread(gain), ALU.mult))
                dve.sem_inc(folds_read, 1)
                step(nc.vector.scalar_tensor_tensor(out=f, in0=h, scalar=ALPHA, in1=t1, op0=ALU.mult, op1=ALU.add))
                step(nc.vector.tensor_tensor(t1, f, spread(b.src_norm), ALU.mult))
                for k in range(SPLITS):
                    part = parts[:, 1 - side, where, k * DN:(k + 1) * DN]
                    of, left = (t1, t2) if k % 2 == 0 else (t2, t1)
                    step(nc.vector.tensor_copy(part, of))
                    if k < SPLITS - 1:
                        step(nc.vector.tensor_tensor(left, of, part, ALU.subtract))
                assert steps[0] == CHAIN
                dve.sem_inc(fresh, 1)

            with dve.Fori(0, steps2) as tt:
                for side in range(2):
                    n = (tt * 2 + side) * (BLOCKS + 1)
                    new_features(n, side, 0, slice(0, HEAD), HEAD)
                    with dve.Fori(0, BLOCKS // 2) as mm:
                        for odd in (1, 0):
                            new_features(n + (mm * 2 + (2 - odd)), side, odd, mm * (2 * TILES) + (HEAD + (1 - odd) * TILES), TILES)

        @block.tensor
        def _(pe):
            def sweep_tile(bank, cols, side, j, matrix):
                return nc.tensor.matmul(b.banks[0:WF, bank, 0:cols], parts[:, side, j, :], matrix.bitcast(FP8),
                                        start=(j == 0), stop=(j == J - 1))

            def fold(parity, tiles):
                for a in range(tiles):
                    last = nc.tensor.matmul(b.banks[:, FOLD[parity], a * (DN + 1):(a + 1) * (DN + 1)],
                                            drain[:, parity, a * P:(a + 1) * P], stack[:, :], start=True, stop=True)
                last.then_inc(folded, 1)

            def head_block(side, known, before):
                for j in range(J):
                    if j in before:
                        before[j]()
                    if (j - HEAD) % TILES == 0 or j == 0:
                        known(0 if j == 0 else (j - HEAD) // TILES + 1)
                    last = sweep_tile(SWEEP[0], HEAD * P, side, j, head[:, :, j, :])
                return last

            pe.wait_ge(stacked, SPLITS + 3)
            pe.wait_ge(head_in, 16)
            pe.sem_inc(swept, CHUNKS)
            pe.wait_ge(prepared, 4 + 2 * SPLITS)
            pe.sem_inc(folded, 1)
            head_block(0, lambda n: None, {}).then_inc(started, 1)
            with pe.Fori(0, steps2) as tt:
                for side in range(2):
                    t = tt * 2 + side
                    with pe.Fori(0, BLOCKS // 2) as mm:
                        for odd in (1, 0):
                            u = 1 if odd else 0
                            n = t * (BLOCKS + 1) + mm * 2 + (1 - u)
                            for k in range(CHUNKS):
                                pe.wait_ge(chunk_in[k], (t * BLOCKS + mm * 2 + (1 - u) + 1) * 16)
                                if k == 0:
                                    pe.wait_ge(drained, n + 1)
                                pe.sem_inc(passed, 1)
                                for j in range(k * KC, (k + 1) * KC):
                                    last = sweep_tile(SWEEP[u], TILES * P, side, j, ring[:, k, :, j - k * KC, :])
                                last.then_inc(swept, 1)
                                if k == 0:
                                    pe.wait_ge(drained, n + 2)
                                    pe.wait_ge(folds_read, n + 1)
                                    pe.sem_inc(passed, 1)
                                    fold(1 - u, TILES)
                    last_n = t * (BLOCKS + 1) + BLOCKS

                    def known(n_block, side=side, last_n=last_n):
                        pe.wait_ge(fresh, last_n - BLOCKS + n_block + 1)
                        pe.sem_inc(passed, 1)

                    def last_fold(last_n=last_n):
                        pe.wait_ge(drained, last_n + 2)
                        pe.wait_ge(folds_read, last_n + 1)
                        pe.sem_inc(passed, 1)
                        fold(0, TILES)

                    pe.wait_ge(drained, last_n + 2)
                    pe.sem_inc(passed, 1)
                    head_block(1 - side, known, {KC: last_fold}).then_inc(started, 1)


def needs_general(nc, b, exact, unsorted, flag):
    with nc.semaphore("flag_made") as made, nc.semaphore("flag_turned") as turned, \
            nc.sbuf_tensor("bad_rows", [P, 2], FP32) as bad, nc.Block() as block:
        @block.vector
        def _(dve):
            nc.vector.tensor_reduce(bad[:, 0:1], exact[:, :], AX.X, ALU.min).then_inc(made, 1)
            dve.wait_ge(made, 1)
            nc.vector.tensor_scalar(bad[:, 0:1], bad[:, 0:1], -1.0, 1.0, ALU.mult, ALU.add).then_inc(made, 1)
            dve.wait_ge(made, 2)
            nc.vector.tensor_tensor(bad[:, 0:1], bad[:, 0:1], unsorted[:, :], ALU.max).then_inc(made, 1)
            dve.wait_ge(turned, 1)
            nc.vector.tensor_reduce(bad[0:1, 1:2], b.banks[0:1, 0, 0:P], AX.X, ALU.max).then_inc(made, 1)
            dve.wait_ge(made, 4)
            nc.vector.tensor_copy(flag[:, :], bad[0:1, 1:2]).then_inc(made, 1)
            dve.wait_ge(made, 5)

        @block.tensor
        def _(pe):
            pe.wait_ge(made, 3)
            nc.tensor.matmul(b.banks[0:1, 0, 0:P], bad[:, 0:1], b.ident[:, :], start=True, stop=True).then_inc(turned, 1)


def general_way(nc, ins, out, dram):
    with ExitStack() as ctx:
        b = Kept(nc, ctx, dram, "any")
        edges = Edges(nc, ctx, "any")
        agg_tile = ctx.enter_context(nc.sbuf_tensor("agg_nodes_any", [P, J * (DH + 1)], FP32))
        setup(nc, b, edges, ins)
        degrees(nc, b, edges, 2)
        general_layers(nc, b, edges, agg_tile)
        store_result(nc, b, out)




def fast_way(nc, ins, out, dram, flag):
    with ExitStack() as ctx:
        b = Kept(nc, ctx, dram, "fast")
        exact = ctx.enter_context(nc.sbuf_tensor("counts_exact", [P, J], FP32))
        unsorted = ctx.enter_context(nc.sbuf_tensor("unsorted", [P, 1], FP32))
        with ExitStack() as edge_ctx:
            sb = lambda name, shape: edge_ctx.enter_context(nc.sbuf_tensor(name, shape, FP32))
            edges = Edges(nc, edge_ctx, "fast")
            same, cont, last_row, tail = sb("same_target", [P, T]), sb("run_goes_on", [P, 1]), sb("last_row", [P, J]), sb("last_sums", [P, DH])
            window_row = edge_ctx.enter_context(nc.sbuf_tensor("window_row", [WG, J + SLOTS], I32))
            setup(nc, b, edges, ins)
            degrees(nc, b, edges, 1)
            layer_norm_relu(nc, b, "in")
            store_table(nc, b, b.h)
            prepare_sorted(nc, b, edges, ins, (same, cont, last_row, window_row, unsorted))
            messages_and_counts(nc, b, edges, same, window_row, tail)
            agg_tile = sb("agg_nodes_fast", [P, J * (DH + 1)])
            sums_of_nodes(nc, b, edges, agg_tile, cont, last_row, tail)
            node_mlp(nc, b, agg_tile)
        layer_norm_relu(nc, b, "mid")
        propagate(nc, b, exact)
        needs_general(nc, b, exact, unsorted, flag)
        store_result(nc, b, out)


def program(nc, ins, out):
    dram = Dram(nc)
    with nc.sbuf_tensor("general_flag", [1, 1], I32) as flag:
        fast_way(nc, ins, out, dram, flag)
        bad = nc.values_load(flag[0:1, 0:1], min_val=0, max_val=1)
        with nc.If(bad > 0):
            nc.all_engine_barrier()
            general_way(nc, ins, out, dram)


INPUTS = ["x", "src", "dst", "edge_attr_16", "L0_gnn_w1a", "L0_gnn_b1a", "L0_gnn_w1b", "L0_gnn_b1b",
          "L0_gnn_w2a", "L0_gnn_b2a", "L0_gnn_w2b", "L0_gnn_b2b"]


def kernel(**inputs):
    import numpy as np
    import concourse.bacc as bacc
    from concourse.bass_utils import run_bass_kernel_spmd

    nc = bacc.Bacc("TRN2", target_bir_lowering=False, num_devices=1)
    arrays, ins = {}, {}
    for name in INPUTS:
        a = np.ascontiguousarray(inputs[name])
        arrays[f"in_{name}"] = a
        ins[name] = nc.dram_tensor(f"in_{name}", a.shape, mybir.dt.from_np(a.dtype), kind="ExternalInput").ap()
    out = nc.dram_tensor("out_nodes", (N, DN), FP32, kind="ExternalOutput").ap()
    program(nc, ins, out)
    result = run_bass_kernel_spmd(nc, [arrays], core_ids=[0])
    return result.results[0]["out_nodes"]
```

```python
from contextlib import ExitStack

import concourse.bass as bass
from concourse import mybir

FP32 = mybir.dt.float32
BF16 = mybir.dt.bfloat16
FP16 = mybir.dt.float16
FP8 = mybir.dt.float8e3
U8 = mybir.dt.uint8
I32 = mybir.dt.int32
ALU = mybir.AluOpType
ACT = mybir.ActivationFunctionType
AX = mybir.AxisListType

P = 128
N = 12500
E = 200000
DN = 32
DE = 16
DI = DN + DE
DH = 2 * DI
STEPS = 10
ALPHA = 0.1
EPS = 1e-5

J = -(-N // P)
NP = P * J
NL = N - P * (J - 1)
G = 16
T = 1568
EP = P * T
EL = E - (P - 1) * T
PAD_NODE = NP - 1
BITS = 7
ROUND = 12582912.0
ZB = 7
ZJ = J // ZB
ZW = ZJ * DN
SLOTS = 2
WD = 4
WBITS = 2
WINDOWS = NP // WD
WG = P // WD
WC = WD * J
TD = T + SLOTS * G
assert P == 1 << BITS and WD == 1 << WBITS and T == J * G and WC <= 512 and T % G == 0 and NP > N and EP >= E and J % ZB == 0 and ZW <= 512


def per_node(tile, d=DN):
    return tile.rearrange("p (j d) -> p j d", d=d)


def spread_over(column, d=DN):
    return column.unsqueeze(2).broadcast_to([P, J, d])


def row_vector(v):
    return v.rearrange("(a d) -> a d", a=1)


class Dram:

    def __init__(self, nc):
        dram = lambda name, shape, dt=FP32: nc.dram_tensor(name, shape, dt).ap()
        self.table = dram("row_table", (NP, DN))
        self.attrs = dram("attrs_padded", (EP, DE))
        self.keys = dram("edge_keys", (EP, 2))
        self.running = dram("running_sums", (P, TD, DH))
        self.counts = dram("edge_counts", (J + SLOTS, P, J, P), U8)


class Kept:

    def __init__(self, nc, ctx, dram, tag):
        self.tag, self.dram = tag, dram
        sb = lambda name, shape, dt=FP32: ctx.enter_context(nc.sbuf_tensor(f"{name}_{tag}", shape, dt))
        self.banks = ctx.enter_context(nc.psum_tensor(f"banks_{tag}", [P, 8, 512], FP32))
        self.attrs_copied = ctx.enter_context(nc.semaphore(f"attrs_copied_{tag}"))
        self.x = sb("x_nodes", [P, J * DN])
        self.h = sb("h_nodes", [P, J * DN])
        self.f = sb("f_nodes", [P, J * DN])
        self.in_deg = sb("in_deg", [P, J])
        self.in_cap = sb("in_cap", [P, J])
        self.out_cap = sb("out_cap", [P, J])
        self.in_inv = sb("in_inv", [P, J])
        self.src_norm = sb("src_norm", [P, J])
        self.dst_norm = sb("dst_norm", [P, J])
        self.iota = sb("iota_row", [P, P])
        self.iota16 = sb("iota_row16", [P, P], BF16)
        self.ident = sb("identity", [P, P])
        self.zeros = sb("zeros", [P, 512])
        self.zeros16 = sb("zeros16", [P, P], BF16)
        self.w1a = sb("w1a_b1a", [P, DH])
        self.w1b = sb("w1b_b1b", [DH + 1, DH])
        self.w2a_h = sb("w2a_h", [DN, DI])
        self.w2a_agg = sb("w2a_agg", [DH, DI])
        self.b2a = sb("b2a_col", [DI, 1])
        self.w2b = sb("w2b_b2b", [P, DN])


class Edges:

    def __init__(self, nc, ctx, tag):
        sb = lambda name, shape, dt=FP32: ctx.enter_context(nc.sbuf_tensor(f"{name}_{tag}", shape, dt))
        self.src = sb("src_ends", [P, T + G], I32)
        self.dst = sb("dst_ends", [P, T], I32)
        self.src_part = sb("src_part", [P, T])
        self.src_place = sb("src_place", [P, T])
        self.dst_part = sb("dst_part", [P, T])
        self.dst_place = sb("dst_place", [P, T])


def setup(nc, b, edges, ins):
    with ExitStack() as ctx:
        sem = lambda name: ctx.enter_context(nc.semaphore(f"{name}_{b.tag}"))
        sb = lambda name, shape, dt=FP32: ctx.enter_context(nc.sbuf_tensor(f"{name}_{b.tag}", shape, dt))
        filled, loaded, iotas, ident_made, split = sem("filled"), sem("loaded"), sem("iotas"), sem("ident_made"), sem("split")
        zero_rows = sb("zero_rows", [P, (EP - E) * DE // 64])
        iota_i = sb("iota_int", [P, P], I32)
        low, high = sb("end_low", [P, T], I32), sb("end_high", [P, T], I32)
        block = ctx.enter_context(nc.Block())
        LOADS = 17

        @block.sync
        def _(sp):
            sp.wait_ge(filled, 8)
            x = ins["x"]
            sp.dma_start(per_node(b.x[:, :])[:, 0:J - 1, :], x[0:P * (J - 1), :].rearrange("(j p) d -> p j d", p=P)).then_inc(loaded, 16)
            sp.dma_start(b.x[0:NL, (J - 1) * DN:J * DN], x[P * (J - 1):N, :]).then_inc(loaded, 16)
            for tile, ends in ((edges.src[:, 0:T], ins["src"]), (edges.dst, ins["dst"])):
                sp.dma_start(tile[0:P - 1, :], ends[0:(P - 1) * T].rearrange("(p t) -> p t", t=T)).then_inc(loaded, 16)
                sp.dma_start(tile[P - 1:P, 0:EL], ends[(P - 1) * T:E].rearrange("(p t) -> p t", p=1)).then_inc(loaded, 16)
            for at in (0, 64):
                sp.dma_start(b.w1a[at:at + DI, :], ins["L0_gnn_w1a"]).then_inc(loaded, 16)
                sp.dma_start(b.w1a[at + DI:at + DI + 1, :], row_vector(ins["L0_gnn_b1a"])).then_inc(loaded, 16)
            sp.dma_start(b.w1b[0:DH, :], ins["L0_gnn_w1b"]).then_inc(loaded, 16)
            sp.dma_start(b.w1b[DH:DH + 1, :], row_vector(ins["L0_gnn_b1b"])).then_inc(loaded, 16)
            sp.dma_start(b.w2a_h[:, :], ins["L0_gnn_w2a"][0:DN, :]).then_inc(loaded, 16)
            sp.dma_start(b.w2a_agg[:, :], ins["L0_gnn_w2a"][DN:DN + DH, :]).then_inc(loaded, 16)
            sp.dma_start(b.b2a[:, :], ins["L0_gnn_b2a"].rearrange("(d a) -> d a", a=1)).then_inc(loaded, 16)
            sp.dma_start(b.w2b[0:DI, :], ins["L0_gnn_w2b"]).then_inc(loaded, 16)
            sp.dma_start(b.w2b[64:65, :], row_vector(ins["L0_gnn_b2b"])).then_inc(loaded, 16)
            sp.wait_ge(loaded, LOADS * 16)
            sp.dma_start(b.dram.attrs[E:EP, :].rearrange("(p r) d -> p (r d)", p=64), zero_rows[0:64, :]).then_inc(b.attrs_copied, 16)
            sp.wait_ge(b.attrs_copied, 16)
            cut = lambda t: t.rearrange("(a r) d -> a (r d)", a=320)
            sp.dma_start(cut(b.dram.attrs[0:E, :]), cut(ins["edge_attr_16"])).then_inc(b.attrs_copied, 16)

        @block.gpsimd
        def _(pool):
            nc.gpsimd.iota(iota_i[:, :], pattern=[[1, P]], base=0, channel_multiplier=0).then_inc(iotas, 1)
            nc.gpsimd.memset(b.ident[:, :], 0.0).then_inc(ident_made, 1)
            pool.wait_ge(ident_made, 1)
            nc.gpsimd.affine_select(out=b.ident[:, :], in_=b.ident[:, :], compare_op=ALU.not_equal, fill=1.0,
                                    base=0, pattern=[[-1, P]], channel_multiplier=1).then_inc(ident_made, 1)
            pool.wait_ge(ident_made, 2)

        @block.vector
        def _(dve):
            for tile, value in ((zero_rows, 0.0), (b.x, 0.0), (edges.src, PAD_NODE), (edges.dst, PAD_NODE), (b.zeros, 0.0),
                                (b.w2b, 0.0), (b.w1a, 0.0), (b.zeros16, 0.0)):
                nc.vector.memset(tile[:, :], value).then_inc(filled, 1)
            dve.wait_ge(iotas, 1)
            nc.vector.tensor_copy(b.iota[:, :], iota_i[:, :]).then_inc(filled, 1)
            nc.vector.tensor_copy(b.iota16[:, :], iota_i[:, :]).then_inc(filled, 1)
            dve.wait_ge(filled, 10)
            dve.wait_ge(loaded, LOADS * 16)
            n = 0
            for ends, part, place in ((edges.src[:, 0:T], edges.src_part, edges.src_place), (edges.dst, edges.dst_part, edges.dst_place)):
                nc.vector.tensor_scalar(low[:, :], ends[:, :], P - 1, None, ALU.bitwise_and).then_inc(split, 1)
                nc.vector.tensor_scalar(high[:, :], ends[:, :], BITS, None, ALU.logical_shift_right).then_inc(split, 1)
                dve.wait_ge(split, n + 2)
                nc.vector.tensor_copy(part[:, :], low[:, :]).then_inc(split, 1)
                nc.vector.tensor_copy(place[:, :], high[:, :]).then_inc(split, 1)
                n += 4
                dve.wait_ge(split, n)
            nc.vector.scalar_tensor_tensor(out=edges.src[:, 0:T], in0=edges.src_part[:, :], scalar=float(J), in1=edges.src_place[:, :],
                                           op0=ALU.mult, op1=ALU.add).then_inc(split, 1)
            dve.wait_ge(split, n + 1)


def inverse_root(nc, dve, root, value, term, done, n):
    nc.vector.reciprocal(root, root).then_inc(done, 1)
    dve.wait_ge(done, n + 1)
    nc.vector.tensor_tensor(term, root, root, ALU.mult).then_inc(done, 1)
    dve.wait_ge(done, n + 2)
    nc.vector.tensor_tensor(term, term, value, ALU.mult).then_inc(done, 1)
    dve.wait_ge(done, n + 3)
    nc.vector.tensor_scalar(term, term, -0.5, 1.5, ALU.mult, ALU.add).then_inc(done, 1)
    dve.wait_ge(done, n + 4)
    nc.vector.tensor_tensor(root, root, term, ALU.mult).then_inc(done, 1)
    dve.wait_ge(done, n + 5)


def layer_norm_relu(nc, b, tag):
    tag = f"{tag}_{b.tag}"
    with ExitStack() as ctx:
        done = ctx.enter_context(nc.semaphore(f"ln_done_{tag}"))
        rooted = ctx.enter_context(nc.semaphore(f"ln_rooted_{tag}"))
        mean = ctx.enter_context(nc.sbuf_tensor(f"ln_mean_{tag}", [P, J], FP32))
        var = ctx.enter_context(nc.sbuf_tensor(f"ln_var_{tag}", [P, J], FP32))
        term = ctx.enter_context(nc.sbuf_tensor(f"ln_newton_{tag}", [P, J], FP32))
        square = ctx.enter_context(nc.sbuf_tensor(f"ln_square_{tag}", [P, J * DN], FP32))
        block = ctx.enter_context(nc.Block())

        @block.vector
        def _(dve):
            h = per_node(b.h[:, :])
            nc.vector.tensor_reduce(mean[:, :], per_node(b.x[:, :]), AX.X, ALU.add).then_inc(done, 1)
            dve.wait_ge(done, 1)
            nc.vector.tensor_scalar(mean[:, :], mean[:, :], 1.0 / DN, None, ALU.mult).then_inc(done, 1)
            dve.wait_ge(done, 2)
            nc.vector.tensor_tensor(h, per_node(b.x[:, :]), spread_over(mean[:, :]), ALU.subtract).then_inc(done, 1)
            dve.wait_ge(done, 3)
            nc.vector.tensor_tensor(square[:, :], b.h[:, :], b.h[:, :], ALU.mult).then_inc(done, 1)
            dve.wait_ge(done, 4)
            nc.vector.tensor_reduce(var[:, :], per_node(square[:, :]), AX.X, ALU.add).then_inc(done, 1)
            dve.wait_ge(done, 5)
            nc.vector.tensor_scalar(var[:, :], var[:, :], 1.0 / DN, EPS, ALU.mult, ALU.add).then_inc(done, 1)
            dve.wait_ge(done, 6)
            dve.wait_ge(rooted, 1)
            inverse_root(nc, dve, mean[:, :], var[:, :], term[:, :], done, 6)
            nc.vector.tensor_tensor(h, h, spread_over(mean[:, :]), ALU.mult).then_inc(done, 1)
            dve.wait_ge(done, 12)
            nc.vector.tensor_scalar(b.h[:, :], b.h[:, :], 0.0, None, ALU.max).then_inc(done, 1)
            dve.wait_ge(done, 13)

        @block.scalar
        def _(act):
            act.wait_ge(done, 6)
            nc.scalar.sqrt(mean[:, :], var[:, :]).then_inc(rooted, 1)


def store_table(nc, b, tile):
    with nc.semaphore(f"table_stored_{b.tag}") as stored, nc.Block() as block:
        @block.sync
        def _(sp):
            sp.dma_start(b.dram.table.rearrange("(p j) d -> p (j d)", j=J), tile[:, :]).then_inc(stored, 16)
            sp.wait_ge(stored, 16)


def degrees(nc, b, edges, sides):
    with ExitStack() as ctx:
        sem = lambda name: ctx.enter_context(nc.semaphore(f"{name}_{b.tag}"))
        sb = lambda name, shape, dt=FP32: ctx.enter_context(nc.sbuf_tensor(f"{name}_{b.tag}", shape, dt))
        hot, used, summed, normed, rooted, packed = (sem("hot_made"), sem("hot_used"), sem("deg_summed"), sem("deg_normed"),
                                                     sem("deg_rooted"), sem("ends_packed"))
        term = sb("deg_newton", [P, J])
        iota_wide = sb("iota_by_columns", [P, P, G], BF16)
        part16, place16 = sb("part16", [P, sides, T], BF16), sb("place16", [P, sides, T], BF16)
        part_hot, place_hot = sb("part_hot", [P, 2, sides, P, G], BF16), sb("place_hot", [P, 2, sides, J, G], BF16)
        count = b.banks
        block = ctx.enter_context(nc.Block())
        ends = ((edges.dst_part, edges.dst_place), (edges.src_part, edges.src_place))[0:sides]
        norms = ((b.in_cap, b.dst_norm), (b.out_cap, b.src_norm))[0:sides]

        @block.vector
        def _(dve):
            nc.vector.tensor_copy(iota_wide[:, :, :], b.iota16[:, :].unsqueeze(2).broadcast_to([P, P, G])).then_inc(packed, 1)
            for k, (part, place) in enumerate(ends):
                nc.vector.tensor_copy(part16[:, k, :], part[:, :]).then_inc(packed, 1)
                nc.vector.tensor_copy(place16[:, k, :], place[:, :]).then_inc(packed, 1)
            dve.wait_ge(packed, 1 + 2 * sides)
            with dve.Fori(0, T // (2 * G)) as i:
                for s in range(2):
                    g = i * 2 + s
                    dve.wait_ge(used, g + 1)
                    for k in range(sides):
                        for one_hot, of, width in ((part_hot, part16, P), (place_hot, place16, J)):
                            nc.vector.tensor_tensor(one_hot[:, s, k, :, :], iota_wide[:, 0:width, :],
                                                    of[:, k, bass.ds(g * G, G)].unsqueeze(1).broadcast_to([P, width, G]),
                                                    ALU.is_equal).then_inc(hot, 1)
            dve.wait_ge(summed, 1)
            nc.vector.tensor_copy(b.in_deg[:, :], count[:, 0, 0:J]).then_inc(normed, 1)
            for k, (cap, _) in enumerate(norms):
                nc.vector.tensor_scalar(cap[:, :], count[:, k, 0:J], 1.0, None, ALU.max).then_inc(normed, 1)
            dve.wait_ge(normed, 1 + sides)
            nc.vector.reciprocal(b.in_inv[:, :], b.in_cap[:, :]).then_inc(normed, 1)
            dve.wait_ge(rooted, sides)
            for k, (cap, norm) in enumerate(norms):
                inverse_root(nc, dve, norm[:, :], cap[:, :], term[:, :], normed, 2 + sides + 5 * k)

        @block.scalar
        def _(act):
            act.wait_ge(normed, 1 + sides)
            for cap, norm in norms:
                nc.scalar.sqrt(norm[:, :], cap[:, :]).then_inc(rooted, 1)

        @block.tensor
        def _(pe):
            zero = lambda k, **flags: nc.tensor.matmul(count[:, k, 0:J], b.zeros16[:, 0:P], b.zeros16[:, 0:J],
                                                       skip_group_check=True, **flags)
            for k in range(sides):
                last = zero(k, start=True, stop=False)
            last.then_inc(used, 2)
            with pe.Fori(0, T // (2 * G)) as i:
                for s in range(2):
                    pe.wait_ge(hot, (i * 2 + s + 1) * (2 * sides))
                    for k in range(sides):
                        for c in range(G):
                            last = nc.tensor.matmul(count[:, k, 0:J], part_hot[:, s, k, :, c], place_hot[:, s, k, :, c],
                                                    start=False, stop=False, skip_group_check=True)
                    last.then_inc(used, 1)
            for k in range(sides):
                last = zero(k, start=False, stop=True)
            last.then_inc(summed, 1)


def edge_sums(nc, b, edges, agg_tile, messages, s, tiles, third=None):
    idx, rows, turn, msg, part_hot, spread, w_third = tiles
    sums, work = b.banks, b.banks[:, ZB, :]
    sums_to = per_node(agg_tile[:, :], DH + 1) if messages else per_node(b.f[:, :])
    with nc.Block() as block:
        @block.gpsimd
        def _(pool):
            with pool.Fori(0, T // G) as i:
                pool.wait_ge(s["idx_ready"], i + 1)
                pool.sem_inc(s["taken"], 1)
                for c in range(G):
                    pool.indirect_dma_start(out=rows[:, c, 0:DN], out_offset=None, in_=b.dram.table,
                                            in_offset=bass.IndirectOffsetOnAxis(ap=idx[:, c:c + 1], axis=0)) \
                        .then_inc(s["gathered"], 16)
                pool.wait_ge(s["gathered"], (i + 1) * (G * 16))
                pool.sem_inc(s["rows_ready"], 1)
            pool.inc_swdge_sem([s["gathered"]], [T * 16], mode="sub")

        if messages:
            @block.sync
            def _(sp):
                attrs = b.dram.attrs.rearrange("(p t) d -> p t d", t=T)
                sp.wait_ge(b.attrs_copied, 32)
                with sp.Fori(0, T // G) as i:
                    sp.wait_ge(s["idx_ready"], i + 1)
                    sp.sem_inc(s["taken"], 1)
                    sp.dma_start(rows[:, :, DN:DI], attrs[:, bass.ds(i * G, G), :]).then_inc(s["attrs"], 16)
                    sp.wait_ge(s["attrs"], (i + 1) * 16)
                    sp.sem_inc(s["attrs_ready"], 1)

            @block.scalar
            def _(act):
                with act.Fori(0, T // G) as i:
                    for c in range(0, G, 2):
                        act.wait_ge(s["turned"], i * (G // 2) + c // 2 + 1)
                        nc.scalar.copy(turn[:, :], work[:, 0:P]).then_inc(s["turn_read"], 1)

        @block.vector
        def _(dve):
            nc.vector.memset(rows[:, :, DN:64], 0.0).then_inc(s["ones"], 1)
            dve.wait_ge(s["ones"], 1)
            nc.vector.memset(rows[:, :, DI:DI + 1], 1.0).then_inc(s["ones"], 1)
            if messages:
                nc.vector.tensor_copy(w_third[:, :], b.w1a[:, bass.ds(third * DN, DN)]).then_inc(s["ones"], 1)
            dve.wait_ge(s["ones"], 3 if messages else 2)
            with dve.Fori(0, T // G) as i:
                nc.vector.tensor_copy(idx[:, :], edges.src[:, bass.ds(i * G, G)]).then_inc(s["idx_ready"], 1)
                dve.wait_ge(s["rows_ready"], i + 1)
                for c in range(G):
                    n, r = i * G + c, c % 2
                    row = rows[:, c, 0:DN]
                    if messages:
                        dve.wait_ge(s["mixed"], n + 1)
                        nc.vector.tensor_scalar(msg[:, r, :], work[:, 256:256 + DN], 0.0, None, ALU.max).then_inc(s["mix_read"], 1)
                        dve.wait_ge(s["mix_read"], n + 2)
                        row = msg[:, r, :]
                    dve.wait_ge(s["used"], n + 1)
                    nc.vector.tensor_scalar(part_hot[:, r, :], b.iota[:, :], edges.dst_part[:, bass.ds(n, 1)], None,
                                            ALU.is_equal).then_inc(s["hot"], 1)
                    nc.vector.scalar_tensor_tensor(
                        out=per_node(spread[:, r, :]), in0=spread_over(b.iota[:, 0:J]), scalar=edges.dst_place[:, bass.ds(n, 1)],
                        in1=row.unsqueeze(1).broadcast_to([P, J, DN]), op0=ALU.is_equal, op1=ALU.mult).then_inc(s["hot"], 1)
                dve.wait_ge(s["hot"], (i + 1) * (2 * G))
            dve.wait_ge(s["summed"], 1)
            for z in range(ZB):
                to = (sums_to[:, z * ZJ:(z + 1) * ZJ, bass.ds(third * DN, DN)] if messages
                      else sums_to[:, z * ZJ:(z + 1) * ZJ, :])
                nc.vector.tensor_copy(to, sums[:, z, 0:ZW].rearrange("p (j d) -> p j d", d=DN)).then_inc(s["copied"], 1)
            dve.wait_ge(s["copied"], ZB)

        @block.tensor
        def _(pe):
            def zero(z, **flags):
                return nc.tensor.matmul(sums[:, z, 0:ZW], b.zeros[:, 0:P], b.zeros[:, 0:ZW], skip_group_check=True, **flags)
            for z in range(ZB):
                last = zero(z, start=True, stop=False)
            last.then_inc(s["used"], 2)
            pe.sem_inc(s["mix_read"], 1)
            with pe.Fori(0, T // G) as i:
                for c in range(G):
                    n, r = i * G + c, c % 2
                    if messages:
                        if c == 0:
                            pe.wait_ge(s["rows_ready"], i + 1)
                            pe.wait_ge(s["attrs_ready"], i + 1)
                        pe.wait_ge(s["mix_read"], n + 1)
                        if c % 2 == 0:
                            nc.tensor.transpose(work[:, 0:P], rows[:, c:c + 2, :].rearrange("p c d -> p (c d)"),
                                                b.ident[:, :]).then_inc(s["turned"], 1)
                            pe.wait_ge(s["turn_read"], i * (G // 2) + c // 2 + 1)
                        at = 64 * (c % 2)
                        nc.tensor.matmul(work[:, 256:256 + DN], turn[at:at + DI + 1, :], w_third[at:at + DI + 1, :],
                                         start=True, stop=True).then_inc(s["mixed"], 1)
                    pe.wait_ge(s["hot"], (n + 1) * 2)
                    for z in range(ZB):
                        last = nc.tensor.matmul(sums[:, z, 0:ZW], part_hot[:, r, :], spread[:, r, z * ZW:(z + 1) * ZW],
                                                start=False, stop=False, skip_group_check=True)
                    last.then_inc(s["used"], 1)
            for z in range(ZB):
                last = zero(z, start=False, stop=True)
            last.then_inc(s["summed"], 1)


def node_mlp(nc, b, agg_tile):
    B, L = 2, 7
    assert J % (B * L) == 0
    with ExitStack() as ctx:
        tag = b.tag
        sem = lambda name: ctx.enter_context(nc.semaphore(f"mlp_{name}_{tag}"))
        staged, turned, turn_read, agg_mixed, agg_read, hidden, hidden_read, out_made, out_added, filled = (
            sem("staged"), sem("tiles_turned"), sem("tiles_turn_read"), sem("agg_mixed"), sem("agg_mix_read"),
            sem("hidden_made"), sem("hidden_read"), sem("out_made"), sem("out_added"), sem("mid_filled"))
        sb = lambda name, shape: ctx.enter_context(nc.sbuf_tensor(f"{name}_{tag}", shape, FP32))
        agg_in, h_in = sb("agg_in", [P, 2, B, DH + 1]), sb("h_in", [P, 2, B, DN])
        agg_t, h_t = sb("agg_t", [DH + 1, 2, B * P]), sb("h_t", [DN, 2, B * P])
        mix, mid = sb("agg_mix", [DH, 2, B * P]), sb("mid", [P, 2, B * P])
        block = ctx.enter_context(nc.Block())
        ps = b.banks
        TURN, MIX, HIDDEN, OUT = 0, 2, 4, 6
        agg = per_node(agg_tile[:, :], DH + 1)
        h = per_node(b.h[:, :])

        @block.vector
        def _(dve):
            nc.vector.memset(mid[:, :, :], 0.0).then_inc(filled, 1)
            dve.wait_ge(filled, 1)
            nc.vector.memset(mid[64:65, :, :], 1.0).then_inc(filled, 1)
            nc.vector.tensor_copy(agg[:, :, DH:DH + 1], b.in_deg[:, :].unsqueeze(2)).then_inc(filled, 1)
            dve.wait_ge(filled, 3)
            with dve.Fori(0, J // (B * L)) as i:

                def stage(n):
                    if n >= 2:
                        dve.wait_ge(turned, i * L + (n - 1))
                    at = bass.ds(i * (B * L) + n * B, B)
                    nc.vector.tensor_tensor(agg_in[:, n % 2, :, :], agg[:, at, :],
                                            b.in_inv[:, at].unsqueeze(2).broadcast_to([P, B, DH + 1]), ALU.mult).then_inc(staged, 1)
                    nc.vector.tensor_copy(h_in[:, n % 2, :, :], h[:, at, :]).then_inc(staged, 1)

                def keep_turned(n):
                    if n >= 2:
                        dve.wait_ge(hidden, i * L + (n - 1))
                    dve.wait_ge(turned, i * L + (n + 1))
                    nc.vector.tensor_copy(agg_t[:, n % 2, :], ps[0:DH + 1, TURN + n % 2, 0:B * P]).then_inc(turn_read, 1)
                    nc.vector.tensor_copy(h_t[:, n % 2, :], ps[0:DN, TURN + n % 2, B * P:2 * B * P]).then_inc(turn_read, 1)

                def add(n):
                    dve.wait_ge(out_made, i * L + (n + 1))
                    x = per_node(b.x[:, :])[:, bass.ds(i * (B * L) + n * B, B), :]
                    nc.vector.tensor_tensor(x, x, ps[:, OUT + n % 2, 0:B * DN].rearrange("p (j d) -> p j d", d=DN),
                                            ALU.add).then_inc(out_added, 1)

                stage(0)
                for k in range(L + 3):
                    if k + 1 < L:
                        stage(k + 1)
                    if k < L:
                        keep_turned(k)
                    if k >= 3:
                        add(k - 3)
            dve.wait_ge(out_added, J // B)

        @block.scalar
        def _(act):
            act.wait_ge(filled, 2)
            with act.Fori(0, J // (B * L)) as i:
                for k in range(1, L + 2):
                    if k - 1 < L:
                        n = k - 1
                        if n >= 2:
                            act.wait_ge(hidden, i * L + (n - 1))
                        act.wait_ge(agg_mixed, i * L + (n + 1))
                        nc.scalar.copy(mix[:, n % 2, :], ps[0:DH, MIX + n % 2, 0:B * P]).then_inc(agg_read, 1)
                    if k >= 2:
                        n = k - 2
                        if n >= 2:
                            act.wait_ge(out_made, i * L + (n - 1))
                        act.wait_ge(hidden, i * L + (n + 1))
                        nc.scalar.activation(mid[0:DI, n % 2, :], ps[0:DI, HIDDEN + n % 2, 0:B * P], ACT.Relu,
                                             bias=b.b2a[:, :]).then_inc(hidden_read, 1)

        @block.tensor
        def _(pe):
            with pe.Fori(0, J // (B * L)) as i:

                def turn(n):
                    pe.wait_ge(staged, i * (2 * L) + 2 * (n + 1))
                    if n >= 2:
                        pe.wait_ge(turn_read, i * (2 * L) + 2 * (n - 1))
                    for c in range(B):
                        nc.tensor.transpose(ps[0:DH + 1, TURN + n % 2, c * P:(c + 1) * P], agg_in[:, n % 2, c, :], b.ident[:, :])
                        last = nc.tensor.transpose(ps[0:DN, TURN + n % 2, (B + c) * P:(B + c + 1) * P], h_in[:, n % 2, c, :],
                                                   b.ident[:, :])
                    last.then_inc(turned, 1)

                def mix_agg(n):
                    pe.wait_ge(turn_read, i * (2 * L) + 2 * (n + 1))
                    nc.tensor.matmul(ps[0:DH, MIX + n % 2, 0:B * P], b.w1b[:, :], agg_t[:, n % 2, :], start=True, stop=True) \
                        .then_inc(agg_mixed, 1)

                def hide(n):
                    pe.wait_ge(agg_read, i * L + (n + 1))
                    nc.tensor.matmul(ps[0:DI, HIDDEN + n % 2, 0:B * P], b.w2a_h[:, :], h_t[:, n % 2, :], start=True, stop=False)
                    nc.tensor.matmul(ps[0:DI, HIDDEN + n % 2, 0:B * P], b.w2a_agg[:, :], mix[:, n % 2, :], start=False,
                                     stop=True).then_inc(hidden, 1)

                def put_out(n):
                    pe.wait_ge(hidden_read, i * L + (n + 1))
                    if n >= 2:
                        pe.wait_ge(out_added, i * L + (n - 1))
                    for c in range(B):
                        last = nc.tensor.matmul(ps[:, OUT + n % 2, c * DN:(c + 1) * DN], mid[0:65, n % 2, c * P:(c + 1) * P],
                                                b.w2b[0:65, :], start=True, stop=True)
                    last.then_inc(out_made, 1)

                for k in range(L + 3):
                    for behind, part in enumerate((turn, mix_agg, hide, put_out)):
                        if 0 <= k - behind < L:
                            part(k - behind)


GATHER_SEMS = ("idx_ready", "taken", "rows_ready", "attrs", "attrs_ready", "turned", "turn_read", "ones", "mixed", "mix_read", "used", "hot",
               "summed", "copied", "scaled", "stored")


def general_layers(nc, b, edges, agg_tile):
    with ExitStack() as ctx:
        s = {name: ctx.enter_context(nc.semaphore(f"any_{name}")) for name in GATHER_SEMS}
        low, high = s["idx_ready"].num, s["stored"].num
        assert high - low == len(GATHER_SEMS) - 1
        s["gathered"] = ctx.enter_context(nc.semaphore("any_gathered"))
        sb = lambda name, shape, dt=FP32: ctx.enter_context(nc.sbuf_tensor(f"any_{name}", shape, dt))
        tiles = (sb("idx", [P, G], I32), sb("rows", [P, G, 64]), sb("turn", [P, P]), sb("msg", [P, 2, DN]),
                 sb("part_hot", [P, 2, P]), sb("spread", [P, 2, J * DN]), sb("w_third", [P, DN]))
        spread = tiles[5]

        def start_again():
            nc.gpsimd.sem_clear(range(low, high + 1))
            nc.all_engine_barrier()

        layer_norm_relu(nc, b, "in")
        store_table(nc, b, b.h)
        with nc.Fori(0, DH // DN) as third:
            edge_sums(nc, b, edges, agg_tile, True, s, tiles, third)
            start_again()
        node_mlp(nc, b, agg_tile)
        layer_norm_relu(nc, b, "mid")
        with nc.Block() as block:
            @block.vector
            def _(dve):
                nc.vector.tensor_copy(b.f[:, :], b.h[:, :]).then_inc(s["scaled"], 1)
                dve.wait_ge(s["scaled"], 1)
        start_again()
        with nc.Fori(0, STEPS) as step:
            with nc.Block() as block:
                @block.vector
                def _(dve):
                    nc.vector.tensor_tensor(per_node(spread[:, 0, :]), per_node(b.f[:, :]), spread_over(b.src_norm[:, :]),
                                            ALU.mult).then_inc(s["scaled"], 1)

                @block.sync
                def _(sp):
                    sp.wait_ge(s["scaled"], 1)
                    sp.dma_start(b.dram.table.rearrange("(p j) d -> p (j d)", j=J), spread[:, 0, :]).then_inc(s["stored"], 16)
                    sp.wait_ge(s["stored"], 16)
            start_again()
            edge_sums(nc, b, edges, agg_tile, False, s, tiles)
            start_again()
            with nc.Block() as block:
                @block.vector
                def _(dve):
                    combine(nc, dve, b, s["scaled"])
            start_again()


def combine(nc, dve, b, scaled):
    nc.vector.tensor_tensor(per_node(b.f[:, :]), per_node(b.f[:, :]), spread_over(b.dst_norm[:, :]), ALU.mult).then_inc(scaled, 1)
    dve.wait_ge(scaled, 1)
    nc.vector.tensor_scalar(b.f[:, :], b.f[:, :], 1.0 - ALPHA, None, ALU.mult).then_inc(scaled, 1)
    dve.wait_ge(scaled, 2)
    nc.vector.scalar_tensor_tensor(out=b.f[:, :], in0=b.h[:, :], scalar=ALPHA, in1=b.f[:, :], op0=ALU.mult,
                                   op1=ALU.add).then_inc(scaled, 1)
    dve.wait_ge(scaled, 3)


def store_result(nc, b, out):
    with nc.semaphore(f"result_added_{b.tag}") as added, nc.semaphore(f"result_stored_{b.tag}") as stored, nc.Block() as block:
        @block.vector
        def _(dve):
            nc.vector.tensor_tensor(b.f[:, :], b.f[:, :], b.x[:, :], ALU.add).then_inc(added, 1)

        @block.sync
        def _(sp):
            sp.wait_ge(added, 1)
            sp.dma_start(out[0:P * (J - 1), :].rearrange("(j p) d -> p j d", p=P), per_node(b.f[:, :])[:, 0:J - 1, :]).then_inc(stored, 16)
            sp.dma_start(out[P * (J - 1):N, :], b.f[0:NL, (J - 1) * DN:J * DN]).then_inc(stored, 16)
            sp.wait_ge(stored, 32)



def prepare_sorted(nc, b, edges, ins, kept):
    same, cont, last_row, window_row, unsorted = kept
    with ExitStack() as ctx:
        sem = lambda name: ctx.enter_context(nc.semaphore(f"{name}_{b.tag}"))
        sb = lambda name, shape, dt=FP32: ctx.enter_context(nc.sbuf_tensor(f"{name}_{b.tag}", shape, dt))
        made, keyed, first_in, summed, counted, moved, tri = (
            sem("prep_made"), sem("keys_made"), sem("next_first_in"), sem("below_summed"), sem("prep_counted"),
            sem("keys_stored"), sem("triangle_made"))
        node = sb("dst_number", [P, T])
        keys = sb("keys", [P, T, 2])
        window = sb("dst_window", [P, T], I32)
        inner = sb("dst_in_window", [P, T], I32)
        window_f, inner_f = sb("dst_window_f", [P, T]), sb("dst_in_window_f", [P, T])
        next_i, next_f = sb("next_first_int", [P, 1], I32), sb("next_first", [P, 1])
        below, ones = sb("triangle", [P, P]), sb("ones", [P, P])
        column, through = sb("column_count", [P, J]), sb("columns_through", [P, J])
        start, last = sb("node_start", [P, J]), sb("node_last", [P, J])
        part, first_of = sb("last_part", [P, J]), sb("first_of_window", [P, WG])
        drop = sb("drop_any", [P, T])
        block = ctx.enter_context(nc.Block())

        @block.gpsimd
        def _(pool):
            nc.gpsimd.memset(ones[:, :], 1.0).then_inc(tri, 1)
            nc.gpsimd.memset(below[:, :], 1.0).then_inc(tri, 1)
            pool.wait_ge(tri, 2)
            nc.gpsimd.affine_select(out=below[:, :], in_=below[:, :], compare_op=ALU.is_gt, fill=0.0, base=0,
                                    pattern=[[1, P]], channel_multiplier=-1).then_inc(tri, 1)
            nc.gpsimd.memset(first_of[:, :], 0.0).then_inc(tri, 1)
            nc.gpsimd.memset(window_row[:, :], 0).then_inc(tri, 1)
            pool.wait_ge(tri, 5)
            nc.gpsimd.affine_select(out=first_of[:, :], in_=first_of[:, :], compare_op=ALU.not_equal, fill=2.0, base=0,
                                    pattern=[[-WD, WG]], channel_multiplier=1).then_inc(tri, 1)

        @block.sync
        def _(sp):
            sp.wait_ge(made, 1)
            sp.dma_start(next_i[0:P - 2, :], ins["dst"][T:T * (P - 1)].rearrange("(p t) -> p t", t=T)[:, 0:1],
                         allow_slow_non_contiguous=True).then_inc(first_in, 16)
            sp.dma_start(next_i[P - 2:P - 1, :], ins["dst"][T * (P - 1):T * (P - 1) + 1].rearrange("(p t) -> p t", t=1)) \
                .then_inc(first_in, 16)
            sp.wait_ge(keyed, 2)
            sp.dma_start(b.dram.keys.rearrange("(p t) k -> p (t k)", t=T), keys[:, :, :].rearrange("p t k -> p (t k)")) \
                .then_inc(moved, 16)
            sp.wait_ge(moved, 16)

        @block.vector
        def _(dve):
            n = [0]

            def step(ins_):
                n[0] += 1
                ins_.then_inc(made, 1)
                dve.wait_ge(made, n[0])

            step(nc.vector.memset(next_i[:, :], NP))
            step(nc.vector.scalar_tensor_tensor(out=node[:, :], in0=edges.dst_place[:, :], scalar=float(P),
                                                in1=edges.dst_part[:, :], op0=ALU.mult, op1=ALU.add))
            step(nc.vector.memset(same[:, :], 0.0))
            step(nc.vector.tensor_tensor(same[:, 1:T], node[:, 1:T], node[:, 0:T - 1], ALU.is_equal))
            dve.wait_ge(first_in, 32)
            step(nc.vector.tensor_copy(next_f[:, :], next_i[:, :]))
            step(nc.vector.tensor_tensor(cont[:, :], next_f[:, :], node[:, T - 1:T], ALU.is_equal))
            step(nc.vector.tensor_tensor(drop[:, 1:T], node[:, 1:T], node[:, 0:T - 1], ALU.is_lt))
            step(nc.vector.tensor_tensor(drop[:, 0:1], next_f[:, :], node[:, T - 1:T], ALU.is_lt))
            step(nc.vector.memset(unsorted[:, :], 0.0))
            step(nc.vector.tensor_reduce(unsorted[:, 0:1], drop[:, :], AX.X, ALU.max))
            step(nc.vector.tensor_scalar(window[:, :], edges.dst[:, :], WBITS, None, ALU.logical_shift_right))
            step(nc.vector.tensor_scalar(inner[:, :], edges.dst[:, :], WD - 1, None, ALU.bitwise_and))
            step(nc.vector.tensor_copy(window_f[:, :], window[:, :]))
            step(nc.vector.tensor_copy(inner_f[:, :], inner[:, :]))
            nc.vector.tensor_copy(keys[:, :, 0:1], edges.src_part[:, :].unsqueeze(2)).then_inc(keyed, 1)
            step(nc.vector.scalar_tensor_tensor(out=inner_f[:, :], in0=edges.src_place[:, :], scalar=float(WD),
                                                in1=inner_f[:, :], op0=ALU.mult, op1=ALU.add))
            step(nc.vector.scalar_tensor_tensor(out=inner_f[:, :], in0=window_f[:, :], scalar=float(WC),
                                                in1=inner_f[:, :], op0=ALU.mult, op1=ALU.add))
            step(nc.vector.tensor_scalar(node[:, :], node[:, :], float(N), float(2 * NP * J), ALU.is_ge, ALU.mult))
            nc.vector.tensor_tensor(keys[:, :, 1:2], inner_f[:, :].unsqueeze(2), node[:, :].unsqueeze(2), ALU.add).then_inc(keyed, 1)
            dve.wait_ge(summed, 1)
            step(nc.vector.tensor_copy(column[:, :], b.banks[:, 1, 0:J]))
            step(nc.vector.tensor_tensor_scan(through[:, :], column[:, :], b.zeros[:, 0:J], 0.0, ALU.add, ALU.add))
            step(nc.vector.tensor_tensor(start[:, :], through[:, :], column[:, :], ALU.subtract))
            step(nc.vector.tensor_tensor(start[:, :], start[:, :], b.banks[:, 0, 0:J], ALU.add))
            nc.vector.tensor_copy(column[:, :], start[:, :]).then_inc(counted, 1)
            step(nc.vector.tensor_tensor(last[:, :], start[:, :], b.in_deg[:, :], ALU.add))
            step(nc.vector.tensor_scalar(last[:, :], last[:, :], -1.0, 0.0, ALU.add, ALU.max))
            step(nc.vector.tensor_scalar(part[:, :], last[:, :], 1.0 / T, 0.5 / T - 0.5, ALU.mult, ALU.add))
            step(nc.vector.tensor_scalar(part[:, :], part[:, :], ROUND, None, ALU.add))
            step(nc.vector.tensor_scalar(part[:, :], part[:, :], ROUND, None, ALU.subtract))
            step(nc.vector.tensor_scalar(part[:, :], part[:, :], float(TD - T), float(TD - T), ALU.mult, ALU.add))
            step(nc.vector.tensor_tensor(last_row[:, :], last[:, :], part[:, :], ALU.add))
            dve.wait_ge(summed, 2)
            step(nc.vector.tensor_copy(window_row[:, 0:J], b.banks[0:WG, 2, 0:J]))
            dve.wait_ge(keyed, 2)

        @block.tensor
        def _(pe):
            pe.wait_ge(tri, 6)
            nc.tensor.matmul(b.banks[:, 0, 0:J], below[:, :], b.in_deg[:, :], start=True, stop=True)
            nc.tensor.matmul(b.banks[:, 1, 0:J], ones[:, :], b.in_deg[:, :], start=True, stop=True).then_inc(summed, 1)
            pe.wait_ge(counted, 1)
            nc.tensor.matmul(b.banks[0:WG, 2, 0:J], first_of[:, :], start[:, :], start=True, stop=True).then_inc(summed, 1)


def messages_and_counts(nc, b, edges, same, window_row, tail):
    Q = 4
    QC, QW = G // Q, WG // Q
    with ExitStack() as ctx:
        sem = lambda name: ctx.enter_context(nc.semaphore(f"{name}_{b.tag}"))
        sb = lambda name, shape, dt=FP32: ctx.enter_context(nc.sbuf_tensor(f"{name}_{b.tag}", shape, dt))
        gathered = [sem(f"gathered{s}") for s in range(SLOTS)]
        attrs_in = [sem(f"attrs_in{s}") for s in range(SLOTS)]
        keys_in = [sem(f"keys_in{s}") for s in range(SLOTS)]
        sums_out = [sem(f"sums_out{s}") for s in range(SLOTS)]
        counts_out = [sem(f"counts_out{s}") for s in range(SLOTS)]
        indexed, taken, passed, turned, turn_read, mixed, mix_read, summed = (
            sem("indexed"), sem("rows_taken"), sem("passed"), sem("pairs_turned"), sem("pairs_read"), sem("mixed"),
            sem("mix_read"), sem("run_summed"))
        first_done = sem("first_done")
        first_act = sb("first_act", [P, 1], U8)
        hot, hot_used, counted, count_read, local_made, filled, keys_pointed, keys_turned, tailed, rooted, all_summed = (
            sem("window_hot"), sem("window_hot_used"), sem("window_counted"), sem("counts_read"), sem("keys_local"), sem("loop_filled"),
            sem("keys_pointed"), sem("keys_turned"), sem("tail_kept"), sem("out_rooted"), sem("all_summed"))
        idx = sb("idx", [P, SLOTS, G], I32)
        rows = sb("rows", [P, SLOTS, G, 64])
        turn = sb("turn", [P, 2, 2 * P])
        sums = sb("run_sums", [P, SLOTS, G, DH])
        key_idx = sb("key_idx", [WG, SLOTS], I32)
        raw_keys = sb("raw_keys", [P, SLOTS, P, 2])
        keys = sb("window_keys", [P, SLOTS, WG], BF16)
        local = sb("local_keys", [P, SLOTS, WG])
        term = sb("out_newton", [P, J])
        base = sb("window_base", [P, 1])
        iota_i, iota_w = sb("iota_wide_int", [P, WC], I32), sb("iota_wide", [P, WC], FP16)
        part_hot = sb("window_src_hot", [P, 2, P, QW], BF16)
        iota_by_windows = sb("iota_by_windows", [P, P, QW], BF16)
        place_hot = sb("window_place_hot", [P, 2, QW, WC], BF16)
        stage = sb("count_stage", [P, SLOTS, J, P], U8)
        block = ctx.enter_context(nc.Block())
        T_BANK, S_BANK, M_BANK, C_BANK = 0, 1, 2, (4, 6)
        KEYS_AT = 400
        n_loops = J // SLOTS

        @block.gpsimd
        def _(pool):
            nc.gpsimd.iota(iota_i[:, :], pattern=[[1, WC]], base=0, channel_multiplier=0).then_inc(filled, 1)

            def fetch_keys(s, g):
                pool.wait_ge(keys_pointed, g + 1)
                pool.sem_inc(taken, 1)
                pool.indirect_dma_start(out=raw_keys[0:WG, s, :, :].rearrange("p e k -> p (e k)"), out_offset=None,
                                        in_=b.dram.keys.rearrange("e (k a) -> (e k) a", a=1),
                                        in_offset=bass.IndirectOffsetOnAxis(ap=key_idx[:, s:s + 1], axis=0)).then_inc(keys_in[s], 16)

            pool.wait_ge(filled, 9)
            fetch_keys(0, 0)
            with pool.Fori(0, n_loops) as i:
                for s in range(SLOTS):
                    g = i * SLOTS + s
                    pool.wait_ge(turned, (g + 1) * Q)
                    pool.sem_inc(taken, 1)
                    pool.wait_ge(keys_turned, g + 1)
                    pool.sem_inc(taken, 1)
                    fetch_keys(1 - s, g + 1)
                    pool.wait_ge(indexed, g + 1)
                    pool.sem_inc(taken, 1)
                    for c in range(G):
                        pool.indirect_dma_start(out=rows[:, s, c, 0:DN], out_offset=None, in_=b.dram.table,
                                                in_offset=bass.IndirectOffsetOnAxis(ap=idx[:, s, c:c + 1], axis=0)) \
                            .then_inc(gathered[s], 16)

        @block.sync
        def _(sp):
            attrs = b.dram.attrs.rearrange("(p t) d -> p t d", t=T)
            sp.wait_ge(filled, 9)
            sp.wait_ge(b.attrs_copied, 32)

            def store(s, at):
                sp.dma_start(b.dram.running[:, bass.ds(at * G, G) if not isinstance(at, int) else slice(at * G, (at + 1) * G), :],
                             sums[:, s, :, :]).then_inc(sums_out[s], 16)
                sp.dma_start(b.dram.counts[bass.ds(at, 1)].rearrange("a p j c -> (a p) (j c)"),
                             stage[:, s, :, :].rearrange("p j c -> p (j c)")).then_inc(counts_out[s], 16)

            with sp.Fori(0, n_loops) as i:
                for s in range(SLOTS):
                    g = i * SLOTS + s
                    sp.wait_ge(turned, (g + 1) * Q)
                    sp.sem_inc(passed, 1)
                    sp.dma_start(rows[:, s, :, DN:DI], attrs[:, bass.ds(g * G, G), :]).then_inc(attrs_in[s], 16)
                    sp.wait_ge(summed, g * G + G + 1)
                    sp.sem_inc(passed, 1)
                    sp.wait_ge(count_read, (g + 1) * (WG // 2))
                    sp.sem_inc(passed, 1)
                    store(s, g)
            for s in range(SLOTS):
                sp.wait_ge(summed, SLOTS * G + J * G - (SLOTS - 1 - s) * G)
                sp.wait_ge(count_read, (SLOTS + J - (SLOTS - 1 - s)) * (WG // 2))
                store(s, J + s)
            for s in range(SLOTS):
                sp.wait_ge(sums_out[s], (n_loops + 1) * 16)
                sp.wait_ge(counts_out[s], (n_loops + 1) * 16)

        @block.vector
        def _(dve):
            nc.vector.memset(rows[:, :, :, DN:64], 0.0).then_inc(filled, 1)
            nc.vector.memset(sums[:, :, :, :], 0.0).then_inc(filled, 1)
            nc.vector.memset(stage[:, :, :, :], 0).then_inc(filled, 1)
            nc.vector.memset(base[:, :], 0.0).then_inc(filled, 1)
            nc.vector.memset(raw_keys[:, :, :, :], 0.0).then_inc(filled, 1)
            dve.wait_ge(filled, 6)
            nc.vector.memset(rows[:, :, :, DI:DI + 1], 1.0).then_inc(filled, 1)
            nc.vector.tensor_copy(iota_w[:, :], iota_i[:, :]).then_inc(filled, 1)
            nc.vector.tensor_copy(iota_by_windows[:, :, :], b.iota16[:, :].unsqueeze(2).broadcast_to([P, P, QW])).then_inc(filled, 1)
            dve.wait_ge(filled, 9)
            nc.vector.tensor_copy(idx[:, 0, :], edges.src[:, 0:G]).then_inc(indexed, 1)
            nc.vector.tensor_copy(key_idx[:, :], window_row[:, 0:SLOTS]).then_inc(keys_pointed, SLOTS)
            dve.sem_inc(hot, SLOTS * WG)
            dve.sem_inc(summed, SLOTS * G)
            with dve.Fori(0, n_loops) as i:
                for s in range(SLOTS):
                    g = i * SLOTS + s
                    nc.vector.tensor_copy(idx[:, 1 - s, :], edges.src[:, bass.ds((g + 1) * G, G)]).then_inc(indexed, 1)
                    dve.wait_ge(keys_turned, g + 2)
                    nc.vector.tensor_copy(key_idx[:, s:s + 1], window_row[:, bass.ds(g + 2, 1)]).then_inc(keys_pointed, 1)
                    nc.vector.tensor_copy(keys[:, s, :], b.banks[:, M_BANK, KEYS_AT:KEYS_AT + WG]).then_inc(local_made, 1)
                    nc.vector.tensor_scalar(local[:, s, :], b.banks[:, M_BANK, KEYS_AT + WG:KEYS_AT + 2 * WG], base[:, :], None,
                                            ALU.subtract).then_inc(local_made, 1)
                    dve.wait_ge(local_made, g * 3 + 2)
                    nc.vector.tensor_scalar(base[:, :], base[:, :], float(WG * WC), None, ALU.add).then_inc(local_made, 1)
                    for q in range(Q):
                        dve.wait_ge(hot_used, g * (WG // 2) + (q + 1) * (QW // 2))
                        nc.vector.tensor_tensor(part_hot[:, q % 2, :, :], iota_by_windows[:, :, :],
                                                keys[:, s, q * QW:(q + 1) * QW].unsqueeze(1).broadcast_to([P, P, QW]), ALU.is_equal)
                        for w in range(QW):
                            k = q * QW + w
                            nc.vector.tensor_scalar(place_hot[:, q % 2, w, :], iota_w[:, :], float(k * WC), local[:, s, k:k + 1],
                                                    ALU.add, ALU.is_equal).then_inc(hot, 1)
                            if q == 0 or (q > 1 and w < QW - QC):
                                continue
                            c = q * QC + w - (QW - QC)
                            if c % QC == 0:
                                dve.wait_ge(mix_read, g * Q + (c // QC + 2))
                            before = sums[:, s, c - 1, :] if c else sums[:, 1 - s, G - 1, :]
                            dve.wait_ge(summed, g * G + (SLOTS * G + c))
                            nc.vector.scalar_tensor_tensor(out=sums[:, s, c, :], in0=before, scalar=same[:, bass.ds(g * G + c, 1)],
                                                           in1=sums[:, s, c, :], op0=ALU.mult, op1=ALU.add).then_inc(summed, 1)
            dve.wait_ge(summed, SLOTS * G + T)
            nc.vector.tensor_copy(tail[:, :], sums[:, SLOTS - 1, G - 1, :]).then_inc(tailed, 1)
            dve.wait_ge(all_summed, 1)
            nc.vector.tensor_reduce(b.src_norm[:, :], b.banks[:, S_BANK, 0:WC].rearrange("p (j d) -> p j d", d=WD), AX.X,
                                    ALU.add).then_inc(tailed, 1)
            dve.wait_ge(tailed, 2)
            nc.vector.tensor_scalar(b.out_cap[:, :], b.src_norm[:, :], 1.0, None, ALU.max).then_inc(tailed, 1)
            dve.wait_ge(rooted, 1)
            inverse_root(nc, dve, b.src_norm[:, :], b.out_cap[:, :], term[:, :], tailed, 3)

        @block.scalar
        def _(act):
            act.wait_ge(filled, 9)
            act.sem_inc(turn_read, 1)
            act.sem_inc(mix_read, 1)
            act.sem_inc(count_read, SLOTS * (WG // 2))
            with act.Fori(0, n_loops) as i:
                nc.scalar.activation(first_act[:, :].bitcast(FP8), b.zeros[:, 0:1], ACT.Copy, scale=0.5, saturate=True) \
                    .then_inc(first_done, 1)
                act.wait_ge(first_done, i + 1)
                act.sem_inc(passed, 1)
                for s in range(SLOTS):
                    g = i * SLOTS + s

                    def read_counts(r):
                        at = C_BANK[r % 2]
                        act.wait_ge(counted, g * (WG // 2) + (r + 1))
                        act.sem_inc(passed, 1)
                        to = stage[:, s, :, 2 * r * WD:(2 * r + 2) * WD].bitcast(FP8).rearrange("p j (w d) -> p w j d", d=WD)
                        of = b.banks[:, at:at + 2, 0:WC].rearrange("p w (j d) -> p w j d", d=WD)
                        nc.scalar.activation(to, of, ACT.Copy, scale=0.5, saturate=True).then_inc(count_read, 1)

                    act.wait_ge(counts_out[s], (i + 1) * 16)
                    act.wait_ge(sums_out[s], (i + 1) * 16)
                    act.sem_inc(passed, 1)

                    def keep_turned(q):
                        act.wait_ge(turned, SLOTS * Q + g * Q + (q + 1))
                        nc.scalar.copy(turn[:, q % 2, :], b.banks[:, T_BANK, 0:2 * P]).then_inc(turn_read, 1)

                    def relu_messages(q):
                        act.wait_ge(mixed, 2 * g * Q + 2 * (q + 1))
                        nc.scalar.activation(sums[:, s, q * QC:(q + 1) * QC, :].rearrange("p (k o) d -> p o k d", o=2),
                                             b.banks[:, M_BANK:M_BANK + 2, 0:QC // 2 * DH].rearrange("p o (k d) -> p o k d", d=DH),
                                             ACT.Relu).then_inc(mix_read, 1)

                    keep_turned(0)
                    relu_messages(0)
                    for r in range(WG // 2):
                        read_counts(r)
                        q, at = divmod(r, QW // 2)
                        if q < Q - 1 and at == 1:
                            keep_turned(q + 1)
                        if q < Q - 1 and at == 2:
                            relu_messages(q + 1)
            act.wait_ge(tailed, 3)
            nc.scalar.sqrt(b.src_norm[:, :], b.out_cap[:, :]).then_inc(rooted, 1)

        @block.tensor
        def _(pe):
            pe.sem_inc(hot_used, SLOTS * (QW // 2))

            def turn_keys(s):
                for k in range(2):
                    last = nc.tensor.matmul(b.banks[:, M_BANK, KEYS_AT + k * WG:KEYS_AT + (k + 1) * WG], raw_keys[:, s, :, k],
                                            b.ident[:, 0:WG], start=True, stop=True, skip_group_check=True)
                last.then_inc(keys_turned, 1)

            nc.tensor.matmul(b.banks[:, S_BANK, 0:P], b.zeros16[:, :], b.zeros16[:, :], start=True, stop=False, skip_group_check=True)
            for at in range(P, WC, P):
                nc.tensor.matmul(b.banks[:, S_BANK, at:min(at + P, WC)], b.zeros16[:, :], b.zeros16[:, 0:min(P, WC - at)],
                                 start=True, stop=False, skip_group_check=True)
            pe.sem_inc(keys_turned, 1)
            pe.wait_ge(keys_in[0], 16)
            turn_keys(0)
            pe.sem_inc(turned, SLOTS * Q)
            with pe.Fori(0, n_loops) as i:
                for s in range(SLOTS):
                    g = i * SLOTS + s

                    def count(r):
                        m = (r // (QW // 2)) % 2
                        pe.wait_ge(hot, SLOTS * WG + g * WG + 2 * (r + 1))
                        pe.wait_ge(count_read, g * (WG // 2) + (r + WG - 1))
                        for k in range(2):
                            w = (2 * r + k) % QW
                            last = nc.tensor.matmul(b.banks[:, C_BANK[r % 2] + k, 0:WC], part_hot[:, m, :, w],
                                                    place_hot[:, m, w, :], start=True, stop=True)
                        last.then_inc(counted, 1)
                        for k in range(2):
                            w = (2 * r + k) % QW
                            last = nc.tensor.matmul(b.banks[:, S_BANK, 0:WC], part_hot[:, m, :, w], place_hot[:, m, w, :],
                                                    start=False, stop=False, skip_group_check=True)
                        last.then_inc(hot_used, 1)

                    pe.wait_ge(gathered[s], (i + 1) * (G * 16))
                    pe.wait_ge(attrs_in[s], (i + 1) * 16)

                    def turn_rows(q):
                        for k in range(QC // 2):
                            c = q * QC + 2 * k
                            last = nc.tensor.transpose(b.banks[:, T_BANK, k * P:(k + 1) * P],
                                                       rows[:, s, c:c + 2, :].rearrange("p c d -> p (c d)"), b.ident[:, :])
                        last.then_inc(turned, 1)

                    def mix(q):
                        pe.wait_ge(turn_read, g * Q + (q + 2))
                        pe.wait_ge(mix_read, g * Q + (q + 1))
                        if q == 0:
                            pe.wait_ge(local_made, g * 3 + 2)
                        if q == Q - 1:
                            pe.wait_ge(keys_in[1 - s], (i + (1 + s)) * 16)
                            turn_keys(1 - s)
                        for k in range(QC):
                            at = 64 * (k % 2)
                            last = nc.tensor.matmul(b.banks[:, M_BANK + k % 2, k // 2 * DH:(k // 2 + 1) * DH],
                                                    turn[at:at + DI + 1, q % 2, (k // 2) * P:(k // 2 + 1) * P],
                                                    b.w1a[at:at + DI + 1, :], start=True, stop=True)
                            if k >= QC - 2:
                                last.then_inc(mixed, 1)

                    turn_rows(0)
                    mix(0)
                    for r in range(WG // 2):
                        count(r)
                        q, at = divmod(r, QW // 2)
                        if q < Q - 1 and at == 1:
                            turn_rows(q + 1)
                        if q < Q - 1 and at == 2:
                            mix(q + 1)
            nc.tensor.matmul(b.banks[:, S_BANK, 0:P], b.zeros16[:, :], b.zeros16[:, :], start=False, stop=True,
                             skip_group_check=True).then_inc(all_summed, 1)


def sums_of_nodes(nc, b, edges, agg_tile, cont, last_row, tail):
    C = 7
    with ExitStack() as ctx:
        sem = lambda name: ctx.enter_context(nc.semaphore(f"{name}_{b.tag}"))
        sb = lambda name, shape, dt=FP32: ctx.enter_context(nc.sbuf_tensor(f"{name}_{b.tag}", shape, dt))
        fetched = [sem(f"fetched{s}") for s in range(SLOTS)]
        pointed, copied, has_made, spread_made, carried, added, passed = (
            sem("pointed"), sem("copied"), sem("has_made"), sem("carry_spread"), sem("carried"), sem("carry_added"),
            sem("fetch_passed"))
        idx, got = sb("last_idx", [P, SLOTS, C], I32), sb("last_rows", [P, SLOTS, C, DH])
        has = sb("has_edges", [P, J])
        end_hot, spread = sb("end_hot", [P, P]), sb("carry_rows", [P, J * DN])
        block = ctx.enter_context(nc.Block())
        agg = per_node(agg_tile[:, :], DH + 1)
        rows_of = b.dram.running.rearrange("p t d -> (p t) d")

        @block.gpsimd
        def _(pool):
            with pool.Fori(0, J // (C * SLOTS)) as i:
                for s in range(SLOTS):
                    g = i * SLOTS + s
                    pool.wait_ge(copied, g + 1)
                    pool.sem_inc(passed, 1)
                    nc.gpsimd.tensor_copy(idx[:, s, :], last_row[:, bass.ds(g * C, C)]).then_inc(pointed, 1)
                    pool.wait_ge(pointed, g + 1)
                    pool.sem_inc(passed, 1)
                    for c in range(C):
                        pool.indirect_dma_start(out=got[:, s, c, :], out_offset=None, in_=rows_of,
                                                in_offset=bass.IndirectOffsetOnAxis(ap=idx[:, s, c:c + 1], axis=0)) \
                            .then_inc(fetched[s], 16)

        @block.vector
        def _(dve):
            dve.sem_inc(copied, SLOTS)
            nc.vector.tensor_scalar(has[:, :], b.in_deg[:, :], 0.0, None, ALU.is_gt).then_inc(has_made, 1)
            nc.vector.tensor_scalar(end_hot[:, :], b.iota[:, :], edges.dst_part[:, T - 1:T], cont[:, :],
                                    ALU.is_equal, ALU.mult).then_inc(has_made, 1)
            dve.wait_ge(has_made, 2)
            with dve.Fori(0, J // (C * SLOTS)) as i:
                for s in range(SLOTS):
                    g = i * SLOTS + s
                    dve.wait_ge(fetched[s], (i + 1) * (C * 16))
                    at = bass.ds(g * C, C)
                    nc.vector.tensor_tensor(agg[:, at, 0:DH], got[:, s, :, :],
                                            has[:, at].unsqueeze(2).broadcast_to([P, C, DH]), ALU.mult).then_inc(copied, 1)
            dve.wait_ge(copied, SLOTS + J // C)
            for third in range(DH // DN):
                if third:
                    dve.wait_ge(carried, third)
                nc.vector.scalar_tensor_tensor(
                    out=per_node(spread[:, :]), in0=spread_over(b.iota[:, 0:J]), scalar=edges.dst_place[:, T - 1:T],
                    in1=tail[:, third * DN:(third + 1) * DN].unsqueeze(1).broadcast_to([P, J, DN]),
                    op0=ALU.is_equal, op1=ALU.mult).then_inc(spread_made, 1)
                dve.wait_ge(carried, third + 1)
                for z in range(ZB):
                    to = agg[:, z * ZJ:(z + 1) * ZJ, third * DN:(third + 1) * DN]
                    nc.vector.tensor_tensor(to, to, b.banks[:, z, 0:ZW].rearrange("p (j d) -> p j d", d=DN),
                                            ALU.add).then_inc(added, 1)
                dve.wait_ge(added, (third + 1) * ZB)

        @block.tensor
        def _(pe):
            for third in range(DH // DN):
                pe.wait_ge(spread_made, third + 1)
                if third:
                    pe.wait_ge(added, third * ZB)
                for z in range(ZB):
                    last = nc.tensor.matmul(b.banks[:, z, 0:ZW], end_hot[:, :], spread[:, z * ZW:(z + 1) * ZW],
                                            start=True, stop=True)
                last.then_inc(carried, 1)


SPLITS = 3
WF = SPLITS * DN + 1
TILES = 4
HEAD = J % TILES
BLOCKS = J // TILES
KC = 14
CHUNKS = J // KC
assert HEAD == 2 and BLOCKS % 2 == 0 and J % KC == 0


def propagate(nc, b, exact):
    with ExitStack() as ctx:
        sem = lambda name: ctx.enter_context(nc.semaphore(f"{name}_{b.tag}"))
        sb = lambda name, shape, dt=FP32: ctx.enter_context(nc.sbuf_tensor(f"{name}_{b.tag}", shape, dt))
        chunk_in = [sem(f"chunk_in{k}") for k in range(CHUNKS)]
        head_in, prepared, started, swept, drained, folded, fresh, passed, chain, stacked = (
            sem("head_in"), sem("prop_prepared"), sem("prop_started"), sem("chunk_used"), sem("block_drained"),
            sem("block_folded"), sem("parts_fresh"), sem("sweep_passed"), sem("fresh_chain"), sem("stack_made"))
        folds_read = sem("folds_read")
        parts = sb("feature_parts", [P, 2, J, WF], BF16)
        head = sb("head_counts", [P, HEAD, J, P], U8)
        ring = sb("count_ring", [P, CHUNKS, TILES, KC, P], U8)
        drain = sb("drained", [WF, 2, TILES * P])
        stack = sb("stacked_identities", [WF, DN + 1])
        gain = sb("target_gain", [P, J])
        expect = sb("expected_in_deg", [P, J])
        scaled, rest = sb("scaled", [P, TILES * DN]), sb("rest", [P, TILES * DN])
        block = ctx.enter_context(nc.Block())
        SWEEP, FOLD = (0, 1), (2, 3)
        steps2 = STEPS // 2
        CHAIN = 3 + 2 * SPLITS

        @block.sync
        def _(sp):
            sp.dma_start(head[:, :, :, :].rearrange("p a j c -> p a (j c)"),
                         b.dram.counts[SLOTS:SLOTS + HEAD].rearrange("a p j c -> p a (j c)")).then_inc(head_in, 16)
            with sp.Fori(0, STEPS) as t:
                with sp.Fori(0, BLOCKS) as m:
                    for k in range(CHUNKS):
                        sp.wait_ge(swept, t * (BLOCKS * CHUNKS) + m * CHUNKS + (k + 1))
                        sp.sem_inc(passed, 1)
                        sp.dma_start(ring[:, k, :, :, :].rearrange("p a j c -> p a (j c)"),
                                     b.dram.counts[bass.ds(m * TILES + (SLOTS + HEAD), TILES), :, k * KC:(k + 1) * KC, :]
                                     .rearrange("a p j c -> p a (j c)")).then_inc(chunk_in[k], 16)
            for k in range(CHUNKS):
                sp.wait_ge(chunk_in[k], STEPS * BLOCKS * 16)

        @block.gpsimd
        def _(pool):
            nc.gpsimd.memset(stack[:, :], 0.0).then_inc(stacked, 1)
            for k in range(SPLITS):
                pool.wait_ge(stacked, k + 1)
                nc.gpsimd.affine_select(out=stack[:, 0:DN], in_=stack[:, 0:DN], compare_op=ALU.not_equal, fill=2.0,
                                        base=-k * DN, pattern=[[-1, DN]], channel_multiplier=1).then_inc(stacked, 1)
            nc.gpsimd.affine_select(out=stack[:, DN:DN + 1], in_=stack[:, DN:DN + 1], compare_op=ALU.not_equal, fill=2.0,
                                    base=-SPLITS * DN, pattern=[[0, 1]], channel_multiplier=1).then_inc(stacked, 1)
            pool.wait_ge(prepared, 1)
            nc.gpsimd.affine_select(out=expect[:, J - 1:J], in_=expect[:, J - 1:J], compare_op=ALU.is_ge, fill=0.0,
                                    base=NL - 1, pattern=[[0, 1]], channel_multiplier=-1).then_inc(stacked, 1)

        @block.scalar
        def _(act):
            def drain_block(parity, cols):
                nc.scalar.copy(drain[:, parity, 0:cols], b.banks[0:WF, SWEEP[parity], 0:cols]).then_inc(drained, 1)

            act.sem_inc(drained, 1)
            act.wait_ge(started, 1)
            drain_block(0, HEAD * P)
            with act.Fori(0, STEPS) as t:
                with act.Fori(0, BLOCKS // 2) as mm:
                    for odd in (1, 0):
                        act.wait_ge(swept, (t * BLOCKS + mm * 2) * CHUNKS + (3 - odd) * CHUNKS)
                        act.wait_ge(folded, t * (BLOCKS + 1) + mm * 2 + (2 - odd))
                        drain_block(odd, TILES * P)
                act.wait_ge(started, t + 2)
                act.wait_ge(folded, (t + 1) * (BLOCKS + 1) + 1)
                drain_block(0, HEAD * P)

        @block.vector
        def _(dve):
            nc.vector.tensor_copy(expect[:, :], b.in_deg[:, :]).then_inc(prepared, 1)
            nc.vector.memset(drain[:, :, :], 0.0).then_inc(prepared, 1)
            nc.vector.memset(parts[:, :, :, SPLITS * DN:WF], 1.0).then_inc(prepared, 1)
            nc.vector.tensor_scalar(gain[:, :], b.dst_norm[:, :], 1.0 - ALPHA, None, ALU.mult).then_inc(prepared, 1)
            nc.vector.tensor_tensor(per_node(b.f[:, :]), per_node(b.h[:, :]), spread_over(b.src_norm[:, :]), ALU.mult).then_inc(prepared, 1)
            for k in range(SPLITS):
                dve.wait_ge(prepared, 5 + 2 * k)
                part = parts[:, 0, :, k * DN:(k + 1) * DN]
                nc.vector.tensor_copy(part, per_node(b.f[:, :])).then_inc(prepared, 1)
                if k < SPLITS - 1:
                    dve.wait_ge(prepared, 6 + 2 * k)
                    nc.vector.tensor_tensor(per_node(b.f[:, :]), per_node(b.f[:, :]), part, ALU.subtract).then_inc(prepared, 1)
            dve.wait_ge(stacked, SPLITS + 3)
            dve.sem_inc(folds_read, 1)

            def new_features(n, side, parity, at, tiles):
                dve.wait_ge(folded, n + 2)
                got = per_node(b.banks[:, FOLD[parity], 0:tiles * (DN + 1)], DN + 1)
                where = at if isinstance(at, slice) else bass.ds(at, tiles)
                t1, t2 = per_node(scaled[:, 0:tiles * DN]), per_node(rest[:, 0:tiles * DN])
                f, h = per_node(b.f[:, :])[:, where, :], per_node(b.h[:, :])[:, where, :]
                spread = lambda column: column[:, where].unsqueeze(2).broadcast_to([P, tiles, DN])
                steps = [0]

                def step(ins_):
                    steps[0] += 1
                    ins_.then_inc(chain, 1)
                    dve.wait_ge(chain, n * CHAIN + steps[0])

                step(nc.vector.tensor_tensor(exact[:, where].unsqueeze(2), got[:, :, DN:DN + 1], expect[:, where].unsqueeze(2),
                                             ALU.is_equal))
                step(nc.vector.tensor_tensor(t1, got[:, :, 0:DN], spread(gain), ALU.mult))
                dve.sem_inc(folds_read, 1)
                step(nc.vector.scalar_tensor_tensor(out=f, in0=h, scalar=ALPHA, in1=t1, op0=ALU.mult, op1=ALU.add))
                step(nc.vector.tensor_tensor(t1, f, spread(b.src_norm), ALU.mult))
                for k in range(SPLITS):
                    part = parts[:, 1 - side, where, k * DN:(k + 1) * DN]
                    of, left = (t1, t2) if k % 2 == 0 else (t2, t1)
                    step(nc.vector.tensor_copy(part, of))
                    if k < SPLITS - 1:
                        step(nc.vector.tensor_tensor(left, of, part, ALU.subtract))
                assert steps[0] == CHAIN
                dve.sem_inc(fresh, 1)

            with dve.Fori(0, steps2) as tt:
                for side in range(2):
                    n = (tt * 2 + side) * (BLOCKS + 1)
                    new_features(n, side, 0, slice(0, HEAD), HEAD)
                    with dve.Fori(0, BLOCKS // 2) as mm:
                        for odd in (1, 0):
                            new_features(n + (mm * 2 + (2 - odd)), side, odd, mm * (2 * TILES) + (HEAD + (1 - odd) * TILES), TILES)

        @block.tensor
        def _(pe):
            def sweep_tile(bank, cols, side, j, matrix):
                return nc.tensor.matmul(b.banks[0:WF, bank, 0:cols], parts[:, side, j, :], matrix.bitcast(FP8),
                                        start=(j == 0), stop=(j == J - 1))

            def fold(parity, tiles):
                for a in range(tiles):
                    last = nc.tensor.matmul(b.banks[:, FOLD[parity], a * (DN + 1):(a + 1) * (DN + 1)],
                                            drain[:, parity, a * P:(a + 1) * P], stack[:, :], start=True, stop=True)
                last.then_inc(folded, 1)

            def head_block(side, known, before):
                for j in range(J):
                    if j in before:
                        before[j]()
                    if (j - HEAD) % TILES == 0 or j == 0:
                        known(0 if j == 0 else (j - HEAD) // TILES + 1)
                    last = sweep_tile(SWEEP[0], HEAD * P, side, j, head[:, :, j, :])
                return last

            pe.wait_ge(stacked, SPLITS + 3)
            pe.wait_ge(head_in, 16)
            pe.sem_inc(swept, CHUNKS)
            pe.wait_ge(prepared, 4 + 2 * SPLITS)
            pe.sem_inc(folded, 1)
            head_block(0, lambda n: None, {}).then_inc(started, 1)
            with pe.Fori(0, steps2) as tt:
                for side in range(2):
                    t = tt * 2 + side
                    with pe.Fori(0, BLOCKS // 2) as mm:
                        for odd in (1, 0):
                            u = 1 if odd else 0
                            n = t * (BLOCKS + 1) + mm * 2 + (1 - u)
                            for k in range(CHUNKS):
                                pe.wait_ge(chunk_in[k], (t * BLOCKS + mm * 2 + (1 - u) + 1) * 16)
                                if k == 0:
                                    pe.wait_ge(drained, n + 1)
                                pe.sem_inc(passed, 1)
                                for j in range(k * KC, (k + 1) * KC):
                                    last = sweep_tile(SWEEP[u], TILES * P, side, j, ring[:, k, :, j - k * KC, :])
                                last.then_inc(swept, 1)
                                if k == 0:
                                    pe.wait_ge(drained, n + 2)
                                    pe.wait_ge(folds_read, n + 1)
                                    pe.sem_inc(passed, 1)
                                    fold(1 - u, TILES)
                    last_n = t * (BLOCKS + 1) + BLOCKS

                    def known(n_block, side=side, last_n=last_n):
                        pe.wait_ge(fresh, last_n - BLOCKS + n_block + 1)
                        pe.sem_inc(passed, 1)

                    def last_fold(last_n=last_n):
                        pe.wait_ge(drained, last_n + 2)
                        pe.wait_ge(folds_read, last_n + 1)
                        pe.sem_inc(passed, 1)
                        fold(0, TILES)

                    pe.wait_ge(drained, last_n + 2)
                    pe.sem_inc(passed, 1)
                    head_block(1 - side, known, {KC: last_fold}).then_inc(started, 1)


def needs_general(nc, b, exact, unsorted, flag):
    with nc.semaphore("flag_made") as made, nc.semaphore("flag_turned") as turned, \
            nc.sbuf_tensor("bad_rows", [P, 2], FP32) as bad, nc.Block() as block:
        @block.vector
        def _(dve):
            nc.vector.tensor_reduce(bad[:, 0:1], exact[:, :], AX.X, ALU.min).then_inc(made, 1)
            dve.wait_ge(made, 1)
            nc.vector.tensor_scalar(bad[:, 0:1], bad[:, 0:1], -1.0, 1.0, ALU.mult, ALU.add).then_inc(made, 1)
            dve.wait_ge(made, 2)
            nc.vector.tensor_tensor(bad[:, 0:1], bad[:, 0:1], unsorted[:, :], ALU.max).then_inc(made, 1)
            dve.wait_ge(turned, 1)
            nc.vector.tensor_reduce(bad[0:1, 1:2], b.banks[0:1, 0, 0:P], AX.X, ALU.max).then_inc(made, 1)
            dve.wait_ge(made, 4)
            nc.vector.tensor_copy(flag[:, :], bad[0:1, 1:2]).then_inc(made, 1)
            dve.wait_ge(made, 5)

        @block.tensor
        def _(pe):
            pe.wait_ge(made, 3)
            nc.tensor.matmul(b.banks[0:1, 0, 0:P], bad[:, 0:1], b.ident[:, :], start=True, stop=True).then_inc(turned, 1)


def general_way(nc, ins, out, dram):
    with ExitStack() as ctx:
        b = Kept(nc, ctx, dram, "any")
        edges = Edges(nc, ctx, "any")
        agg_tile = ctx.enter_context(nc.sbuf_tensor("agg_nodes_any", [P, J * (DH + 1)], FP32))
        setup(nc, b, edges, ins)
        degrees(nc, b, edges, 2)
        general_layers(nc, b, edges, agg_tile)
        store_result(nc, b, out)




def fast_way(nc, ins, out, dram, flag):
    with ExitStack() as ctx:
        b = Kept(nc, ctx, dram, "fast")
        exact = ctx.enter_context(nc.sbuf_tensor("counts_exact", [P, J], FP32))
        unsorted = ctx.enter_context(nc.sbuf_tensor("unsorted", [P, 1], FP32))
        with ExitStack() as edge_ctx:
            sb = lambda name, shape: edge_ctx.enter_context(nc.sbuf_tensor(name, shape, FP32))
            edges = Edges(nc, edge_ctx, "fast")
            same, cont, last_row, tail = sb("same_target", [P, T]), sb("run_goes_on", [P, 1]), sb("last_row", [P, J]), sb("last_sums", [P, DH])
            window_row = edge_ctx.enter_context(nc.sbuf_tensor("window_row", [WG, J + SLOTS], I32))
            setup(nc, b, edges, ins)
            degrees(nc, b, edges, 1)
            layer_norm_relu(nc, b, "in")
            store_table(nc, b, b.h)
            prepare_sorted(nc, b, edges, ins, (same, cont, last_row, window_row, unsorted))
            messages_and_counts(nc, b, edges, same, window_row, tail)
            agg_tile = sb("agg_nodes_fast", [P, J * (DH + 1)])
            sums_of_nodes(nc, b, edges, agg_tile, cont, last_row, tail)
            node_mlp(nc, b, agg_tile)
        layer_norm_relu(nc, b, "mid")
        propagate(nc, b, exact)
        needs_general(nc, b, exact, unsorted, flag)
        store_result(nc, b, out)


def program(nc, ins, out):
    dram = Dram(nc)
    with nc.sbuf_tensor("general_flag", [1, 1], I32) as flag:
        fast_way(nc, ins, out, dram, flag)
        bad = nc.values_load(flag[0:1, 0:1], min_val=0, max_val=1)
        with nc.If(bad > 0):
            nc.all_engine_barrier()
            general_way(nc, ins, out, dram)


INPUTS = ["x", "src", "dst", "edge_attr_16", "L0_gnn_w1a", "L0_gnn_b1a", "L0_gnn_w1b", "L0_gnn_b1b",
          "L0_gnn_w2a", "L0_gnn_b2a", "L0_gnn_w2b", "L0_gnn_b2b"]


def kernel(**inputs):
    import numpy as np
    import concourse.bacc as bacc
    from concourse.bass_utils import run_bass_kernel_spmd

    nc = bacc.Bacc("TRN2", target_bir_lowering=False, num_devices=1)
    arrays, ins = {}, {}
    for name in INPUTS:
        a = np.ascontiguousarray(inputs[name])
        arrays[f"in_{name}"] = a
        ins[name] = nc.dram_tensor(f"in_{name}", a.shape, mybir.dt.from_np(a.dtype), kind="ExternalInput").ap()
    out = nc.dram_tensor("out_nodes", (N, DN), FP32, kind="ExternalOutput").ap()
    program(nc, ins, out)
    result = run_bass_kernel_spmd(nc, [arrays], core_ids=[0])
    return result.results[0]["out_nodes"]
```
